# Optimizing a Trainium2 kernel written in Bass

```python
import numpy as np
import jax
import jax.numpy as jnp

def _softmax(x, axis=-1):
    return jax.nn.softmax(x, axis=axis)

def _gelu(x):
    return jax.nn.gelu(x, approximate=True)

def _silu(x):
    return jax.nn.silu(x)

def _sigmoid(x):
    return jax.nn.sigmoid(x)

def _layernorm(x, axis=-1, eps=1e-05):
    m = jnp.mean(x, axis=axis, keepdims=True)
    v = jnp.var(x, axis=axis, keepdims=True)
    return (x - m) / jnp.sqrt(v + eps)

def _scatter_add(tgt, idx, src, axis=0):
    return tgt.at[idx].add(src)

def _segment_sum(src, seg, n):
    return jax.ops.segment_sum(src, seg, n)
kernel_name = 'mk_adaln_d1_jaxref_r8_23ed2e'

def setup_inputs(seed: int=0):
    np.random.seed(seed)
    _w = jnp.asarray

    def _L0_attn_setup():
        import jax, jax.numpy as jnp
        import numpy as np
        EMBED = 256
        HEADS = 16
        HEAD_DIM = EMBED // HEADS
        CHUNK = 128
        BASE = 10000.0
        EPS = 1e-06

        def _alibi_log_decay(h):
            slopes = 2.0 ** (-8.0 * (jnp.arange(h, dtype=jnp.float32) + 1.0) / h)
            return -slopes

        def _lrpe_rotate(x):
            b, n, h, d = x.shape
            half = d // 2
            theta = BASE ** (-2.0 * jnp.arange(half, dtype=jnp.float32) / d)
            ang = jnp.arange(n, dtype=jnp.float32)[:, None] * theta[None, :]
            cos = jnp.cos(ang)[None, :, None, :]
            sin = jnp.sin(ang)[None, :, None, :]
            x1, x2 = (x[..., :half], x[..., half:])
            return jnp.concatenate([x1 * cos - x2 * sin, x1 * sin + x2 * cos], axis=-1)

        def _lightning_attn(q, k, v, log_lam):
            b, n, h, d = q.shape
            C = CHUNK
            nc = n // C
            qc = q.reshape(b, nc, C, h, d).transpose(1, 0, 2, 3, 4)
            kc = k.reshape(b, nc, C, h, d).transpose(1, 0, 2, 3, 4)
            vc = v.reshape(b, nc, C, h, d).transpose(1, 0, 2, 3, 4)
            i = jnp.arange(C, dtype=jnp.float32)
            diff = i[:, None] - i[None, :]
            D = jnp.where(diff[None] >= 0, jnp.exp(log_lam[:, None, None] * diff[None]), 0.0)
            decay_q = jnp.exp(log_lam[None, :] * (i[:, None] + 1.0))
            decay_k = jnp.exp(log_lam[None, :] * (C - 1.0 - i[:, None]))
            lam_C = jnp.exp(log_lam * C)

            def step(S, qkv):
                qi, ki, vi = qkv
                scores = jnp.einsum('bthd,bshd->bhts', qi, ki) * D[None]
                o_intra = jnp.einsum('bhts,bshd->bthd', scores, vi)
                o_inter = jnp.einsum('bthd,bhde->bthe', qi * decay_q[None, :, :, None], S)
                S_new = lam_C[None, :, None, None] * S + jnp.einsum('bshd,bshe->bhde', ki * decay_k[None, :, :, None], vi)
                return (S_new, o_intra + o_inter)
            S0 = jnp.zeros((b, h, d, d), q.dtype)
            _, o = jax.lax.scan(step, S0, (qc, kc, vc))
            return o.transpose(1, 0, 2, 3, 4).reshape(b, n, h, d)

        def _gated_group_rmsnorm(o, gate, weight):
            b, n, d = o.shape
            x = o * jax.nn.sigmoid(gate)
            xg = x.reshape(b, n, HEADS, HEAD_DIM)
            ms = jnp.mean(xg * xg, axis=-1, keepdims=True)
            xg = xg * jax.lax.rsqrt(ms + EPS)
            return xg.reshape(b, n, d) * weight
        key = jax.random.key(seed)
        ks = jax.random.split(key, 8)
        b, n, d = (2, 256, EMBED)
        std = 0.02
        return {'x': jax.random.normal(ks[0], (b, n, d), jnp.float32), 'Wq': jax.random.normal(ks[1], (d, d), jnp.float32) * std, 'Wk': jax.random.normal(ks[2], (d, d), jnp.float32) * std, 'Wv': jax.random.normal(ks[3], (d, d), jnp.float32) * std, 'Wo': jax.random.normal(ks[4], (d, d), jnp.float32) * std, 'Wg1': jax.random.normal(ks[5], (d, HEAD_DIM), jnp.float32) * std, 'Wg2': jax.random.normal(ks[6], (HEAD_DIM, d), jnp.float32) * std, 'norm_weight': jnp.ones((d,), jnp.float32)}
    _L0_attn_in = _L0_attn_setup()

    def _L0_ffn_setup():
        import jax, jax.numpy as jnp
        import numpy as np
        B, S, H = (4, 128, 256)
        E, K, I, SI = (16, 4, 176, 704)

        def _silu_mul(gu, inter):
            return jax.nn.silu(gu[:, :inter]) * gu[:, inter:]
        key = jax.random.key(seed)
        ks = jax.random.split(key, 7)
        s = 0.02
        return {'hidden_states': jax.random.normal(ks[0], (B, S, H), jnp.float32), 'gate_w': jax.random.normal(ks[1], (E, H), jnp.float32) * s, 'expert_gate_up': jax.random.normal(ks[2], (E, 2 * I, H), jnp.float32) * s, 'expert_down': jax.random.normal(ks[3], (E, H, I), jnp.float32) * s, 'shared_gate_up': jax.random.normal(ks[4], (2 * SI, H), jnp.float32) * s, 'shared_down': jax.random.normal(ks[5], (H, SI), jnp.float32) * s, 'shared_gate_vec': jax.random.normal(ks[6], (1, H), jnp.float32) * s}
    _L0_ffn_in = _L0_ffn_setup()
    _L0_c = _w((lambda *s: np.random.randn(*s).astype(np.float32) * 0.05)(2, 256))
    _L0_wmod = _w((lambda *s: np.random.randn(*s).astype(np.float32) * 0.05)(256, 6 * 256) * 256 ** (-0.5))
    _d = {'L0_attn_x': _L0_attn_in['x'], 'L0_attn_Wq': _L0_attn_in['Wq'], 'L0_attn_Wk': _L0_attn_in['Wk'], 'L0_attn_Wv': _L0_attn_in['Wv'], 'L0_attn_Wo': _L0_attn_in['Wo'], 'L0_attn_Wg1': _L0_attn_in['Wg1'], 'L0_attn_Wg2': _L0_attn_in['Wg2'], 'L0_attn_norm_weight': _L0_attn_in['norm_weight'], 'L0_ffn_gate_w': _L0_ffn_in['gate_w'], 'L0_ffn_expert_gate_up': _L0_ffn_in['expert_gate_up'], 'L0_ffn_expert_down': _L0_ffn_in['expert_down'], 'L0_ffn_shared_gate_up': _L0_ffn_in['shared_gate_up'], 'L0_ffn_shared_down': _L0_ffn_in['shared_down'], 'L0_ffn_shared_gate_vec': _L0_ffn_in['shared_gate_vec'], 'L0_c': _L0_c, 'L0_wmod': _L0_wmod}
    _x0 = _d['L0_attn_x']
    _d['L0_attn_x'] = jax.random.normal(jax.random.fold_in(jax.random.key(seed), 1), (2, 1024, 256), dtype=_x0.dtype)
    del _x0
    return _d

def reference(L0_attn_x, L0_attn_Wq, L0_attn_Wk, L0_attn_Wv, L0_attn_Wo, L0_attn_Wg1, L0_attn_Wg2, L0_attn_norm_weight, L0_ffn_gate_w, L0_ffn_expert_gate_up, L0_ffn_expert_down, L0_ffn_shared_gate_up, L0_ffn_shared_down, L0_ffn_shared_gate_vec, L0_c, L0_wmod):

    def _L0_attn_ref(x, Wq, Wk, Wv, Wo, Wg1, Wg2, norm_weight):
        import jax, jax.numpy as jnp
        import numpy as np
        EMBED = 256
        HEADS = 16
        HEAD_DIM = EMBED // HEADS
        CHUNK = 128
        BASE = 10000.0
        EPS = 1e-06

        def _alibi_log_decay(h):
            slopes = 2.0 ** (-8.0 * (jnp.arange(h, dtype=jnp.float32) + 1.0) / h)
            return -slopes

        def _lrpe_rotate(x):
            b, n, h, d = x.shape
            half = d // 2
            theta = BASE ** (-2.0 * jnp.arange(half, dtype=jnp.float32) / d)
            ang = jnp.arange(n, dtype=jnp.float32)[:, None] * theta[None, :]
            cos = jnp.cos(ang)[None, :, None, :]
            sin = jnp.sin(ang)[None, :, None, :]
            x1, x2 = (x[..., :half], x[..., half:])
            return jnp.concatenate([x1 * cos - x2 * sin, x1 * sin + x2 * cos], axis=-1)

        def _lightning_attn(q, k, v, log_lam):
            b, n, h, d = q.shape
            C = CHUNK
            nc = n // C
            qc = q.reshape(b, nc, C, h, d).transpose(1, 0, 2, 3, 4)
            kc = k.reshape(b, nc, C, h, d).transpose(1, 0, 2, 3, 4)
            vc = v.reshape(b, nc, C, h, d).transpose(1, 0, 2, 3, 4)
            i = jnp.arange(C, dtype=jnp.float32)
            diff = i[:, None] - i[None, :]
            D = jnp.where(diff[None] >= 0, jnp.exp(log_lam[:, None, None] * diff[None]), 0.0)
            decay_q = jnp.exp(log_lam[None, :] * (i[:, None] + 1.0))
            decay_k = jnp.exp(log_lam[None, :] * (C - 1.0 - i[:, None]))
            lam_C = jnp.exp(log_lam * C)

            def step(S, qkv):
                qi, ki, vi = qkv
                scores = jnp.einsum('bthd,bshd->bhts', qi, ki) * D[None]
                o_intra = jnp.einsum('bhts,bshd->bthd', scores, vi)
                o_inter = jnp.einsum('bthd,bhde->bthe', qi * decay_q[None, :, :, None], S)
                S_new = lam_C[None, :, None, None] * S + jnp.einsum('bshd,bshe->bhde', ki * decay_k[None, :, :, None], vi)
                return (S_new, o_intra + o_inter)
            S0 = jnp.zeros((b, h, d, d), q.dtype)
            _, o = jax.lax.scan(step, S0, (qc, kc, vc))
            return o.transpose(1, 0, 2, 3, 4).reshape(b, n, h, d)

        def _gated_group_rmsnorm(o, gate, weight):
            b, n, d = o.shape
            x = o * jax.nn.sigmoid(gate)
            xg = x.reshape(b, n, HEADS, HEAD_DIM)
            ms = jnp.mean(xg * xg, axis=-1, keepdims=True)
            xg = xg * jax.lax.rsqrt(ms + EPS)
            return xg.reshape(b, n, d) * weight
        b, n, d = x.shape
        q = (x @ Wq).reshape(b, n, HEADS, HEAD_DIM)
        k = (x @ Wk).reshape(b, n, HEADS, HEAD_DIM)
        v = (x @ Wv).reshape(b, n, HEADS, HEAD_DIM)
        q = jax.nn.silu(q)
        k = jax.nn.silu(k)
        q = _lrpe_rotate(q)
        k = _lrpe_rotate(k)
        log_lam = _alibi_log_decay(HEADS)
        o = _lightning_attn(q, k, v, log_lam).reshape(b, n, d)
        gate = x @ Wg1 @ Wg2
        o = _gated_group_rmsnorm(o, gate, norm_weight)
        return o @ Wo

    def _L0_ffn_ref(hidden_states, gate_w, expert_gate_up, expert_down, shared_gate_up, shared_down, shared_gate_vec):
        import jax, jax.numpy as jnp
        import numpy as np
        B, S, H = (4, 128, 256)
        E, K, I, SI = (16, 4, 176, 704)

        def _silu_mul(gu, inter):
            return jax.nn.silu(gu[:, :inter]) * gu[:, inter:]
        orig_shape = hidden_states.shape
        x = hidden_states.reshape(-1, H)
        router_logits = x @ gate_w.T
        routing_probs = jax.nn.softmax(router_logits.astype(jnp.float32), axis=-1)
        topk_w, topk_idx = jax.lax.top_k(routing_probs, K)
        topk_w = topk_w / topk_w.sum(axis=-1, keepdims=True)
        topk_w = topk_w.astype(x.dtype)
        combine = (jax.nn.one_hot(topk_idx, E, dtype=x.dtype) * topk_w[..., None]).sum(1)
        shared = _silu_mul(x @ shared_gate_up.T, SI) @ shared_down.T
        shared = shared * jax.nn.sigmoid(x @ shared_gate_vec.T)

        def step(acc, ew):
            w_gu, w_d, cw = ew
            h = _silu_mul(x @ w_gu.T, I)
            return (acc + h @ w_d.T * cw[:, None], None)
        acc0 = jnp.zeros_like(x)
        sparse, _ = jax.lax.scan(step, acc0, (expert_gate_up, expert_down, combine.T))
        return (shared + sparse).reshape(orig_shape)
    x = L0_attn_x
    mod = (_silu(L0_c) @ L0_wmod).reshape(L0_c.shape[0], 6, 1, -1)
    sa, ca, ga, sb, cb, gb = (mod[:, 0], mod[:, 1], mod[:, 2], mod[:, 3], mod[:, 4], mod[:, 5])
    ga = (2 * (ga >= 0) - 1) * jnp.maximum(jnp.abs(ga), 0.25)
    gb = (2 * (gb >= 0) - 1) * jnp.maximum(jnp.abs(gb), 0.25)
    h = _layernorm(x, axis=-1) * (1 + ca) + sa
    x = x + ga * _L0_attn_ref(h, L0_attn_Wq, L0_attn_Wk, L0_attn_Wv, L0_attn_Wo, L0_attn_Wg1, L0_attn_Wg2, L0_attn_norm_weight)
    h = _layernorm(x, axis=-1) * (1 + cb) + sb
    x = x + gb * _L0_ffn_ref(h, L0_ffn_gate_w, L0_ffn_expert_gate_up, L0_ffn_expert_down, L0_ffn_shared_gate_up, L0_ffn_shared_down, L0_ffn_shared_gate_vec)
    return x

_drawn_inputs = setup_inputs


def setup_inputs(seed=0):
    import zlib

    import numpy as np

    out = dict(_drawn_inputs(seed))
    spreads = {'L0_attn_norm_weight': (1.0, 0.6)}
    factors = {'L0_attn_Wg1': 8.0,
     'L0_attn_Wg2': 8.0,
     'L0_ffn_gate_w': 8.0,
     'L0_ffn_expert_gate_up': 8.0,
     'L0_ffn_expert_down': 8.0,
     'L0_ffn_shared_gate_up': 8.0,
     'L0_ffn_shared_down': 8.0,
     'L0_ffn_shared_gate_vec': 8.0}
    for name, (base, spread) in spreads.items():
        noise = np.random.default_rng([zlib.crc32(name.encode()), seed]).standard_normal(out[name].shape)
        drawn = base * np.exp(spread * noise) if base else spread * noise
        out[name] = jnp.asarray(drawn.astype(out[name].dtype))
    for name, factor in factors.items():
        out[name] = (out[name] * factor).astype(out[name].dtype)
    return out
```

```python
from contextlib import ExitStack

import numpy as np

import concourse.bass as bass
from concourse import mybir

F32 = mybir.dt.float32
I32 = mybir.dt.int32
U32 = mybir.dt.uint32
BF16 = mybir.dt.bfloat16
F32R = mybir.dt.float32r
ALU = mybir.AluOpType
ACT = mybir.ActivationFunctionType
AX = mybir.AxisListType

P = 128
B, N, D = 2, 1024, 256
H, HD = 16, 16
KC = D // P
NCH = N // P
NT = B * NCH
HG = 4
NR = H // HG
PAD = P // HG
LN_EPS = 1e-5
RMS_EPS = 1e-6
GATE_MIN = 0.25
E, TOPK = 16, 4
I_E = 176
HC = I_E // 2
SI = 704
SM = -(-SI // P)
NQ = NT * TOPK
NJ = NT * TOPK + E
SHARED_T = 4
SHARED_STEPS = NT // SHARED_T


def at_least(eng, semaphore, value):
    if not (isinstance(value, int) and value <= 0):
        eng.wait_ge(semaphore, value)


def build(nc, x, Wq, Wk, Wv, Wo, Wg1, Wg2, norm_w, c, wmod, router_w, expert_gu, expert_d, shared_gu, shared_d,
          rope, decay, decay_qk, decay_s, state_mask, ident_in, out):
    h2_rows = nc.dram_tensor("h2_rows", [NT * P, D], F32, kind="Internal").ap()
    y_rows = nc.dram_tensor("y_rows", [NJ * P, D], F32, kind="Internal").ap()
    with ExitStack() as ctx, ExitStack() as attention, ExitStack() as routing:
        def sb(name, shape, dt=F32):
            return ctx.enter_context(nc.sbuf_tensor(name, shape, dt))

        def sem(name):
            return ctx.enter_context(nc.semaphore(name))

        def sem2(name):
            return [sem(f"{name}{b}") for b in range(B)]

        def sb2(name, shape, dt=F32):
            return [sb(f"{name}{b}", shape, dt) for b in range(B)]

        ident = sb("ident", [P, P])
        settle_from, settle_to = sb("settle_from", [1, 1]), sb("settle_to", [1, 32])
        x_all = sb("x_all", [P, NT, D])
        mod_rows = sb2("mod_rows", [P, 4, D])
        w_gu = sb("w_gu", [P, E, KC, 2 * I_E])
        w_r = sb("w_r", [P, KC, E + 1])
        h2T = sb("h2T", [P, KC, NT * P])

        def at(name, shape, dt=F32):
            return attention.enter_context(nc.sbuf_tensor(name, shape, dt))

        def at2(name, shape, dt=F32):
            return [at(f"{name}{b}", shape, dt) for b in range(B)]

        score_bank = [ctx.enter_context(nc.psum_tensor(f"score_bank{g}", [P, HG, P], F32)) for g in range(HG)]
        bank_a = [ctx.enter_context(nc.psum_tensor(f"bank_a{b}", [P, 512], F32)) for b in range(B)]
        bank_b = [ctx.enter_context(nc.psum_tensor(f"bank_b{b}", [P, 512], F32)) for b in range(B)]

        w_in = at("w_in", [P, KC, 3 * D + HD])
        w_g2 = at("w_g2", [HD, D])
        w_o = at("w_o", [P, KC, D])
        w_og = at2("w_og", [P, KC, D])
        norm_half = at("norm_half", [P, KC])
        norm_col = at("norm_col", [P, KC])
        c_raw = at("c_raw", [P, KC, B])
        c_silu = at("c_silu", [P, KC, B])
        c_rows = at("c_rows", [P, KC, B, P])
        mod_cols = at("mod_cols", [P, 2, KC, B])
        gate_abs = at("gate_abs", [P, D])
        gate_sgn = at("gate_sgn", [P, D])
        gate_max = at("gate_max", [P, D])
        rope_t = at("rope_t", [P, NCH, 2, HD])
        decay_t = at("decay_t", [P, HG, NR, P])
        decay_qk_t = at("decay_qk_t", [P, 2, H])
        decay_s_t = at("decay_s_t", [P, NR, HG * HD])
        state_mask_t = at("state_mask_t", [P, NR, HG * HD])
        half_neg = at("half_neg", [P, H])
        bn = at("bn", [P, NT, 6])
        mean_var = at("mean_var", [P, NT, 2])
        rstd1 = at("rstd1", [P, NT])

        xn = at2("xn", [P, D])
        hT = at2("hT", [P, KC, P])
        qk = at2("qk", [P, 2 * H, HD])
        v = at2("v", [P, D])
        g1T = at2("g1T", [HD, P])
        rope_a = at2("rope_a", [P, 2 * H, HD])
        rope_b = at2("rope_b", [P, 2 * H, HD])
        rot = at2("rot", [P, 2, H, PAD])
        k_dec = at2("k_dec", [P, H, PAD])
        qT = at2("qT", [P, NR, P])
        kT = at2("kT", [P, NR, P])
        probs_all = at("probs_all", [P, B, HG, NR, P])
        probs = [probs_all[:, b] for b in range(B)]
        w_mod = probs_all[:, :, :, :, :].rearrange("p b g r t -> p (b g r t)")[:, 0:KC * 6 * D].rearrange("p (k n) -> p k n", k=KC)
        state = at2("state", [P, NR, HG * HD])
        state_old = at2("state_old", [P, NR, HG * HD])
        state_new = at2("state_new", [P, NR, HG * HD])
        th = at2("th", [P, D])
        o_t = at2("o_t", [P, D])
        o_i = at2("o_i", [P, D])
        o_g = at2("o_g", [P, H, HD])
        o_sq = at2("o_sq", [P, H, HD])
        ss = at2("ss", [P, H])
        ss_eps = at2("ss_eps", [P, H])
        rms = at2("rms", [P, H])
        o_n = at2("o_n", [P, H, HD])
        oT = at2("oT", [P, KC, P])

        bn2 = at2("bn2", [P, 6])
        mv2 = at2("mv2", [P, 2])
        var2 = at2("var2", [P, 1])
        rstd2 = at2("rstd2", [P, 1])
        xn2 = at2("xn2", [P, D])
        h2_scaled = at2("h2_scaled", [P, D])
        h2 = at2("h2", [P, D])

        attention.close()
        w_d = sb("w_d", [HC, E, 2, D])
        ws_gu = sb("ws_gu", [P, KC, 2, SM * P])
        ws_d = sb("ws_d", [P, SM, D])
        weight = sb("weight", [P, NT, TOPK])
        shared_gate = sb("shared_gate", [P, NT])
        iota_f = sb("iota_f", [P, P])
        token_id = sb("token_id", [P, NT])
        slot = sb("slot", [P, NQ], I32)
        job_expert = sb("job_expert", [1, NJ], I32)
        token_of = sb("token_of", [P, NJ], I32)
        s_silu = [sb(f"s_silu{i}", [P, 512]) for i in range(2)]
        s_hid = sb("s_hid", [P, SM, 512])
        acc = sb("acc", [P, NT, D])
        def rt(name, shape, dt=F32):
            return routing.enter_context(nc.sbuf_tensor(name, shape, dt))

        logits = rt("logits", [P, NT, E + 1])
        top8 = rt("top8", [P, NT, 8])
        top8_i = rt("top8_i", [P, NT, 8], U32)
        choice = rt("choice", [P, NQ])
        gap = rt("gap", [P, NT, TOPK])
        weight_e = rt("weight_e", [P, NT, TOPK])
        weight_sum = rt("weight_sum", [P, NT])
        weight_rec = rt("weight_rec", [P, NT])
        shared_th = rt("shared_th", [P, NT])
        before = rt("before", [P, P], BF16)
        ones = rt("ones", [P, P], BF16)
        onehot = rt("onehot", [P, NQ, E])
        mask = rt("mask", [P, NT, E], BF16)
        mask_sum = rt("mask_sum", [P, E], BF16)
        count_i = rt("count_i", [P, E], I32)
        blocks_i = rt("blocks_i", [P, E], I32)
        blocks = rt("blocks", [P, E])
        one_row = rt("one_row", [P, E])
        block_end = rt("block_end", [P, E])
        block_start = rt("block_start", [P, E])
        place = rt("place", [P, NT, E])
        placed = rt("placed", [P, NQ, E])
        slot_f = rt("slot_f", [P, NQ])
        slot_blk_i = rt("slot_blk_i", [P, NQ], I32)
        slot_row_i = rt("slot_row_i", [P, NQ], I32)
        slot_blk = rt("slot_blk", [P, NQ])
        slot_row = rt("slot_row", [P, NQ])
        job_ge = rt("job_ge", [1, NJ, E])
        job_sum = rt("job_sum", [1, NJ])
        row_hot = rt("row_hot", [P, 2, TOPK, P], F32R)
        blk_hot = rt("blk_hot", [P, 2, TOPK, NJ], F32R)
        zero_r = rt("zero_r", [P, P], F32R)
        routing.close()
        idx = [sb(f"idx{i}", [P, 1], I32) for i in range(4)]
        xg = [sb(f"xg{i}", [P, D]) for i in range(4)]
        xeT = [sb(f"xeT{i}", [P, KC, P]) for i in range(2)]
        sg = [sb(f"sg{i}", [P, I_E]) for i in range(2)]
        hid = [sb(f"hid{i}", [P, I_E]) for i in range(2)]
        hidT = [sb(f"hidT{i}", [HC, 2, P]) for i in range(2)]
        ys = [sb(f"ys{i}", [P, D]) for i in range(4)]
        cidx = [sb(f"cidx{i}", [P, 1], I32) for i in range(2 * TOPK)]
        yg = [sb(f"yg{i}", [P, D]) for i in range(2 * TOPK)]
        total = [sb(f"total{i}", [P, D]) for i in range(2)]
        total_g = [sb(f"total_g{i}", [P, D]) for i in range(2)]
        result = [sb(f"result{i}", [P, D]) for i in range(2)]

        x_in = [sem(f"x_in{i}") for i in range(NT // 4)]
        consts_in, w_mod_in, c_in, w_in_in = sem("consts_in"), sem("w_mod_in"), sem("c_in"), sem("w_in_in")
        c_silu_done, c_rows_done = sem("c_silu_done"), sem("c_rows_done")
        mod_cols_ready, mod_cols_done = sem("mod_cols_ready"), sem("mod_cols_done")
        mod_rows_ready, mod_rows_done = sem2("mod_rows_ready"), sem("mod_rows_done")
        gate_steps = sem("gate_steps")
        consts_set = sem("consts_set")
        ln1_steps, rstd1_done = sem("ln1_steps"), sem("rstd1_done")

        xn_done, xT_ready, hT_done = sem2("xn_done"), sem2("xT_ready"), sem2("hT_done")
        qk_ready, vg_ready, qk_done, vg_done = sem2("qk_ready"), sem2("vg_ready"), sem2("qk_done"), sem2("vg_done")
        rope_a_done, rope_b_done, rot_done = sem2("rope_a_done"), sem2("rope_b_done"), sem2("rot_done")
        k_dec_done, qkT_ready, qkT_done = sem2("k_dec_done"), sem2("qkT_ready"), sem2("qkT_done")
        scores_ready, probs_done = sem2("scores_ready"), sem2("probs_done")
        gate_state_ready, th_done = sem2("gate_state_ready"), sem2("th_done")
        state_old_done, state_new_done, state_done = sem2("state_old_done"), sem2("state_new_done"), sem2("state_done")
        o_ready, o_steps, o_g_done = sem2("o_ready"), sem2("o_steps"), sem2("o_g_done")
        o_sq_done, ss_done, ss_eps_done, rms_done, o_n_done = (sem2("o_sq_done"), sem2("ss_done"), sem2("ss_eps_done"),
                                                               sem2("rms_done"), sem2("o_n_done"))
        oT_ready, oT_done, y_ready, x2_done = sem2("oT_ready"), sem2("oT_done"), sem2("y_ready"), sem2("x2_done")
        ln2_steps, var2_done, rstd2_done, xn2_done = sem2("ln2_steps"), sem2("var2_done"), sem2("rstd2_done"), sem2("xn2_done")
        h2_scaled_done, h2_done, h2_stored = sem2("h2_scaled_done"), sem2("h2_done"), sem2("h2_stored")
        h2T_ready, h2T_done = sem2("h2T_ready"), sem2("h2T_done")
        ws_zero = sem("ws_zero")
        w_gu_in, ws_in, w_r_in, w_d_in = sem("w_gu_in"), sem("ws_in"), sem("w_r_in"), sem("w_d_in")
        logits_ready, gap_done, exp_done = sem("logits_ready"), sem("gap_done"), sem("exp_done")
        iota_done, route, counts_ready, masks_done = sem("iota_done"), sem("route"), sem("counts_ready"), sem("masks_done")
        hot_done, hot_used, tokens_ready, tokens_done = sem2("hot_done"), sem2("hot_used"), sem("tokens_ready"), sem("tokens_done")
        s_gu_ready, s_silu_done, s_hid_done, s_y_ready, s_y_done = (sem("s_gu_ready"), sem("s_silu_done"), sem("s_hid_done"),
                                                                    sem("s_y_ready"), sem("s_y_done"))
        idx_done = sem("idx_done")
        gathered = [sem(f"gathered{i}") for i in range(4)]
        xeT_ready, xeT_done = sem("xeT_ready"), sem("xeT_done")
        gu_ready, sg_done, hid_done = sem("gu_ready"), sem("sg_done"), sem("hid_done")
        hidT_ready, hidT_done, ye_ready, ye_done = sem("hidT_ready"), sem("hidT_done"), sem("ye_ready"), sem("ye_done")
        y_stored = [sem(f"y_stored{i}") for i in range(4)]
        cidx_done = sem("cidx_done")
        y_back = [sem(f"y_back{i}") for i in range(2 * TOPK)]
        sums, result_done = sem("sums"), [sem(f"result_done{i}") for i in range(2)]
        stored = [sem(f"stored{i}") for i in range(2)]

        def heads(ap):
            return ap.rearrange("p (h d) -> p h d", d=HD)

        bank = [t[:, :, :].rearrange("p a t -> p (a t)") for t in score_bank] + [bank_a[0][:, :], bank_b[0][:, :], bank_a[1][:, :], bank_b[1][:, :]]
        w_gu_flat = w_gu[:, :, :, :].rearrange("p e k n -> p (e k n)")
        w_d_flat = w_d[:, :, :, :].rearrange("p e c n -> p (e c n)")
        ROUTE_BANK, COUNT_BANK = bank[4], bank[5]

        settled = iter(range(32))

        def settle_pool():
            i = next(settled)
            nc.gpsimd.tensor_tensor(settle_to[0:1, i:i + 1], settle_from[0:1, 0:1], settle_from[0:1, 0:1], ALU.add)

        def settle_dve():
            i = next(settled)
            nc.vector.memset(settle_to[0:1, i:i + 1], 0.0)

        def run_jobs(eng, step):
            for s in range(4):
                step(0, s, "xghy"[0:s + 1])
            with eng.Fori(1, NJ // 4) as i:
                for u in range(4):
                    step(i, u, "xghy")
            for s in range(3):
                step(NJ // 4, s, "xghy"[s + 1:])

        block = ctx.enter_context(nc.Block())

        @block.sync
        def _(sp):
            sp.dma_start(c_raw[:, :, :], c).then_inc(c_in, 16)
            sp.dma_start(ident[:, :], ident_in).then_inc(consts_in, 16)
            x_rows = x.rearrange("(t p) d -> p t d", p=P)
            for j in range(0, NT, 4):
                sp.dma_start(x_all[:, j:j + 4, :], x_rows[:, j:j + 4, :]).then_inc(x_in[j // 4], 16)
            sp.dma_start(rope_t[:, :, :, :], rope.rearrange("(j p) s d -> p j s d", p=P)).then_inc(consts_in, 16)
            sp.dma_start(decay_qk_t[:, :, :], decay_qk).then_inc(consts_in, 16)
            sp.dma_start(decay_s_t[:, :, :], decay_s).then_inc(consts_in, 16)
            sp.dma_start(state_mask_t[:, :, :], state_mask).then_inc(consts_in, 16)
            sp.dma_start(norm_col[:, :], norm_w).then_inc(consts_in, 16)
            sp.dma_start(decay_t[:, :, :, :], decay).then_inc(consts_in, 16)

            sp.dma_start(w_gu[:, :, :, :], expert_gu.rearrange("e (k p) n -> p e k n", p=P)).then_inc(w_gu_in, 16)
            sp.dma_start(w_r[:, :, :], router_w.rearrange("(k p) e -> p k e", p=P)).then_inc(w_r_in, 16)
            with sp.Fori(1, NCH + 1) as n:
                for b in range(B):
                    sp.wait_ge(h2_done[b], n)
                    sp.dma_start(h2_rows[bass.ds((n + (b * NCH - 1)) * P, P), :], h2[b][:, :]).then_inc(h2_stored[b], 16)
            for b in range(B):
                sp.wait_ge(h2_stored[b], 16 * NCH)
                sp.wait_ge(h2T_done[b], NCH)
            full = SI // P * P
            for k in range(KC):
                sp.dma_start(ws_gu[:, k, :, 0:SI], shared_gu[k * P:(k + 1) * P]).then_inc(ws_in, 16)
            sp.dma_start(ws_d[:, 0:SM - 1, :], shared_d[0:full, :].rearrange("(m p) n -> p m n", p=P)).then_inc(ws_in, 16)
            sp.wait_ge(ws_zero, 2)
            sp.dma_start(ws_d[0:SI - full, SM - 1, :], shared_d[full:SI, :]).then_inc(ws_in, 16)
            sp.dma_start(w_d[:, :, :, :], expert_d.rearrange("e (c p) n -> p e c n", p=HC)).then_inc(w_d_in, 16)
            with sp.Fori(0, NJ // 4) as i:
                for u in range(4):
                    sp.wait_ge(ye_done, i * 4 + (u + 1))
                    sp.dma_start(y_rows[bass.ds((i * 4 + u) * P, P), :], ys[u][:, :]).then_inc(y_stored[u], 16)
            with sp.Fori(0, NT // 2) as i:
                for u in range(2):
                    sp.wait_ge(result_done[u], i + 1)
                    sp.dma_start(out[bass.ds((i * 2 + u) * P, P), :], result[u][:, :]).then_inc(stored[u], 16)
            for u in range(2):
                sp.wait_ge(stored[u], 16 * (NT // 2))

        @block.scalar
        def _(act):
            act.dma_start(w_mod, wmod.rearrange("(k p) n -> p k n", p=P)).then_inc(w_mod_in, 16)
            for w, off in ((Wq, 0), (Wk, D), (Wv, 2 * D), (Wg1, 3 * D)):
                act.dma_start(w_in[:, :, off:off + w.shape[1]], w.rearrange("(k p) n -> p k n", p=P)).then_inc(w_in_in, 16)
            act.dma_start(w_g2[:, :], Wg2).then_inc(w_in_in, 16)
            act.dma_start(w_o[:, :, :], Wo.rearrange("(k p) n -> p k n", p=P)).then_inc(w_in_in, 16)
            act.wait_ge(c_in, 16)
            act.activation(c_silu[:, :, :], c_raw[:, :, :], ACT.Silu).then_inc(c_silu_done, 1)

            with act.Fori(1, NCH + 1) as n:
                for b in range(B):
                    act.wait_ge(xT_ready[b], n)
                    act.wait_ge(mod_cols_done, 2)
                    for k in range(KC):
                        last = act.activation(hT[b][:, k, :], bank_a[b][:, k * P:(k + 1) * P], ACT.Identity,
                                              bias=mod_cols[:, 0, k, b:b + 1], scale=mod_cols[:, 1, k, b:b + 1])
                    last.then_inc(hT_done[b], 1)
                for b in range(B):
                    act.wait_ge(qk_ready[b], n)
                    act.activation(qk[b][:, :, :], bank_a[b][:, :].rearrange("p (h d) -> p h d", d=HD),
                                   ACT.Silu).then_inc(qk_done[b], 1)
                    act.wait_ge(vg_ready[b], n)
                    act.copy(v[b][:, :], bank_b[b][:, 0:D])
                    act.copy(g1T[b][:, :], bank_b[b][0:HD, D:D + P]).then_inc(vg_done[b], 1)
                for b in range(B):
                    act.wait_ge(qkT_ready[b], n)
                    act.copy(qT[b][:, :, :], bank_a[b][:, :].rearrange("p (r t) -> p r t", t=P))
                    act.copy(kT[b][:, :, :], bank_b[b][:, :].rearrange("p (r t) -> p r t", t=P)).then_inc(qkT_done[b], 1)
                for b in range(B):
                    act.wait_ge(gate_state_ready[b], n)
                    act.activation(th[b][:, :], bank_b[b][:, 0:D], ACT.Tanh, scale=0.5).then_inc(th_done[b], 1)
                for b in range(B):
                    act.wait_ge(o_g_done[b], n)
                    act.activation(o_sq[b][:, :, :], o_g[b][:, :, :], ACT.Square).then_inc(o_sq_done[b], 1)
                for b in range(B):
                    act.wait_ge(oT_ready[b], n)
                    for k in range(KC):
                        last = act.activation(oT[b][:, k, :], bank_a[b][:, k * P:(k + 1) * P], ACT.Copy,
                                              scale=norm_half[:, k:k + 1])
                    last.then_inc(oT_done[b], 1)
                for b in range(B):
                    act.wait_ge(h2T_ready[b], n)
                    act.copy(h2T[:, :, bass.ds((n + (b * NCH - 1)) * P, P)],
                             bank_b[b][:, 0:D].rearrange("p (k t) -> p k t", k=KC)).then_inc(h2T_done[b], 1)

            for b in range(B):
                act.wait_ge(h2_stored[b], 16 * NCH)
            act.wait_ge(gap_done, 1)
            act.activation(weight_e[:, :, :], gap[:, :, :], ACT.Exp)
            act.activation(shared_th[:, :], logits[:, :, E], ACT.Tanh, scale=0.5).then_inc(exp_done, 1)

            def shared_silu(first):
                with act.Fori(first, first + SHARED_STEPS // 2) as q:
                    for m in range(SM):
                        act.wait_ge(s_gu_ready, q * SM + (m + 1))
                        act.wait_ge(s_hid_done, q * SM + max(m - 1, 0))
                        act.activation(s_silu[m % 2][:, :], bank[2 * (m % 2)][:, :], ACT.Silu).then_inc(s_silu_done, 1)

            def job_step(i, u, parts):
                s = i * 4 + u
                if "x" in parts:
                    act.wait_ge(xeT_ready, s + 1)
                    at_least(act, gu_ready, s - 1)
                    act.copy(xeT[u % 2][:, :, :], bank[u % 2][:, 0:D].rearrange("p (k t) -> p k t", k=KC)).then_inc(xeT_done, 1)
                if "g" in parts:
                    act.wait_ge(gu_ready, s)
                    at_least(act, hid_done, s - 2)
                    act.activation(sg[(u + 1) % 2][:, :], bank[2 + (u + 1) % 2][:, 0:I_E], ACT.Silu).then_inc(sg_done, 1)
                if "y" in parts:
                    act.wait_ge(ye_ready, s - 2)
                    at_least(act, y_stored[(u + 1) % 4], (i + (u - 3) // 4) * 16)
                    act.copy(ys[(u + 1) % 4][:, :], bank[6 + (u + 1) % 2][:, 0:D]).then_inc(ye_done, 1)

            shared_silu(0)
            run_jobs(act, job_step)
            shared_silu(SHARED_STEPS // 2)

        @block.gpsimd
        def _(pool):
            pool.memset(half_neg[:, :], -0.5).then_inc(consts_set, 1)
            pool.memset(settle_from[:, :], 0.0).then_inc(consts_set, 1)
            for b in range(B):
                pool.memset(state[b][:, :, :], 0.0).then_inc(state_done[b], 1)
                pool.memset(rot[b][:, :, :, :], 0.0).then_inc(consts_set, 1)
                pool.memset(k_dec[b][:, :, :], 0.0).then_inc(consts_set, 1)
            pool.wait_ge(consts_set, 6)
            pool.wait_ge(ln1_steps, 2 * NT + 1)
            pool.tensor_tensor(rstd1[:, :], rstd1[:, :], half_neg[:, :], ALU.pow).then_inc(rstd1_done, 1)
            with pool.Fori(1, NCH + 1) as n:
                for b in range(B):
                    half = HD // 2
                    pool.wait_ge(qk_done[b], n)
                    settle_pool()
                    sin = rope_t[:, bass.ds(n - 1, 1), 1, :]
                    pool.tensor_tensor(rope_b[b][:, :, 0:half], qk[b][:, :, half:HD],
                                       sin[:, :, 0:half].to_broadcast([P, 2 * H, half]), ALU.mult)
                    pool.tensor_tensor(rope_b[b][:, :, half:HD], qk[b][:, :, 0:half],
                                       sin[:, :, half:HD].to_broadcast([P, 2 * H, half]), ALU.mult).then_inc(rope_b_done[b], 1)
                for b in range(B):
                    pool.wait_ge(rot_done[b], n)
                    pool.wait_ge(gate_state_ready[b], n - 1)
                    pool.tensor_tensor(k_dec[b][:, :, 0:HD], rot[b][:, 1, :, 0:HD],
                                       decay_qk_t[:, 1, :].unsqueeze(2).to_broadcast([P, H, HD]), ALU.mult).then_inc(k_dec_done[b], 1)
                    pool.wait_ge(state_done[b], n)
                    pool.tensor_tensor(state_old[b][:, :, :], state[b][:, :, :], decay_s_t[:, :, :],
                                       ALU.mult).then_inc(state_old_done[b], 1)
                for b in range(B):
                    pool.wait_ge(ss_eps_done[b], n)
                    pool.tensor_tensor(rms[b][:, :], ss_eps[b][:, :], half_neg[:, :], ALU.pow).then_inc(rms_done[b], 1)
                for b in range(B):
                    pool.wait_ge(var2_done[b], n)
                    pool.tensor_tensor(rstd2[b][:, :], var2[b][:, :], half_neg[:, 0:1], ALU.pow).then_inc(rstd2_done[b], 1)
                for b in range(B):
                    pool.wait_ge(xn2_done[b], n)
                    pool.tensor_tensor(h2_scaled[b][:, :], xn2[b][:, :], mod_rows[b][:, 2, :], ALU.mult).then_inc(h2_scaled_done[b], 1)
                    pool.wait_ge(h2_scaled_done[b], n)
                    pool.wait_ge(h2T_ready[b], n - 1)
                    pool.wait_ge(h2_stored[b], (n - 1) * 16)
                    pool.tensor_tensor(h2[b][:, :], h2_scaled[b][:, :], mod_rows[b][:, 1, :], ALU.add).then_inc(h2_done[b], 1)

            for b in range(B):
                pool.wait_ge(h2_stored[b], 16 * NCH)
                pool.wait_ge(h2T_done[b], NCH)
            pool.memset(ws_gu[:, :, :, SI:SM * P], 0.0).then_inc(ws_zero, 1)
            pool.memset(ws_d[:, SM - 1, :], 0.0).then_inc(ws_zero, 1)
            pool.iota(iota_f[:, :], [[1, P]], base=0, channel_multiplier=0, allow_small_or_imprecise_dtypes=True).then_inc(iota_done, 1)
            pool.iota(token_id[:, :], [[P, NT]], base=0, channel_multiplier=1, allow_small_or_imprecise_dtypes=True).then_inc(iota_done, 1)
            pool.memset(ones[:, :], 1.0).then_inc(iota_done, 1)
            pool.memset(one_row[:, :], 1.0).then_inc(iota_done, 1)
            pool.memset(zero_r[:, :].bitcast(F32), 0.0).then_inc(iota_done, 1)

            def gather_job(i, u):
                pool.tensor_copy(idx[u][:, :], token_of[:, bass.ds(i * 4 + u, 1)]).then_inc(idx_done, 1)
                pool.wait_ge(idx_done, i * 4 + (u + 1))
                settle_pool()
                pool.indirect_dma_start(xg[u][:, :], None, h2_rows, bass.IndirectOffsetOnAxis(ap=idx[u][:, 0:1], axis=0)).then_inc(gathered[u], 16)

            pool.wait_ge(tokens_done, 1)
            for u in range(4):
                gather_job(0, u)
            with pool.Fori(1, NJ // 4) as i:
                for u in range(4):
                    pool.wait_ge(gathered[u], i * 16)
                    pool.wait_ge(xeT_ready, i * 4 + (u - 3))
                    gather_job(i, u)
            for u in range(4):
                pool.wait_ge(y_stored[u], 16 * (NJ // 4))
            with pool.Fori(0, NT // 2) as i:
                for u in range(2):
                    pool.wait_ge(result_done[u], i)
                    for k in range(TOPK):
                        m = u * TOPK + k
                        pool.wait_ge(y_back[m], i * 16)
                        pool.tensor_copy(cidx[m][:, :], slot[:, bass.ds(i * 2 * TOPK + m, 1)]).then_inc(cidx_done, 1)
                        pool.wait_ge(cidx_done, i * 2 * TOPK + (m + 1))
                        settle_pool()
                        pool.indirect_dma_start(yg[m][:, :], None, y_rows,
                                                bass.IndirectOffsetOnAxis(ap=cidx[m][:, 0:1], axis=0)).then_inc(y_back[m], 16)

        @block.vector
        def _(dve):
            dve.wait_ge(c_silu_done, 1)
            dve.tensor_copy(c_rows[:, :, :, :], c_silu[:, :, :].unsqueeze(3).to_broadcast([P, KC, B, P])).then_inc(c_rows_done, 1)
            for t in range(NT):
                if t % 4 == 0:
                    dve.wait_ge(x_in[t // 4], 16)
                dve.bn_stats(bn[:, t, :], x_all[:, t, :]).then_inc(ln1_steps, 1)
            dve.wait_ge(ln1_steps, NT)
            for t in range(NT):
                dve.bn_aggr(mean_var[:, t, :], bn[:, t, :]).then_inc(ln1_steps, 1)
            dve.wait_ge(ln1_steps, 2 * NT)
            dve.tensor_scalar(rstd1[:, :], mean_var[:, :, 1], LN_EPS, None, ALU.add).then_inc(ln1_steps, 1)
            dve.wait_ge(mod_cols_ready, 1)
            dve.tensor_copy(mod_cols[:, 0, :, :], bank_a[0][:, 0:KC * B].rearrange("p (k b) -> p k b", b=B)).then_inc(mod_cols_done, 1)
            dve.tensor_scalar(mod_cols[:, 1, :, :], bank_a[0][:, KC * B:2 * KC * B].rearrange("p (k b) -> p k b", b=B),
                              1.0, None, ALU.add).then_inc(mod_cols_done, 1)
            dve.wait_ge(consts_in, 16 * 7)
            dve.tensor_scalar(norm_half[:, :], norm_col[:, :], 0.5, None, ALU.mult).then_inc(mod_cols_done, 1)
            dve.wait_ge(rstd1_done, 1)
            dve.wait_ge(w_in_in, 16 * 6)
            steps = 0
            for b in range(B):
                dve.wait_ge(mod_rows_ready[b], 1)
                raw = [score_bank[2 * b + i // 2][:, 2 * (i % 2):2 * (i % 2) + 2, :].rearrange("p a t -> p (a t)") for i in range(4)]
                for i in (0, 3):
                    for op in (lambda: dve.tensor_scalar(gate_sgn[:, :], raw[i], 0.0, 2.0, ALU.is_ge, ALU.mult),
                               lambda: dve.scalar_tensor_tensor(gate_abs[:, :], gate_sgn[:, :], 1.0, raw[i], ALU.subtract, ALU.mult),
                               lambda: dve.tensor_scalar(gate_max[:, :], gate_abs[:, :], GATE_MIN, None, ALU.max),
                               lambda: dve.scalar_tensor_tensor(mod_rows[b][:, i, :], gate_sgn[:, :], 1.0, gate_max[:, :],
                                                                ALU.subtract, ALU.mult)):
                        op().then_inc(gate_steps, 1)
                        steps += 1
                        dve.wait_ge(gate_steps, steps)
                dve.tensor_copy(mod_rows[b][:, 1, :], raw[1])
                dve.tensor_scalar(mod_rows[b][:, 2, :], raw[2], 1.0, None, ALU.add)
                dve.tensor_tensor(w_og[b][:, :, :], w_o[:, :, :], mod_rows[b][:, 0, :].unsqueeze(1).to_broadcast([P, KC, D]),
                                  ALU.mult).then_inc(mod_rows_done, 1)

            with dve.Fori(1, NCH + 1) as n:
                tile = [n - 1, n + (NCH - 1)]
                for b in range(B):
                    dve.wait_ge(xT_ready[b], n - 1)
                    dve.tensor_scalar(xn[b][:, :], x_all[:, bass.ds(tile[b], 1), :], mean_var[:, bass.ds(tile[b], 1), 0],
                                      rstd1[:, bass.ds(tile[b], 1)], ALU.subtract, ALU.mult).then_inc(xn_done[b], 1)
                for b in range(B):
                    dve.wait_ge(qk_done[b], n)
                    dve.tensor_tensor(rope_a[b][:, :, :], qk[b][:, :, :],
                                      rope_t[:, bass.ds(n - 1, 1), 0, :].to_broadcast([P, 2 * H, HD]), ALU.mult).then_inc(rope_a_done[b], 1)
                    dve.wait_ge(rope_a_done[b], n)
                    dve.wait_ge(rope_b_done[b], n)
                    dve.tensor_tensor(rot[b][:, :, :, 0:HD], rope_a[b][:, :, :].rearrange("p (s h) d -> p s h d", s=2),
                                      rope_b[b][:, :, :].rearrange("p (s h) d -> p s h d", s=2), ALU.add).then_inc(rot_done[b], 1)
                for b in range(B):
                    dve.wait_ge(scores_ready[b], n)
                    for g in range(HG):
                        last = dve.tensor_tensor(probs[b][:, g], score_bank[g][:, :, :], decay_t[:, g, :, :], ALU.mult)
                    last.then_inc(probs_done[b], 1)
                for b in range(B):
                    dve.wait_ge(th_done[b], n)
                    dve.tensor_tensor(state_new[b][:, :, :], bank_b[b][:, D:2 * D].rearrange("p (r e) -> p r e", r=NR),
                                      state_mask_t[:, :, :], ALU.mult).then_inc(state_new_done[b], 1)
                    dve.wait_ge(o_ready[b], n)
                    dve.wait_ge(state_new_done[b], n)
                    dve.wait_ge(state_old_done[b], n)
                    dve.tensor_tensor(state[b][:, :, :], state_old[b][:, :, :], state_new[b][:, :, :], ALU.add).then_inc(state_done[b], 1)
                    dve.tensor_tensor(heads(o_i[b][:, :]), heads(bank_a[b][:, D:2 * D]),
                                      decay_qk_t[:, 0, :].unsqueeze(2).to_broadcast([P, H, HD]), ALU.mult).then_inc(o_steps[b], 1)
                    dve.wait_ge(o_steps[b], n * 2 - 1)
                    dve.tensor_tensor(o_t[b][:, :], bank_a[b][:, 0:D], o_i[b][:, :], ALU.add).then_inc(o_steps[b], 1)
                    dve.wait_ge(o_steps[b], n * 2)
                    dve.scalar_tensor_tensor(o_g[b][:, :, :], heads(th[b][:, :]), 1.0, heads(o_t[b][:, :]),
                                             ALU.add, ALU.mult).then_inc(o_g_done[b], 1)
                for b in range(B):
                    dve.wait_ge(o_sq_done[b], n)
                    dve.tensor_reduce(ss[b][:, :], o_sq[b][:, :, :], AX.X, ALU.add).then_inc(ss_done[b], 1)
                    dve.wait_ge(ss_done[b], n)
                    dve.tensor_scalar(ss_eps[b][:, :], ss[b][:, :], 1.0 / (4 * HD), RMS_EPS, ALU.mult, ALU.add).then_inc(ss_eps_done[b], 1)
                for b in range(B):
                    dve.wait_ge(rms_done[b], n)
                    dve.tensor_tensor(o_n[b][:, :, :], o_g[b][:, :, :], rms[b][:, :].unsqueeze(2).to_broadcast([P, H, HD]),
                                      ALU.mult).then_inc(o_n_done[b], 1)
                for b in range(B):
                    dve.wait_ge(y_ready[b], n)
                    dve.tensor_tensor(x_all[:, bass.ds(tile[b], 1), :], bank_b[b][:, 0:D].unsqueeze(1),
                                      x_all[:, bass.ds(tile[b], 1), :], ALU.add).then_inc(x2_done[b], 1)
                    dve.wait_ge(x2_done[b], n)
                    settle_dve()
                    dve.bn_stats(bn2[b][:, :], x_all[:, bass.ds(tile[b], 1), :]).then_inc(ln2_steps[b], 1)
                    dve.wait_ge(ln2_steps[b], n * 2 - 1)
                    settle_dve()
                    dve.bn_aggr(mv2[b][:, :], bn2[b][:, :]).then_inc(ln2_steps[b], 1)
                    dve.wait_ge(ln2_steps[b], n * 2)
                    dve.tensor_scalar(var2[b][:, :], mv2[b][:, 1:2], LN_EPS, None, ALU.add).then_inc(var2_done[b], 1)
                for b in range(B):
                    dve.wait_ge(rstd2_done[b], n)
                    dve.wait_ge(h2_scaled_done[b], n - 1)
                    dve.tensor_scalar(xn2[b][:, :], x_all[:, bass.ds(tile[b], 1), :], mv2[b][:, 0:1], rstd2[b][:, 0:1],
                                      ALU.subtract, ALU.mult).then_inc(xn2_done[b], 1)

            for b in range(B):
                dve.wait_ge(h2_stored[b], 16 * NCH)
            links = 0

            def link(instruction):
                nonlocal links
                links += 1
                instruction.then_inc(route, 1)
                dve.wait_ge(route, links)

            def per_choice(ap):
                return ap.unsqueeze(2).to_broadcast([P, NT, TOPK, E])

            dve.wait_ge(logits_ready, 1)
            link(dve.tensor_copy(logits[:, :, :], ROUTE_BANK.rearrange("p (t e) -> p t e", t=NT)[:, :, 0:E + 1]))
            for t in range(NT):
                last = dve.max(top8[:, t, :], logits[:, t, 0:E])
            link(last)
            dve.tensor_tensor(gap[:, :, :], top8[:, :, 0:TOPK], top8[:, :, 0:1].to_broadcast([P, NT, TOPK]), ALU.subtract).then_inc(gap_done, 1)
            for t in range(NT):
                last = dve.max_index(top8_i[:, t, :], top8[:, t, :], logits[:, t, 0:E])
            link(last)
            link(dve.tensor_copy(choice[:, :].rearrange("p (t k) -> p t k", k=TOPK), top8_i[:, :, 0:TOPK]))
            dve.wait_ge(iota_done, 5)
            dve.tensor_scalar(before[:, :], iota_f[:, :], token_id[:, 0:1], None, ALU.is_gt)
            link(dve.tensor_tensor(onehot[:, :, :], iota_f[:, 0:E].unsqueeze(1).to_broadcast([P, NQ, E]),
                                   choice[:, :].unsqueeze(2).to_broadcast([P, NQ, E]), ALU.is_equal))
            with nc.allow_low_precision(reason="counts up to 16 are exact in bfloat16"):
                link(dve.tensor_reduce(mask[:, :, :], onehot[:, :, :].rearrange("p (t k) e -> p t e k", k=TOPK), AX.X, ALU.add))
                dve.tensor_reduce(mask_sum[:, :], mask[:, :, :].rearrange("p t e -> p e t"), AX.X, ALU.add).then_inc(masks_done, 1)
            dve.wait_ge(exp_done, 1)
            link(dve.tensor_reduce(weight_sum[:, :], weight_e[:, :, :], AX.X, ALU.add))
            link(dve.reciprocal(weight_rec[:, :], weight_sum[:, :]))
            dve.tensor_scalar(shared_gate[:, :], shared_th[:, :], 0.5, 0.5, ALU.mult, ALU.add)
            link(dve.tensor_tensor(weight[:, :, :], weight_e[:, :, :], weight_rec[:, :].unsqueeze(2).to_broadcast([P, NT, TOPK]), ALU.mult))
            dve.wait_ge(counts_ready, 1)
            link(dve.tensor_scalar(count_i[:, :], COUNT_BANK[:, NT * E:NT * E + E], float(P - 1), None, ALU.add))
            link(dve.tensor_scalar(blocks_i[:, :], count_i[:, :], 7, None, ALU.logical_shift_right))
            link(dve.tensor_copy(blocks[:, :], blocks_i[:, :]))
            link(dve.tensor_tensor_scan(block_end[:, :], one_row[:, :], blocks[:, :], 0.0, ALU.mult, ALU.add))
            link(dve.tensor_tensor(block_start[:, :], block_end[:, :], blocks[:, :], ALU.subtract))
            link(dve.scalar_tensor_tensor(place[:, :, :], block_start[:, :].unsqueeze(1).to_broadcast([P, NT, E]), float(P),
                                          COUNT_BANK[:, 0:NT * E].rearrange("p (t e) -> p t e", e=E), ALU.mult, ALU.add))
            link(dve.tensor_tensor(placed[:, :, :].rearrange("p (t k) e -> p t k e", k=TOPK),
                                   onehot[:, :, :].rearrange("p (t k) e -> p t k e", k=TOPK), per_choice(place[:, :, :]), ALU.mult))
            link(dve.tensor_reduce(slot_f[:, :], placed[:, :, :], AX.X, ALU.add))
            link(dve.tensor_copy(slot[:, :], slot_f[:, :]))
            link(dve.tensor_scalar(slot_blk_i[:, :], slot[:, :], 7, None, ALU.logical_shift_right))
            link(dve.tensor_scalar(slot_row_i[:, :], slot[:, :], P - 1, None, ALU.bitwise_and))
            dve.tensor_copy(slot_blk[:, :], slot_blk_i[:, :])
            link(dve.tensor_copy(slot_row[:, :], slot_row_i[:, :]))
            link(dve.tensor_tensor(job_ge[:, :, :], block_end[0:1, :].unsqueeze(1).to_broadcast([1, NJ, E]),
                                   iota_f[0:1, 0:NJ].unsqueeze(2).to_broadcast([1, NJ, E]), ALU.is_le))
            link(dve.tensor_reduce(job_sum[:, :], job_ge[:, :, :], AX.X, ALU.add))
            link(dve.tensor_scalar(job_expert[:, :], job_sum[:, :], float(E - 1), None, ALU.min))
            with dve.Fori(0, NT // 2) as i:
                for u in range(2):
                    dve.wait_ge(hot_used[u], i)
                    for k in range(TOPK):
                        q = i * (2 * TOPK) + (u * TOPK + k)
                        dve.tensor_scalar(row_hot[:, u, k, :], iota_f[:, :], slot_row[:, bass.ds(q, 1)], None, ALU.is_equal)
                        last = dve.tensor_scalar(blk_hot[:, u, k, :], iota_f[:, 0:NJ], slot_blk[:, bass.ds(q, 1)],
                                                 token_id[:, bass.ds(i * 2 + u, 1)], ALU.is_equal, ALU.mult)
                    last.then_inc(hot_done[u], 1)
            dve.wait_ge(tokens_ready, 1)
            dve.tensor_copy(token_of[:, :], ROUTE_BANK[:, 0:NJ]).then_inc(tokens_done, 1)

            def shared(first):
                with dve.Fori(first, first + SHARED_STEPS // 2) as q:
                    dve.wait_ge(s_y_ready, q * SHARED_T)
                    for m in range(SM):
                        dve.wait_ge(s_silu_done, q * SM + (m + 1))
                        dve.tensor_tensor(s_hid[:, m, :], s_silu[m % 2][:, :], bank[2 * (m % 2) + 1][:, :],
                                          ALU.mult).then_inc(s_hid_done, 1)
                    for t in range(SHARED_T):
                        dve.wait_ge(s_y_ready, q * SHARED_T + (t + 1))
                        dve.tensor_scalar(acc[:, bass.ds(q * SHARED_T + t, 1), :], bank[6 + t % 2][:, 0:D].unsqueeze(1),
                                          shared_gate[:, bass.ds(q * SHARED_T + t, 1)], None, ALU.mult).then_inc(s_y_done, 1)

            def job_step(i, u, parts):
                s = i * 4 + u
                if "g" in parts:
                    dve.wait_ge(sg_done, s)
                    at_least(dve, hidT_ready, s - 2)
                    dve.tensor_tensor(hid[(u + 1) % 2][:, :], sg[(u + 1) % 2][:, :], bank[2 + (u + 1) % 2][:, I_E:2 * I_E],
                                      ALU.mult).then_inc(hid_done, 1)
                if "h" in parts:
                    dve.wait_ge(hidT_ready, s - 1)
                    at_least(dve, ye_ready, s - 3)
                    dve.tensor_copy(hidT[u % 2][:, :, :], bank[4 + u % 2][0:HC, 0:2 * P].rearrange("p (c t) -> p c t", c=2)).then_inc(hidT_done, 1)

            shared(0)
            run_jobs(dve, job_step)
            shared(SHARED_STEPS // 2)

            for b in range(B):
                with dve.Fori(b * NT // 4, (b + 1) * NT // 4) as i:
                    for u in range(2):
                        n0 = i * 2 * (TOPK + 1) + u * (TOPK + 1)
                        t = i * 2 + u
                        dve.wait_ge(result_done[u], i)
                        for k in range(TOPK):
                            dve.wait_ge(y_back[u * TOPK + k], i * 16 + 16)
                            if k:
                                dve.wait_ge(sums, n0 + k)
                            dve.scalar_tensor_tensor(total[u][:, :].unsqueeze(1), yg[u * TOPK + k][:, :].unsqueeze(1), weight[:, bass.ds(t, 1), k],
                                                     total[u][:, :].unsqueeze(1) if k else acc[:, bass.ds(t, 1), :],
                                                     ALU.mult, ALU.add).then_inc(sums, 1)
                        dve.wait_ge(sums, n0 + TOPK)
                        dve.tensor_tensor(total_g[u][:, :], total[u][:, :], mod_rows[b][:, 3, :], ALU.mult).then_inc(sums, 1)
                        dve.wait_ge(sums, n0 + TOPK + 1)
                        dve.wait_ge(stored[u], i * 16)
                        dve.tensor_tensor(result[u][:, :].unsqueeze(1), total_g[u][:, :].unsqueeze(1), x_all[:, bass.ds(t, 1), :],
                                          ALU.add).then_inc(result_done[u], 1)

        @block.tensor
        def _(pe):
            pe.wait_ge(w_mod_in, 16)
            pe.wait_ge(c_rows_done, 1)
            for i in range(2):
                for m in range(KC):
                    for k in range(KC):
                        last = pe.matmul(bank_a[0][:, (i * KC + m) * B:(i * KC + m + 1) * B],
                                         w_mod[:, k, i * D + m * P:i * D + (m + 1) * P], c_silu[:, k, :],
                                         start=(k == 0), stop=(k == KC - 1))
            last.then_inc(mod_cols_ready, 1)
            for b in range(B):
                for i in range(2):
                    for k in range(KC):
                        last = pe.matmul(score_bank[2 * b + i][:, :, :].rearrange("p a t -> p (a t)"), c_rows[:, k, b, :],
                                         w_mod[:, k, 2 * D + i * 512:2 * D + (i + 1) * 512], start=(k == 0), stop=(k == KC - 1))
                last.then_inc(mod_rows_ready[b], 1)
            pe.wait_ge(consts_in, 16 * 7)
            pe.wait_ge(w_in_in, 16 * 6)
            pe.wait_ge(mod_cols_done, 2)

            with pe.Fori(1, NCH + 1) as n:
                for b in range(B):
                    pe.wait_ge(xn_done[b], n)
                    pe.wait_ge(oT_done[b], n - 1)
                    for k in range(KC):
                        last = pe.transpose(bank_a[b][:, k * P:(k + 1) * P], xn[b][:, k * P:(k + 1) * P], ident[:, :])
                    last.then_inc(xT_ready[b], 1)
                for b in range(B):
                    pe.wait_ge(hT_done[b], n)
                    for k in range(KC):
                        last = pe.matmul(bank_a[b][:, :], hT[b][:, k, :], w_in[:, k, 0:2 * D], start=(k == 0), stop=(k == KC - 1))
                    last.then_inc(qk_ready[b], 1)
                    pe.wait_ge(h2T_done[b], n - 1)
                    for k in range(KC):
                        pe.matmul(bank_b[b][:, 0:D], hT[b][:, k, :], w_in[:, k, 2 * D:3 * D], start=(k == 0), stop=(k == KC - 1))
                    for k in range(KC):
                        last = pe.matmul(bank_b[b][0:HD, D:D + P], w_in[:, k, 3 * D:3 * D + HD], hT[b][:, k, :],
                                         start=(k == 0), stop=(k == KC - 1))
                    last.then_inc(vg_ready[b], 1)
                for b in range(B):
                    pe.wait_ge(rot_done[b], n)
                    pe.wait_ge(vg_done[b], n)
                    for s, target in ((0, bank_a[b]), (1, bank_b[b])):
                        for r in range(NR):
                            last = pe.transpose(target[:, r * P:(r + 1) * P],
                                                rot[b][:, s, HG * r:HG * (r + 1), :].rearrange("p h d -> p (h d)"), ident[:, :])
                    last.then_inc(qkT_ready[b], 1)
                pe.wait_ge(mod_rows_done, 2)
                for b in range(B):
                    pe.wait_ge(qkT_done[b], n)
                    if b == 0:
                        pe.wait_ge(probs_done[1], n - 1)
                    else:
                        pe.wait_ge(probs_done[0], n)
                    for r in range(NR):
                        for g in range(HG):
                            q0 = PAD * g
                            last = pe.matmul(score_bank[g][:, r, :], kT[b][q0:q0 + HD, r, :], qT[b][q0:q0 + HD, r, :],
                                             start=True, stop=True)
                    last.then_inc(scores_ready[b], 1)
                    pe.matmul(bank_b[b][:, 0:D], g1T[b][:, :], w_g2[:, :], start=True, stop=True)
                    pe.wait_ge(k_dec_done[b], n)
                    for r in range(NR):
                        e = HG * HD
                        last = pe.matmul(bank_b[b][:, D + r * e:D + (r + 1) * e],
                                         k_dec[b][:, HG * r:HG * (r + 1), :].rearrange("p h d -> p (h d)"),
                                         v[b][:, r * e:(r + 1) * e], start=True, stop=True)
                    last.then_inc(gate_state_ready[b], 1)
                for b in range(B):
                    e = HG * HD
                    pe.wait_ge(state_done[b], n)
                    for r in range(NR):
                        pe.matmul(bank_a[b][:, D + r * e:D + (r + 1) * e], qT[b][:, r, :], state[b][:, r, :], start=True, stop=True)
                    pe.wait_ge(probs_done[b], n)
                    for h in range(H):
                        last = pe.matmul(bank_a[b][:, h * HD:(h + 1) * HD], probs[b][:, h % HG, h // HG, :],
                                         v[b][:, h * HD:(h + 1) * HD], start=True, stop=True)
                    last.then_inc(o_ready[b], 1)
                for b in range(B):
                    pe.wait_ge(o_n_done[b], n)
                    for k in range(KC):
                        last = pe.transpose(bank_a[b][:, k * P:(k + 1) * P],
                                            o_n[b][:, :, :].rearrange("p h d -> p (h d)")[:, k * P:(k + 1) * P], ident[:, :])
                    last.then_inc(oT_ready[b], 1)
                for b in range(B):
                    pe.wait_ge(oT_done[b], n)
                    pe.wait_ge(state_done[b], n + 1)
                    for k in range(KC):
                        last = pe.matmul(bank_b[b][:, 0:D], oT[b][:, k, :], w_og[b][:, k, :], start=(k == 0), stop=(k == KC - 1))
                    last.then_inc(y_ready[b], 1)
                for b in range(B):
                    pe.wait_ge(h2_done[b], n)
                    for k in range(KC):
                        last = pe.transpose(bank_b[b][:, k * P:(k + 1) * P], h2[b][:, k * P:(k + 1) * P], ident[:, :])
                    last.then_inc(h2T_ready[b], 1)

            for b in range(B):
                pe.wait_ge(h2T_done[b], NCH)
            pe.wait_ge(w_r_in, 16)
            for t in range(NT):
                for k in range(KC):
                    last = pe.matmul(ROUTE_BANK[:, t * 2 * E:t * 2 * E + E + 1], h2T[:, k, t * P:(t + 1) * P], w_r[:, k, :],
                                     start=(k == 0), stop=(k == KC - 1))
            last.then_inc(logits_ready, 1)

            pe.wait_ge(masks_done, 1)
            pe.matmul(COUNT_BANK[:, 0:NT * E], before[:, :], mask[:, :, :].rearrange("p t e -> p (t e)"), start=True, stop=False)
            for d in range(1, NT):
                pe.matmul(COUNT_BANK[:, d * E:NT * E], ones[:, :], mask[:, 0:NT - d, :].rearrange("p t e -> p (t e)"),
                          start=False, stop=(d == NT - 1))
            pe.matmul(COUNT_BANK[:, NT * E:NT * E + E], ones[:, :], mask_sum[:, :], start=True, stop=True).then_inc(counts_ready, 1)

            pe.matmul(ROUTE_BANK[:, 0:NJ], zero_r[:, :], zero_r[:, 0:NJ], start=True, stop=False)
            with pe.Fori(0, NT // 2) as i:
                for u in range(2):
                    pe.wait_ge(hot_done[u], i + 1)
                    for k in range(TOPK):
                        last = pe.matmul(ROUTE_BANK[:, 0:NJ], row_hot[:, u, k, :], blk_hot[:, u, k, :], start=False, stop=False)
                    last.then_inc(hot_used[u], 1)
            pe.matmul(ROUTE_BANK[:, 0:NJ], zero_r[:, :], zero_r[:, 0:NJ], start=False, stop=True).then_inc(tokens_ready, 1)
            pe.wait_ge(ws_in, 16 * 4)
            pe.wait_ge(ws_zero, 2)

            def shared(first):
                with pe.Fori(first, first + SHARED_STEPS // 2) as q:
                    for m in range(SM):
                        if m >= 2:
                            pe.wait_ge(s_hid_done, q * SM + (m - 1))
                        for g in range(2):
                            for k in range(KC):
                                last = pe.matmul(bank[2 * (m % 2) + g][:, :], ws_gu[:, k, g, m * P:(m + 1) * P],
                                                 h2T[:, k, bass.ds(q * 512, 512)], start=(k == 0), stop=(k == KC - 1))
                        last.then_inc(s_gu_ready, 1)
                    pe.wait_ge(s_hid_done, q * SM + SM)
                    for t in range(SHARED_T):
                        pe.wait_ge(s_y_done, q * SHARED_T + max(t - 1, 0))
                        for m in range(SM):
                            last = pe.matmul(bank[6 + t % 2][:, 0:D], s_hid[:, m, t * P:(t + 1) * P], ws_d[:, m, :],
                                             start=(m == 0), stop=(m == SM - 1))
                        last.then_inc(s_y_ready, 1)

            def expert_of(job):
                return pe.value_load(job_expert[0:1, bass.ds(job, 1)], min_val=0, max_val=E - 1)

            def job_step(i, u, parts):
                s = i * 4 + u
                if "x" in parts:
                    pe.wait_ge(gathered[u], i * 16 + 16)
                    at_least(pe, xeT_done, s - 1)
                    for k in range(KC):
                        last = pe.transpose(bank[u % 2][:, k * P:(k + 1) * P], xg[u][:, k * P:(k + 1) * P], ident[:, :])
                    last.then_inc(xeT_ready, 1)
                if "g" in parts:
                    e = expert_of(s - 1)
                    pe.wait_ge(xeT_done, s)
                    at_least(pe, hid_done, s - 2)
                    for k in range(KC):
                        last = pe.matmul(bank[2 + (u + 1) % 2][:, 0:2 * I_E], xeT[(u + 1) % 2][:, k, :],
                                         w_gu_flat[:, bass.ds(e * (KC * 2 * I_E) + k * 2 * I_E, 2 * I_E)], start=(k == 0), stop=(k == KC - 1))
                    last.then_inc(gu_ready, 1)
                if "h" in parts:
                    pe.wait_ge(hid_done, s - 1)
                    at_least(pe, hidT_done, s - 3)
                    for h in range(2):
                        last = pe.transpose(bank[4 + u % 2][0:HC, h * P:(h + 1) * P], hid[u % 2][:, h * HC:(h + 1) * HC], ident[:, :])
                    last.then_inc(hidT_ready, 1)
                if "y" in parts:
                    e = expert_of(s - 3)
                    pe.wait_ge(hidT_done, s - 2)
                    at_least(pe, ye_done, s - 4)
                    for h in range(2):
                        last = pe.matmul(bank[6 + (u + 1) % 2][:, 0:D], hidT[(u + 1) % 2][:, h, :],
                                         w_d_flat[:, bass.ds(e * (2 * D) + h * D, D)], start=(h == 0), stop=(h == 1))
                    last.then_inc(ye_ready, 1)

            shared(0)
            pe.wait_ge(s_y_done, NT // 2)
            pe.wait_ge(w_gu_in, 16)
            pe.wait_ge(w_d_in, 16)
            run_jobs(pe, job_step)
            for done in (xeT_done, hid_done, ye_done):
                pe.wait_ge(done, NJ)
            shared(SHARED_STEPS // 2)


def constants():
    f = np.float32
    slope = (2.0 ** (-8.0 * (np.arange(H, dtype=f) + 1.0) / H)).astype(f)
    log_lam = -slope
    theta = (f(10000.0) ** (-2.0 * np.arange(HD // 2, dtype=f) / HD)).astype(f)
    ang = np.arange(N, dtype=f)[:, None] * theta[None, :]
    cos, sin = np.cos(ang).astype(f), np.sin(ang).astype(f)
    rope = np.stack([np.concatenate([cos, cos], 1), np.concatenate([-sin, sin], 1)], 1)
    i = np.arange(P, dtype=f)
    diff = i[None, :] - i[:, None]
    dec = np.where(diff[:, None, :] >= 0, np.exp(log_lam[None, :, None] * np.maximum(diff, 0)[:, None, :]), 0).astype(f)
    decay = dec.reshape(P, NR, HG, P).transpose(0, 2, 1, 3)
    dq = np.exp(log_lam[None] * (i[:, None] + 1)).astype(f)
    dk = np.exp(log_lam[None] * (P - 1 - i[:, None])).astype(f)
    mask = np.zeros((P, NR, HG, HD), f)
    for g in range(HG):
        mask[PAD * g:PAD * g + HD, :, g, :] = 1
    lam_c = np.exp(log_lam * P).astype(f).reshape(1, NR, HG, 1)
    return {
        "rope": rope.astype(f), "decay": np.ascontiguousarray(decay), "decay_qk": np.stack([dq, dk], 1),
        "decay_s": (mask * lam_c).reshape(P, NR, HG * HD), "state_mask": mask.reshape(P, NR, HG * HD), "ident": np.eye(P, dtype=f),
    }


def kernel(**inputs):
    import concourse.bacc as bacc
    from concourse.bass_utils import run_bass_kernel_spmd

    a = {k: np.asarray(v) for k, v in inputs.items()}
    shared_gu = a["L0_ffn_shared_gate_up"].reshape(2, SI, D).transpose(2, 0, 1)
    arrays = {
        "x": a["L0_attn_x"].reshape(B * N, D),
        "Wq": a["L0_attn_Wq"], "Wk": a["L0_attn_Wk"], "Wv": a["L0_attn_Wv"], "Wo": a["L0_attn_Wo"],
        "Wg1": a["L0_attn_Wg1"], "Wg2": a["L0_attn_Wg2"],
        "norm_w": a["L0_attn_norm_weight"].reshape(KC, P).T,
        "c": a["L0_c"].reshape(B, KC, P).transpose(2, 1, 0),
        "wmod": a["L0_wmod"],
        "router_w": np.concatenate([a["L0_ffn_gate_w"], a["L0_ffn_shared_gate_vec"]], 0).T,
        "expert_gu": a["L0_ffn_expert_gate_up"].transpose(0, 2, 1),
        "expert_d": a["L0_ffn_expert_down"].transpose(0, 2, 1),
        "shared_gu": shared_gu,
        "shared_d": a["L0_ffn_shared_down"].T,
    }
    arrays.update(constants())
    arrays = {f"in_{k}": np.ascontiguousarray(v) for k, v in arrays.items()}
    nc = bacc.Bacc("TRN2", target_bir_lowering=False, num_devices=1)
    args = [nc.dram_tensor(k, v.shape, mybir.dt.from_np(v.dtype), kind="ExternalInput").ap() for k, v in arrays.items()]
    out = nc.dram_tensor("out_rows", [B * N, D], F32, kind="ExternalOutput").ap()
    build(nc, *args, out)
    r = run_bass_kernel_spmd(nc, [arrays], core_ids=[0])
    return r.results[0]["out_rows"].reshape(B, N, D)
```

```python
from contextlib import ExitStack

import numpy as np

import concourse.bass as bass
from concourse import mybir

F32 = mybir.dt.float32
I32 = mybir.dt.int32
U32 = mybir.dt.uint32
BF16 = mybir.dt.bfloat16
F32R = mybir.dt.float32r
ALU = mybir.AluOpType
ACT = mybir.ActivationFunctionType
AX = mybir.AxisListType

P = 128
B, N, D = 2, 1024, 256
H, HD = 16, 16
KC = D // P
NCH = N // P
NT = B * NCH
HG = 4
NR = H // HG
PAD = P // HG
LN_EPS = 1e-5
RMS_EPS = 1e-6
GATE_MIN = 0.25
E, TOPK = 16, 4
I_E = 176
HC = I_E // 2
SI = 704
SM = -(-SI // P)
NQ = NT * TOPK
NJ = NT * TOPK + E
SHARED_T = 4
SHARED_STEPS = NT // SHARED_T


def at_least(eng, semaphore, value):
    if not (isinstance(value, int) and value <= 0):
        eng.wait_ge(semaphore, value)


def build(nc, x, Wq, Wk, Wv, Wo, Wg1, Wg2, norm_w, c, wmod, router_w, expert_gu, expert_d, shared_gu, shared_d,
          rope, decay, decay_q, decay_k, decay_s, state_mask, ident_in, out):
    h2_rows = nc.dram_tensor("h2_rows", [NT * P, D], F32, kind="Internal").ap()
    y_rows = nc.dram_tensor("y_rows", [NJ * P, D], F32, kind="Internal").ap()
    with ExitStack() as ctx, ExitStack() as attention, ExitStack() as routing:
        def sb(name, shape, dt=F32):
            return ctx.enter_context(nc.sbuf_tensor(name, shape, dt))

        def sem(name):
            return ctx.enter_context(nc.semaphore(name))

        def sem2(name):
            return [sem(f"{name}{b}") for b in range(B)]

        def sb2(name, shape, dt=F32):
            return [sb(f"{name}{b}", shape, dt) for b in range(B)]

        ident = sb("ident", [P, P])
        settle_from, settle_to = sb("settle_from", [1, 1]), sb("settle_to", [1, 32])
        x_all = sb("x_all", [P, NT, D])
        mod_rows = sb2("mod_rows", [P, 4, D])
        w_gu = sb("w_gu", [P, E, KC, 2 * I_E])
        w_r = sb("w_r", [P, KC, E + 1])
        h2T = sb("h2T", [P, KC, NT * P])

        def at(name, shape, dt=F32):
            return attention.enter_context(nc.sbuf_tensor(name, shape, dt))

        def at2(name, shape, dt=F32):
            return [at(f"{name}{b}", shape, dt) for b in range(B)]

        score_bank = [ctx.enter_context(nc.psum_tensor(f"score_bank{g}", [P, HG, P], F32)) for g in range(HG)]
        a_bank = [ctx.enter_context(nc.psum_tensor(f"a_bank{b}", [P, 512], F32)) for b in range(B)]
        v_bank = ctx.enter_context(nc.psum_tensor("v_bank", [P, 512], F32))
        g_bank = ctx.enter_context(nc.psum_tensor("g_bank", [P, 512], F32))

        w_in = at("w_in", [P, KC, 3 * D + HD])
        w_g2 = at("w_g2", [HD, D])
        w_o = at("w_o", [P, KC, D])
        w_og = at2("w_og", [P, KC, D])
        norm_half = at("norm_half", [P, KC])
        norm_col = at("norm_col", [P, KC])
        c_raw = at("c_raw", [P, KC, B])
        c_silu = at("c_silu", [P, KC, B])
        c_rows = at("c_rows", [P, KC, B, P])
        mod_cols = at("mod_cols", [P, 2, KC, B])
        gate_abs = at("gate_abs", [P, D])
        gate_sgn = at("gate_sgn", [P, D])
        gate_max = at("gate_max", [P, D])
        rope_t = at("rope_t", [P, NCH, 2, HD])
        decay_t = at("decay_t", [P, HG, NR, P])
        decay_q_t = at("decay_q_t", [P, NR, P])
        decay_k_t = at("decay_k_t", [P, H])
        decay_s_t = at("decay_s_t", [P, NR, HG * HD])
        state_mask_t = at("state_mask_t", [P, NR, HG * HD])
        half_neg = at("half_neg", [P, H])
        bn = at("bn", [P, NT, 6])
        mean_var = at("mean_var", [P, NT, 2])
        rstd1 = at("rstd1", [P, NT])

        xn = at2("xn", [P, D])
        hT = at2("hT", [P, KC, P])
        qk = at2("qk", [P, 2 * H, HD])
        v = at2("v", [P, D])
        g1T = at2("g1T", [HD, P])
        rope_a = at2("rope_a", [P, 2 * H, HD])
        rope_b = at2("rope_b", [P, 2 * H, HD])
        rot = at2("rot", [P, 2, H, PAD])
        k_dec = at2("k_dec", [P, H, PAD])
        qT = at2("qT", [P, NR, P])
        kT = at2("kT", [P, NR, P])
        probs_all = at("probs_all", [P, B, HG, NR, P])
        probs = [probs_all[:, b] for b in range(B)]
        w_mod = probs_all[:, :, :, :, :].rearrange("p b g r t -> p (b g r t)")[:, 0:KC * 6 * D].rearrange("p (k n) -> p k n", k=KC)
        state = at2("state", [P, NR, HG * HD])
        state_old = at2("state_old", [P, NR, HG * HD])
        state_new = at2("state_new", [P, NR, HG * HD])
        th = at2("th", [P, D])
        qdT = at2("qdT", [P, NR, P])
        oP = at2("oP", [P, NR, P])
        o_g = at2("o_g", [P, H, HD])
        o_sq = at2("o_sq", [P, H, HD])
        ss = at2("ss", [P, H])
        ss_eps = at2("ss_eps", [P, H])
        rms = at2("rms", [P, H])
        o_n = at2("o_n", [P, H, HD])
        oT = at2("oT", [P, KC, P])

        bn2 = at2("bn2", [P, 6])
        mv2 = at2("mv2", [P, 2])
        var2 = at2("var2", [P, 1])
        rstd2 = at2("rstd2", [P, 1])
        xn2 = at2("xn2", [P, D])
        h2_scaled = at2("h2_scaled", [P, D])
        h2 = at2("h2", [P, D])

        attention.close()
        w_d = sb("w_d", [HC, E, 2, D])
        ws_gu = sb("ws_gu", [P, KC, 2, SM * P])
        ws_d = sb("ws_d", [P, SM, D])
        weight = sb("weight", [P, NT, TOPK])
        shared_gate = sb("shared_gate", [P, NT])
        iota_f = sb("iota_f", [P, P])
        token_id = sb("token_id", [P, NT])
        slot = sb("slot", [P, NQ], I32)
        job_expert = sb("job_expert", [1, NJ], I32)
        token_of = sb("token_of", [P, NJ], I32)
        s_silu = [sb(f"s_silu{i}", [P, 512]) for i in range(2)]
        s_hid = sb("s_hid", [P, SM, 512])
        acc = sb("acc", [P, NT, D])
        def rt(name, shape, dt=F32):
            return routing.enter_context(nc.sbuf_tensor(name, shape, dt))

        logits = rt("logits", [P, NT, E + 1])
        top8 = rt("top8", [P, NT, 8])
        top8_i = rt("top8_i", [P, NT, 8], U32)
        choice = rt("choice", [P, NQ])
        gap = rt("gap", [P, NT, TOPK])
        weight_e = rt("weight_e", [P, NT, TOPK])
        weight_sum = rt("weight_sum", [P, NT])
        weight_rec = rt("weight_rec", [P, NT])
        shared_th = rt("shared_th", [P, NT])
        before = rt("before", [P, P], BF16)
        ones = rt("ones", [P, P], BF16)
        onehot = rt("onehot", [P, NQ, E])
        mask = rt("mask", [P, NT, E], BF16)
        mask_sum = rt("mask_sum", [P, E], BF16)
        count_i = rt("count_i", [P, E], I32)
        blocks_i = rt("blocks_i", [P, E], I32)
        blocks = rt("blocks", [P, E])
        one_row = rt("one_row", [P, E])
        block_end = rt("block_end", [P, E])
        block_start = rt("block_start", [P, E])
        place = rt("place", [P, NT, E])
        placed = rt("placed", [P, NQ, E])
        slot_f = rt("slot_f", [P, NQ])
        slot_blk_i = rt("slot_blk_i", [P, NQ], I32)
        slot_row_i = rt("slot_row_i", [P, NQ], I32)
        slot_blk = rt("slot_blk", [P, NQ])
        slot_row = rt("slot_row", [P, NQ])
        job_ge = rt("job_ge", [1, NJ, E])
        job_sum = rt("job_sum", [1, NJ])
        row_hot = rt("row_hot", [P, 2, TOPK, P], F32R)
        blk_hot = rt("blk_hot", [P, 2, TOPK, NJ], F32R)
        zero_r = rt("zero_r", [P, P], F32R)
        routing.close()
        idx = [sb(f"idx{i}", [P, 1], I32) for i in range(4)]
        xg = [sb(f"xg{i}", [P, D]) for i in range(4)]
        xeT = [sb(f"xeT{i}", [P, KC, P]) for i in range(2)]
        sg = [sb(f"sg{i}", [P, I_E]) for i in range(2)]
        hid = [sb(f"hid{i}", [P, I_E]) for i in range(2)]
        hidT = [sb(f"hidT{i}", [HC, 2, P]) for i in range(2)]
        ys = [sb(f"ys{i}", [P, D]) for i in range(4)]
        cidx = [sb(f"cidx{i}", [P, 1], I32) for i in range(2 * TOPK)]
        yg = [sb(f"yg{i}", [P, D]) for i in range(2 * TOPK)]
        total = [sb(f"total{i}", [P, D]) for i in range(2)]
        total_g = [sb(f"total_g{i}", [P, D]) for i in range(2)]
        result = [sb(f"result{i}", [P, D]) for i in range(2)]

        x_in = [sem(f"x_in{i}") for i in range(NT // 4)]
        consts_in, w_mod_in, c_in, w_in_in = sem("consts_in"), sem("w_mod_in"), sem("c_in"), sem("w_in_in")
        c_silu_done, c_rows_done = sem("c_silu_done"), sem("c_rows_done")
        mod_cols_ready, mod_cols_done = sem("mod_cols_ready"), sem("mod_cols_done")
        mod_rows_ready, mod_rows_done = sem2("mod_rows_ready"), sem("mod_rows_done")
        gate_steps = sem("gate_steps")
        consts_set = sem("consts_set")
        ln1_steps, rstd1_done = sem("ln1_steps"), sem("rstd1_done")

        xn_done, xT_ready, hT_done = sem2("xn_done"), sem2("xT_ready"), sem2("hT_done")
        qk_ready, vg_ready, qk_done, vg_done = sem2("qk_ready"), sem2("vg_ready"), sem2("qk_done"), sem2("vg_done")
        rope_a_done, rope_b_done, rot_done = sem2("rope_a_done"), sem2("rope_b_done"), sem2("rot_done")
        k_dec_done, qkT_ready, qkT_done = sem2("k_dec_done"), sem2("qkT_ready"), sem2("qkT_done")
        scores_ready, probs_done = sem2("scores_ready"), sem2("probs_done")
        gate_state_ready, th_done = sem2("gate_state_ready"), sem2("th_done")
        state_old_done, state_new_done, state_done = sem2("state_old_done"), sem2("state_new_done"), sem2("state_done")
        o_ready, o_copied, o_rows_ready, o_g_done = sem2("o_ready"), sem2("o_copied"), sem2("o_rows_ready"), sem2("o_g_done")
        qd_done = sem2("qd_done")
        o_sq_done, ss_done, ss_eps_done, rms_done, o_n_done = (sem2("o_sq_done"), sem2("ss_done"), sem2("ss_eps_done"),
                                                               sem2("rms_done"), sem2("o_n_done"))
        oT_ready, oT_done, y_ready, x2_done = sem2("oT_ready"), sem2("oT_done"), sem2("y_ready"), sem2("x2_done")
        ln2_steps, var2_done, rstd2_done, xn2_done = sem2("ln2_steps"), sem2("var2_done"), sem2("rstd2_done"), sem2("xn2_done")
        h2_scaled_done, h2_done, h2_stored = sem2("h2_scaled_done"), sem2("h2_done"), sem2("h2_stored")
        h2T_ready, h2T_done = sem("h2T_ready"), sem2("h2T_done")
        w_e_in, ws_in, w_r_in = sem("w_e_in"), sem("ws_in"), sem("w_r_in")
        logits_ready, gap_done, exp_done = sem("logits_ready"), sem("gap_done"), sem("exp_done")
        iota_done, route, counts_ready, masks_done = sem("iota_done"), sem("route"), sem("counts_ready"), sem("masks_done")
        hot_done, hot_used, tokens_ready, tokens_done = sem2("hot_done"), sem2("hot_used"), sem("tokens_ready"), sem("tokens_done")
        s_gu_ready, s_silu_done, s_hid_done, s_y_ready, s_y_done = (sem("s_gu_ready"), sem("s_silu_done"), sem("s_hid_done"),
                                                                    sem("s_y_ready"), sem("s_y_done"))
        idx_done = sem("idx_done")
        gathered = [sem(f"gathered{i}") for i in range(4)]
        xeT_ready, xeT_done = sem("xeT_ready"), sem("xeT_done")
        gu_ready, sg_done, hid_done = sem("gu_ready"), sem("sg_done"), sem("hid_done")
        hidT_ready, hidT_done, ye_ready, ye_done = sem("hidT_ready"), sem("hidT_done"), sem("ye_ready"), sem("ye_done")
        y_stored = [sem(f"y_stored{i}") for i in range(4)]
        cidx_done = sem("cidx_done")
        y_back = [sem(f"y_back{i}") for i in range(2 * TOPK)]
        sums, result_done = sem("sums"), [sem(f"result_done{i}") for i in range(2)]
        stored = [sem(f"stored{i}") for i in range(2)]

        def heads(ap):
            return ap.rearrange("p (h d) -> p h d", d=HD)

        def flat(t):
            return t[:, :, :].rearrange("p a t -> p (a t)")

        o_bank = [v_bank[:, :].rearrange("p (r t) -> p r t", t=P), score_bank[0]]
        o_rows_bank = [score_bank[1], score_bank[0]]
        kT_bank = [flat(score_bank[1]), v_bank[:, :]]
        oT_bank = [flat(score_bank[2])[:, 0:D], g_bank[:, D:2 * D]]
        y_bank = [flat(score_bank[2])[:, D:2 * D], g_bank[:, 0:D]]
        h2T_bank = flat(score_bank[3])

        def run_steps(eng, step):
            step(0, "a")
            step(1, "ab")
            with eng.Fori(2, NCH) as n:
                step(n, "abc")
            step(NCH, "bc")
            step(NCH + 1, "c")

        bank = [t[:, :, :].rearrange("p a t -> p (a t)") for t in score_bank] + [a_bank[0][:, :], v_bank[:, :], a_bank[1][:, :], g_bank[:, :]]
        w_gu_flat = w_gu[:, :, :, :].rearrange("p e k n -> p (e k n)")
        w_d_flat = w_d[:, :, :, :].rearrange("p e c n -> p (e c n)")
        ROUTE_BANK, COUNT_BANK = bank[4], bank[5]

        def settle_pool(i):
            nc.gpsimd.tensor_tensor(settle_to[0:1, i:i + 1], settle_from[0:1, 0:1], settle_from[0:1, 0:1], ALU.add)

        def settle_dve(i):
            nc.vector.memset(settle_to[0:1, i:i + 1], 0.0)

        def run_jobs(eng, step):
            for s in range(4):
                step(0, s, "xghy"[0:s + 1])
            with eng.Fori(1, NJ // 4) as i:
                for u in range(4):
                    step(i, u, "xghy")
            for s in range(3):
                step(NJ // 4, s, "xghy"[s + 1:])

        block = ctx.enter_context(nc.Block())

        @block.sync
        def _(sp):
            sp.dma_start(c_raw[:, :, :], c).then_inc(c_in, 16)
            sp.dma_start(ident[:, :], ident_in).then_inc(consts_in, 16)
            x_rows = x.rearrange("(t p) d -> p t d", p=P)
            for j in range(0, NT, 4):
                sp.dma_start(x_all[:, j:j + 4, :], x_rows[:, j:j + 4, :]).then_inc(x_in[j // 4], 16)
            sp.dma_start(rope_t[:, :, :, :], rope.rearrange("(j p) s d -> p j s d", p=P)).then_inc(consts_in, 16)
            sp.dma_start(decay_q_t[:, :, :], decay_q).then_inc(consts_in, 16)
            sp.dma_start(decay_k_t[:, :], decay_k).then_inc(consts_in, 16)
            sp.dma_start(decay_s_t[:, :, :], decay_s).then_inc(consts_in, 16)
            sp.dma_start(state_mask_t[:, :, :], state_mask).then_inc(consts_in, 16)
            sp.dma_start(norm_col[:, :], norm_w).then_inc(consts_in, 16)
            sp.dma_start(decay_t[:, :, :, :], decay).then_inc(consts_in, 16)

            sp.dma_start(w_gu[:, :, :, :], expert_gu.rearrange("e (k p) n -> p e k n", p=P)).then_inc(w_e_in, 16)
            sp.dma_start(w_r[:, :, :], router_w.rearrange("(k p) e -> p k e", p=P)).then_inc(w_r_in, 16)
            with sp.Fori(1, NCH + 1) as n:
                for b in range(B):
                    sp.wait_ge(h2_done[b], n)
                    sp.dma_start(h2_rows[bass.ds((n + (b * NCH - 1)) * P, P), :], h2[b][:, :]).then_inc(h2_stored[b], 16)
            for b in range(B):
                sp.wait_ge(h2_stored[b], 16 * NCH)
                sp.wait_ge(h2T_done[b], NCH)
            full = SI // P * P
            for k in range(KC):
                sp.dma_start(ws_gu[:, k, :, 0:SI], shared_gu[k * P:(k + 1) * P]).then_inc(ws_in, 16)
            sp.dma_start(ws_d[:, 0:SM - 1, :], shared_d[0:full, :].rearrange("(m p) n -> p m n", p=P)).then_inc(ws_in, 16)
            sp.wait_ge(iota_done, 2)
            sp.dma_start(ws_d[0:SI - full, SM - 1, :], shared_d[full:SI, :]).then_inc(ws_in, 16)
            sp.dma_start(w_d[:, :, :, :], expert_d.rearrange("e (c p) n -> p e c n", p=HC)).then_inc(w_e_in, 16)
            with sp.Fori(0, NJ // 4) as i:
                for u in range(4):
                    sp.wait_ge(ye_done, i * 4 + (u + 1))
                    sp.dma_start(y_rows[bass.ds((i * 4 + u) * P, P), :], ys[u][:, :]).then_inc(y_stored[u], 16)
            with sp.Fori(0, NT // 2) as i:
                for u in range(2):
                    sp.wait_ge(result_done[u], i + 1)
                    sp.dma_start(out[bass.ds((i * 2 + u) * P, P), :], result[u][:, :]).then_inc(stored[u], 16)
            for u in range(2):
                sp.wait_ge(stored[u], 16 * (NT // 2))

        @block.scalar
        def _(act):
            act.dma_start(w_mod, wmod.rearrange("(k p) n -> p k n", p=P)).then_inc(w_mod_in, 16)
            for w, off in ((Wq, 0), (Wk, D), (Wv, 2 * D), (Wg1, 3 * D)):
                act.dma_start(w_in[:, :, off:off + w.shape[1]], w.rearrange("(k p) n -> p k n", p=P)).then_inc(w_in_in, 16)
            act.dma_start(w_g2[:, :], Wg2).then_inc(w_in_in, 16)
            act.dma_start(w_o[:, :, :], Wo.rearrange("(k p) n -> p k n", p=P)).then_inc(w_in_in, 16)
            act.wait_ge(c_in, 16)
            act.activation(c_silu[:, :, :], c_raw[:, :, :], ACT.Silu).then_inc(c_silu_done, 1)

            def modulate(b, n, parts):
                act.wait_ge(xT_ready[b], n + 1)
                if "c" not in parts:
                    act.wait_ge(mod_cols_done, 3)
                for k in range(KC):
                    last = act.activation(hT[b][:, k, :], a_bank[b][:, k * P:(k + 1) * P], ACT.Identity,
                                          bias=mod_cols[:, 0, k, b:b + 1], scale=mod_cols[:, 1, k, b:b + 1])
                last.then_inc(hT_done[b], 1)

            def silu_qk(b, n):
                act.wait_ge(qk_ready[b], n + 1)
                act.activation(qk[b][:, :, :], heads(a_bank[b][:, :]), ACT.Silu).then_inc(qk_done[b], 1)

            def copy_vg(b, n):
                act.wait_ge(vg_ready[b], n + 1)
                act.copy(v[b][:, :], v_bank[:, 0:D])
                act.copy(g1T[b][:, :], v_bank[0:HD, D:D + P]).then_inc(vg_done[b], 1)

            def copy_qT(b, n):
                act.wait_ge(qkT_ready[b], n + 1)
                act.copy(qT[b][:, :, :], a_bank[b][:, :].rearrange("p (r t) -> p r t", t=P))

            def copy_kT(b, n):
                act.copy(kT[b][:, :, :], kT_bank[b].rearrange("p (r t) -> p r t", t=P)).then_inc(qkT_done[b], 1)

            def gate_tanh(b, n):
                act.wait_ge(gate_state_ready[b], n)
                act.activation(th[b][:, :], g_bank[:, 0:D], ACT.Tanh, scale=0.5).then_inc(th_done[b], 1)

            def copy_o(b, n):
                act.wait_ge(o_ready[b], n)
                act.copy(oP[b][:, :, :], o_bank[b][:, :, :]).then_inc(o_copied[b], 1)

            def square(b, n):
                act.wait_ge(o_g_done[b], n)
                act.activation(o_sq[b][:, :, :], o_g[b][:, :, :], ACT.Square).then_inc(o_sq_done[b], 1)

            def copy_oT(b, n):
                act.wait_ge(oT_ready[b], n)
                for k in range(KC):
                    last = act.activation(oT[b][:, k, :], oT_bank[b][:, k * P:(k + 1) * P], ACT.Copy, scale=norm_half[:, k:k + 1])
                last.then_inc(oT_done[b], 1)

            def step(n, parts):
                if "a" in parts:
                    modulate(0, n, parts)
                if "c" in parts:
                    copy_oT(1, n - 1)
                if "a" in parts:
                    modulate(1, n, parts)
                    silu_qk(0, n)
                if "b" in parts:
                    gate_tanh(0, n)
                if "a" in parts:
                    silu_qk(1, n)
                if "b" in parts:
                    copy_o(0, n)
                    gate_tanh(1, n)
                if "a" in parts:
                    copy_vg(0, n)
                if "b" in parts:
                    square(0, n)
                if "c" in parts:
                    act.wait_ge(h2T_ready, n - 1)
                    for b in range(B):
                        act.copy(h2T[:, :, bass.ds((n + (b * NCH - 2)) * P, P)],
                                 h2T_bank[:, b * D:(b + 1) * D].rearrange("p (k t) -> p k t", k=KC)).then_inc(h2T_done[b], 1)
                if "b" in parts:
                    copy_o(1, n)
                    square(1, n)
                if "a" in parts:
                    copy_vg(1, n)
                    copy_qT(0, n)
                if "b" in parts:
                    copy_oT(0, n)
                if "a" in parts:
                    copy_kT(0, n)
                    copy_qT(1, n)
                    copy_kT(1, n)

            run_steps(act, step)
            for b in range(B):
                act.wait_ge(h2_stored[b], 16 * NCH)
            act.wait_ge(gap_done, 1)
            act.activation(weight_e[:, :, :], gap[:, :, :], ACT.Exp)
            act.activation(shared_th[:, :], logits[:, :, E], ACT.Tanh, scale=0.5).then_inc(exp_done, 1)

            def shared_silu(first):
                with act.Fori(first, first + SHARED_STEPS // 2) as q:
                    for m in range(SM):
                        act.wait_ge(s_gu_ready, q * SM + (m + 1))
                        act.wait_ge(s_hid_done, q * SM + max(m - 1, 0))
                        act.activation(s_silu[m % 2][:, :], bank[2 * (m % 2)][:, :], ACT.Silu).then_inc(s_silu_done, 1)

            def job_step(i, u, parts):
                s = i * 4 + u
                if "x" in parts:
                    act.wait_ge(xeT_ready, s + 1)
                    at_least(act, gu_ready, s - 1)
                    act.copy(xeT[u % 2][:, :, :], bank[u % 2][:, 0:D].rearrange("p (k t) -> p k t", k=KC)).then_inc(xeT_done, 1)
                if "g" in parts:
                    act.wait_ge(gu_ready, s)
                    at_least(act, hid_done, s - 2)
                    act.activation(sg[(u + 1) % 2][:, :], bank[2 + (u + 1) % 2][:, 0:I_E], ACT.Silu).then_inc(sg_done, 1)
                if "y" in parts:
                    act.wait_ge(ye_ready, s - 2)
                    at_least(act, y_stored[(u + 1) % 4], (i + (u - 3) // 4) * 16)
                    act.copy(ys[(u + 1) % 4][:, :], bank[6 + (u + 1) % 2][:, 0:D]).then_inc(ye_done, 1)

            shared_silu(0)
            run_jobs(act, job_step)
            shared_silu(SHARED_STEPS // 2)

        @block.gpsimd
        def _(pool):
            pool.memset(half_neg[:, :], -0.5).then_inc(consts_set, 1)
            pool.memset(settle_from[:, :], 0.0).then_inc(consts_set, 1)
            for b in range(B):
                pool.memset(state[b][:, :, :], 0.0).then_inc(state_done[b], 1)
                pool.memset(rot[b][:, :, :, :], 0.0).then_inc(consts_set, 1)
                pool.memset(k_dec[b][:, :, :], 0.0).then_inc(consts_set, 1)
            pool.wait_ge(consts_set, 6)
            pool.wait_ge(ln1_steps, 2 * NT + 1)
            pool.tensor_tensor(rstd1[:, :], rstd1[:, :], half_neg[:, :], ALU.pow).then_inc(rstd1_done, 1)

            def rope_sin(b, n):
                half = HD // 2
                pool.wait_ge(qk_done[b], n + 1)
                settle_pool(4 + b)
                sin = rope_t[:, bass.ds(n, 1), 1, :]
                pool.tensor_tensor(rope_b[b][:, :, 0:half], qk[b][:, :, half:HD],
                                   sin[:, :, 0:half].to_broadcast([P, 2 * H, half]), ALU.mult)
                pool.tensor_tensor(rope_b[b][:, :, half:HD], qk[b][:, :, 0:half],
                                   sin[:, :, half:HD].to_broadcast([P, 2 * H, half]), ALU.mult).then_inc(rope_b_done[b], 1)

            def decay_keys(b, n):
                pool.wait_ge(rot_done[b], n + 1)
                at_least(pool, gate_state_ready[b], n)
                pool.tensor_tensor(k_dec[b][:, :, 0:HD], rot[b][:, 1, :, 0:HD],
                                   decay_k_t[:, :].unsqueeze(2).to_broadcast([P, H, HD]), ALU.mult).then_inc(k_dec_done[b], 1)

            def rms_norm(b, n):
                pool.wait_ge(ss_eps_done[b], n)
                pool.tensor_tensor(rms[b][:, :], ss_eps[b][:, :], half_neg[:, :], ALU.pow).then_inc(rms_done[b], 1)

            def second_norm(b, n):
                pool.wait_ge(var2_done[b], n)
                pool.tensor_tensor(rstd2[b][:, :], var2[b][:, :], half_neg[:, 0:1], ALU.pow).then_inc(rstd2_done[b], 1)
                pool.wait_ge(xn2_done[b], n)
                pool.tensor_tensor(h2_scaled[b][:, :], xn2[b][:, :], mod_rows[b][:, 2, :], ALU.mult).then_inc(h2_scaled_done[b], 1)
                pool.wait_ge(h2_scaled_done[b], n)
                pool.tensor_tensor(h2[b][:, :], h2_scaled[b][:, :], mod_rows[b][:, 1, :], ALU.add).then_inc(h2_done[b], 1)

            def step(n, parts):
                if "b" in parts:
                    for b in range(B):
                        pool.wait_ge(state_done[b], n)
                        pool.tensor_tensor(state_old[b][:, :, :], state[b][:, :, :], decay_s_t[:, :, :],
                                           ALU.mult).then_inc(state_old_done[b], 1)
                if "a" in parts:
                    rope_sin(0, n)
                if "c" in parts:
                    second_norm(1, n - 1)
                if "a" in parts:
                    decay_keys(0, n)
                    rope_sin(1, n)
                    decay_keys(1, n)
                if "b" in parts:
                    rms_norm(0, n)
                    rms_norm(1, n)
                if "c" in parts:
                    for b in range(B):
                        pool.wait_ge(h2_stored[b], (n - 1) * 16)
                    pool.wait_ge(h2T_ready, n - 1)
                if "b" in parts:
                    second_norm(0, n)

            run_steps(pool, step)

            for b in range(B):
                pool.wait_ge(h2_stored[b], 16 * NCH)
                pool.wait_ge(h2T_done[b], NCH)
            pool.memset(ws_gu[:, :, :, SI:SM * P], 0.0).then_inc(iota_done, 1)
            pool.memset(ws_d[:, SM - 1, :], 0.0).then_inc(iota_done, 1)
            pool.iota(iota_f[:, :], [[1, P]], base=0, channel_multiplier=0, allow_small_or_imprecise_dtypes=True).then_inc(iota_done, 1)
            pool.iota(token_id[:, :], [[P, NT]], base=0, channel_multiplier=1, allow_small_or_imprecise_dtypes=True).then_inc(iota_done, 1)
            pool.memset(ones[:, :], 1.0).then_inc(iota_done, 1)
            pool.memset(one_row[:, :], 1.0).then_inc(iota_done, 1)
            pool.memset(zero_r[:, :].bitcast(F32), 0.0).then_inc(iota_done, 1)

            def gather_job(i, u):
                pool.tensor_copy(idx[u][:, :], token_of[:, bass.ds(i * 4 + u, 1)]).then_inc(idx_done, 1)
                pool.wait_ge(idx_done, i * 4 + (u + 1))
                settle_pool(6 + u)
                pool.indirect_dma_start(xg[u][:, :], None, h2_rows, bass.IndirectOffsetOnAxis(ap=idx[u][:, 0:1], axis=0)).then_inc(gathered[u], 16)

            pool.wait_ge(tokens_done, 1)
            for u in range(4):
                gather_job(0, u)
            with pool.Fori(1, NJ // 4) as i:
                for u in range(4):
                    pool.wait_ge(gathered[u], i * 16)
                    pool.wait_ge(xeT_ready, i * 4 + (u - 3))
                    gather_job(i, u)
            for u in range(4):
                pool.wait_ge(y_stored[u], 16 * (NJ // 4))
            with pool.Fori(0, NT // 2) as i:
                for u in range(2):
                    pool.wait_ge(result_done[u], i)
                    for k in range(TOPK):
                        m = u * TOPK + k
                        pool.wait_ge(y_back[m], i * 16)
                        pool.tensor_copy(cidx[m][:, :], slot[:, bass.ds(i * 2 * TOPK + m, 1)]).then_inc(cidx_done, 1)
                        pool.wait_ge(cidx_done, i * 2 * TOPK + (m + 1))
                        settle_pool(10 + m)
                        pool.indirect_dma_start(yg[m][:, :], None, y_rows,
                                                bass.IndirectOffsetOnAxis(ap=cidx[m][:, 0:1], axis=0)).then_inc(y_back[m], 16)

        @block.vector
        def _(dve):
            dve.wait_ge(c_silu_done, 1)
            dve.tensor_copy(c_rows[:, :, :, :], c_silu[:, :, :].unsqueeze(3).to_broadcast([P, KC, B, P])).then_inc(c_rows_done, 1)
            for t in range(NT):
                if t % 4 == 0:
                    dve.wait_ge(x_in[t // 4], 16)
                dve.bn_stats(bn[:, t, :], x_all[:, t, :]).then_inc(ln1_steps, 1)
            dve.wait_ge(ln1_steps, NT)
            for t in range(NT):
                dve.bn_aggr(mean_var[:, t, :], bn[:, t, :]).then_inc(ln1_steps, 1)
            dve.wait_ge(ln1_steps, 2 * NT)
            dve.tensor_scalar(rstd1[:, :], mean_var[:, :, 1], LN_EPS, None, ALU.add).then_inc(ln1_steps, 1)
            dve.wait_ge(mod_cols_ready, 1)
            dve.tensor_copy(mod_cols[:, 0, :, :], a_bank[0][:, 0:KC * B].rearrange("p (k b) -> p k b", b=B)).then_inc(mod_cols_done, 1)
            dve.tensor_scalar(mod_cols[:, 1, :, :], a_bank[0][:, KC * B:2 * KC * B].rearrange("p (k b) -> p k b", b=B),
                              1.0, None, ALU.add).then_inc(mod_cols_done, 1)
            dve.wait_ge(consts_in, 16 * 8)
            dve.tensor_scalar(norm_half[:, :], norm_col[:, :], 0.5, None, ALU.mult).then_inc(mod_cols_done, 1)
            dve.wait_ge(rstd1_done, 1)
            dve.wait_ge(w_in_in, 16 * 6)
            steps = 0
            for b in range(B):
                dve.wait_ge(mod_rows_ready[b], 1)
                raw = [score_bank[2 * b + i // 2][:, 2 * (i % 2):2 * (i % 2) + 2, :].rearrange("p a t -> p (a t)") for i in range(4)]
                for i in (0, 3):
                    for op in (lambda: dve.tensor_scalar(gate_sgn[:, :], raw[i], 0.0, 2.0, ALU.is_ge, ALU.mult),
                               lambda: dve.scalar_tensor_tensor(gate_abs[:, :], gate_sgn[:, :], 1.0, raw[i], ALU.subtract, ALU.mult),
                               lambda: dve.tensor_scalar(gate_max[:, :], gate_abs[:, :], GATE_MIN, None, ALU.max),
                               lambda: dve.scalar_tensor_tensor(mod_rows[b][:, i, :], gate_sgn[:, :], 1.0, gate_max[:, :],
                                                                ALU.subtract, ALU.mult)):
                        op().then_inc(gate_steps, 1)
                        steps += 1
                        dve.wait_ge(gate_steps, steps)
                dve.tensor_copy(mod_rows[b][:, 1, :], raw[1])
                dve.tensor_scalar(mod_rows[b][:, 2, :], raw[2], 1.0, None, ALU.add)
                dve.tensor_tensor(w_og[b][:, :, :], w_o[:, :, :], mod_rows[b][:, 0, :].unsqueeze(1).to_broadcast([P, KC, D]),
                                  ALU.mult).then_inc(mod_rows_done, 1)

            def tile(b, n):
                return bass.ds(n + (b * NCH - 1), 1)

            def first_norm(n):
                for b in range(B):
                    at_least(dve, xT_ready[b], n)
                    t = bass.ds(n % NCH + b * NCH, 1)
                    dve.tensor_scalar(xn[b][:, :], x_all[:, t, :], mean_var[:, t, 0], rstd1[:, t],
                                      ALU.subtract, ALU.mult).then_inc(xn_done[b], 1)

            def rotate_cos(b, n):
                dve.wait_ge(qk_done[b], n + 1)
                dve.tensor_tensor(rope_a[b][:, :, :], qk[b][:, :, :],
                                  rope_t[:, bass.ds(n, 1), 0, :].to_broadcast([P, 2 * H, HD]), ALU.mult).then_inc(rope_a_done[b], 1)

            def rotate_sum(b, n):
                dve.wait_ge(rope_a_done[b], n + 1)
                dve.wait_ge(rope_b_done[b], n + 1)
                at_least(dve, k_dec_done[b], n)
                dve.tensor_tensor(rot[b][:, :, :, 0:HD], rope_a[b][:, :, :].rearrange("p (s h) d -> p s h d", s=2),
                                  rope_b[b][:, :, :].rearrange("p (s h) d -> p s h d", s=2), ALU.add).then_inc(rot_done[b], 1)

            def mask_scores(b, n):
                dve.wait_ge(scores_ready[b], n)
                for g in range(HG):
                    last = dve.tensor_tensor(probs[b][:, g], score_bank[g][:, :, :], decay_t[:, g, :, :], ALU.mult)
                last.then_inc(probs_done[b], 1)

            def mask_state(b, n):
                dve.wait_ge(th_done[b], n)
                dve.tensor_tensor(state_new[b][:, :, :], g_bank[:, D:2 * D].rearrange("p (r e) -> p r e", r=NR),
                                  state_mask_t[:, :, :], ALU.mult).then_inc(state_new_done[b], 1)

            def decay_queries(b, n):
                dve.wait_ge(qkT_done[b], n)
                dve.tensor_tensor(qdT[b][:, :, :], qT[b][:, :, :], decay_q_t[:, :, :], ALU.mult).then_inc(qd_done[b], 1)

            def update_state(b, n):
                dve.wait_ge(o_ready[b], n)
                dve.wait_ge(state_new_done[b], n)
                dve.wait_ge(state_old_done[b], n)
                dve.tensor_tensor(state[b][:, :, :], state_old[b][:, :, :], state_new[b][:, :, :], ALU.add).then_inc(state_done[b], 1)

            def gate_output(b, n):
                dve.wait_ge(o_rows_ready[b], n)
                dve.wait_ge(th_done[b], n)
                dve.scalar_tensor_tensor(o_g[b][:, :, :], heads(th[b][:, :]), 1.0,
                                         o_rows_bank[b][:, :, :].rearrange("p r (g d) -> p (r g) d", g=HG)[:, :, 0:HD],
                                         ALU.add, ALU.mult).then_inc(o_g_done[b], 1)

            def mean_square(b, n):
                dve.wait_ge(o_sq_done[b], n)
                dve.tensor_reduce(ss[b][:, :], o_sq[b][:, :, :], AX.X, ALU.add).then_inc(ss_done[b], 1)
                dve.wait_ge(ss_done[b], n)
                dve.tensor_scalar(ss_eps[b][:, :], ss[b][:, :], 1.0 / (4 * HD), RMS_EPS, ALU.mult, ALU.add).then_inc(ss_eps_done[b], 1)

            def normalize_output(b, n):
                dve.wait_ge(rms_done[b], n)
                dve.tensor_tensor(o_n[b][:, :, :], o_g[b][:, :, :], rms[b][:, :].unsqueeze(2).to_broadcast([P, H, HD]),
                                  ALU.mult).then_inc(o_n_done[b], 1)

            def add_residual(b, n):
                dve.wait_ge(y_ready[b], n)
                dve.tensor_tensor(x_all[:, tile(b, n), :], y_bank[b].unsqueeze(1), x_all[:, tile(b, n), :], ALU.add).then_inc(x2_done[b], 1)
                dve.wait_ge(x2_done[b], n)
                settle_dve(b)
                dve.bn_stats(bn2[b][:, :], x_all[:, tile(b, n), :]).then_inc(ln2_steps[b], 1)
                dve.wait_ge(ln2_steps[b], n * 2 - 1)
                settle_dve(2 + b)
                dve.bn_aggr(mv2[b][:, :], bn2[b][:, :]).then_inc(ln2_steps[b], 1)
                dve.wait_ge(ln2_steps[b], n * 2)
                dve.tensor_scalar(var2[b][:, :], mv2[b][:, 1:2], LN_EPS, None, ALU.add).then_inc(var2_done[b], 1)

            def normalize_x2(b, n):
                dve.wait_ge(rstd2_done[b], n)
                dve.tensor_scalar(xn2[b][:, :], x_all[:, tile(b, n), :], mv2[b][:, 0:1], rstd2[b][:, 0:1],
                                  ALU.subtract, ALU.mult).then_inc(xn2_done[b], 1)

            def step(n, parts):
                if "b" in parts:
                    decay_queries(0, n)
                if "c" in parts:
                    add_residual(1, n - 1)
                if "b" in parts:
                    mask_scores(0, n)
                if "a" in parts:
                    rotate_cos(0, n)
                if "b" in parts:
                    mask_state(0, n)
                if "a" in parts:
                    rotate_sum(0, n)
                if "b" in parts:
                    decay_queries(1, n)
                if "c" in parts:
                    normalize_x2(1, n - 1)
                if "b" in parts:
                    mask_scores(1, n)
                if "a" in parts:
                    rotate_cos(1, n)
                    rotate_sum(1, n)
                    first_norm(n + 1)
                if "b" in parts:
                    update_state(0, n)
                    mask_state(1, n)
                    gate_output(0, n)
                    mean_square(0, n)
                    update_state(1, n)
                    gate_output(1, n)
                    normalize_output(0, n)
                    mean_square(1, n)
                    add_residual(0, n)
                    normalize_output(1, n)
                    normalize_x2(0, n)

            first_norm(0)
            run_steps(dve, step)

            for b in range(B):
                dve.wait_ge(h2_stored[b], 16 * NCH)
            links = 0

            def link(instruction):
                nonlocal links
                links += 1
                instruction.then_inc(route, 1)
                dve.wait_ge(route, links)

            def per_choice(ap):
                return ap.unsqueeze(2).to_broadcast([P, NT, TOPK, E])

            dve.wait_ge(logits_ready, 1)
            link(dve.tensor_copy(logits[:, :, :], ROUTE_BANK.rearrange("p (t e) -> p t e", t=NT)[:, :, 0:E + 1]))
            for t in range(NT):
                last = dve.max(top8[:, t, :], logits[:, t, 0:E])
            link(last)
            dve.tensor_tensor(gap[:, :, :], top8[:, :, 0:TOPK], top8[:, :, 0:1].to_broadcast([P, NT, TOPK]), ALU.subtract).then_inc(gap_done, 1)
            for t in range(NT):
                last = dve.max_index(top8_i[:, t, :], top8[:, t, :], logits[:, t, 0:E])
            link(last)
            link(dve.tensor_copy(choice[:, :].rearrange("p (t k) -> p t k", k=TOPK), top8_i[:, :, 0:TOPK]))
            dve.wait_ge(iota_done, 7)
            dve.tensor_scalar(before[:, :], iota_f[:, :], token_id[:, 0:1], None, ALU.is_gt)
            link(dve.tensor_tensor(onehot[:, :, :], iota_f[:, 0:E].unsqueeze(1).to_broadcast([P, NQ, E]),
                                   choice[:, :].unsqueeze(2).to_broadcast([P, NQ, E]), ALU.is_equal))
            with nc.allow_low_precision(reason="counts up to 16 are exact in bfloat16"):
                link(dve.tensor_reduce(mask[:, :, :], onehot[:, :, :].rearrange("p (t k) e -> p t e k", k=TOPK), AX.X, ALU.add))
                dve.tensor_reduce(mask_sum[:, :], mask[:, :, :].rearrange("p t e -> p e t"), AX.X, ALU.add).then_inc(masks_done, 1)
            dve.wait_ge(exp_done, 1)
            link(dve.tensor_reduce(weight_sum[:, :], weight_e[:, :, :], AX.X, ALU.add))
            link(dve.reciprocal(weight_rec[:, :], weight_sum[:, :]))
            dve.tensor_scalar(shared_gate[:, :], shared_th[:, :], 0.5, 0.5, ALU.mult, ALU.add)
            link(dve.tensor_tensor(weight[:, :, :], weight_e[:, :, :], weight_rec[:, :].unsqueeze(2).to_broadcast([P, NT, TOPK]), ALU.mult))
            dve.wait_ge(counts_ready, 1)
            link(dve.tensor_scalar(count_i[:, :], COUNT_BANK[:, NT * E:NT * E + E], float(P - 1), None, ALU.add))
            link(dve.tensor_scalar(blocks_i[:, :], count_i[:, :], 7, None, ALU.logical_shift_right))
            link(dve.tensor_copy(blocks[:, :], blocks_i[:, :]))
            link(dve.tensor_tensor_scan(block_end[:, :], one_row[:, :], blocks[:, :], 0.0, ALU.mult, ALU.add))
            link(dve.tensor_tensor(block_start[:, :], block_end[:, :], blocks[:, :], ALU.subtract))
            link(dve.scalar_tensor_tensor(place[:, :, :], block_start[:, :].unsqueeze(1).to_broadcast([P, NT, E]), float(P),
                                          COUNT_BANK[:, 0:NT * E].rearrange("p (t e) -> p t e", e=E), ALU.mult, ALU.add))
            link(dve.tensor_tensor(placed[:, :, :].rearrange("p (t k) e -> p t k e", k=TOPK),
                                   onehot[:, :, :].rearrange("p (t k) e -> p t k e", k=TOPK), per_choice(place[:, :, :]), ALU.mult))
            link(dve.tensor_reduce(slot_f[:, :], placed[:, :, :], AX.X, ALU.add))
            link(dve.tensor_copy(slot[:, :], slot_f[:, :]))
            link(dve.tensor_scalar(slot_blk_i[:, :], slot[:, :], 7, None, ALU.logical_shift_right))
            link(dve.tensor_scalar(slot_row_i[:, :], slot[:, :], P - 1, None, ALU.bitwise_and))
            dve.tensor_copy(slot_blk[:, :], slot_blk_i[:, :])
            link(dve.tensor_copy(slot_row[:, :], slot_row_i[:, :]))
            link(dve.tensor_tensor(job_ge[:, :, :], block_end[0:1, :].unsqueeze(1).to_broadcast([1, NJ, E]),
                                   iota_f[0:1, 0:NJ].unsqueeze(2).to_broadcast([1, NJ, E]), ALU.is_le))
            link(dve.tensor_reduce(job_sum[:, :], job_ge[:, :, :], AX.X, ALU.add))
            link(dve.tensor_scalar(job_expert[:, :], job_sum[:, :], float(E - 1), None, ALU.min))
            with dve.Fori(0, NT // 2) as i:
                for u in range(2):
                    dve.wait_ge(hot_used[u], i)
                    for k in range(TOPK):
                        q = i * (2 * TOPK) + (u * TOPK + k)
                        dve.tensor_scalar(row_hot[:, u, k, :], iota_f[:, :], slot_row[:, bass.ds(q, 1)], None, ALU.is_equal)
                        last = dve.tensor_scalar(blk_hot[:, u, k, :], iota_f[:, 0:NJ], slot_blk[:, bass.ds(q, 1)],
                                                 token_id[:, bass.ds(i * 2 + u, 1)], ALU.is_equal, ALU.mult)
                    last.then_inc(hot_done[u], 1)
            dve.wait_ge(tokens_ready, 1)
            dve.tensor_copy(token_of[:, :], ROUTE_BANK[:, 0:NJ]).then_inc(tokens_done, 1)

            def shared(first):
                with dve.Fori(first, first + SHARED_STEPS // 2) as q:
                    dve.wait_ge(s_y_ready, q * SHARED_T)
                    for m in range(SM):
                        dve.wait_ge(s_silu_done, q * SM + (m + 1))
                        dve.tensor_tensor(s_hid[:, m, :], s_silu[m % 2][:, :], bank[2 * (m % 2) + 1][:, :],
                                          ALU.mult).then_inc(s_hid_done, 1)
                    for t in range(SHARED_T):
                        dve.wait_ge(s_y_ready, q * SHARED_T + (t + 1))
                        dve.tensor_scalar(acc[:, bass.ds(q * SHARED_T + t, 1), :], bank[6 + t % 2][:, 0:D].unsqueeze(1),
                                          shared_gate[:, bass.ds(q * SHARED_T + t, 1)], None, ALU.mult).then_inc(s_y_done, 1)

            def job_step(i, u, parts):
                s = i * 4 + u
                if "g" in parts:
                    dve.wait_ge(sg_done, s)
                    at_least(dve, hidT_ready, s - 2)
                    dve.tensor_tensor(hid[(u + 1) % 2][:, :], sg[(u + 1) % 2][:, :], bank[2 + (u + 1) % 2][:, I_E:2 * I_E],
                                      ALU.mult).then_inc(hid_done, 1)
                if "h" in parts:
                    dve.wait_ge(hidT_ready, s - 1)
                    at_least(dve, ye_ready, s - 3)
                    dve.tensor_copy(hidT[u % 2][:, :, :], bank[4 + u % 2][0:HC, 0:2 * P].rearrange("p (c t) -> p c t", c=2)).then_inc(hidT_done, 1)

            shared(0)
            run_jobs(dve, job_step)
            shared(SHARED_STEPS // 2)

            for b in range(B):
                with dve.Fori(b * NT // 4, (b + 1) * NT // 4) as i:
                    for u in range(2):
                        n0 = i * 2 * (TOPK + 1) + u * (TOPK + 1)
                        t = i * 2 + u
                        dve.wait_ge(result_done[u], i)
                        for k in range(TOPK):
                            dve.wait_ge(y_back[u * TOPK + k], i * 16 + 16)
                            if k:
                                dve.wait_ge(sums, n0 + k)
                            dve.scalar_tensor_tensor(total[u][:, :].unsqueeze(1), yg[u * TOPK + k][:, :].unsqueeze(1), weight[:, bass.ds(t, 1), k],
                                                     total[u][:, :].unsqueeze(1) if k else acc[:, bass.ds(t, 1), :],
                                                     ALU.mult, ALU.add).then_inc(sums, 1)
                        dve.wait_ge(sums, n0 + TOPK)
                        dve.tensor_tensor(total_g[u][:, :], total[u][:, :], mod_rows[b][:, 3, :], ALU.mult).then_inc(sums, 1)
                        dve.wait_ge(sums, n0 + TOPK + 1)
                        dve.wait_ge(stored[u], i * 16)
                        dve.tensor_tensor(result[u][:, :].unsqueeze(1), total_g[u][:, :].unsqueeze(1), x_all[:, bass.ds(t, 1), :],
                                          ALU.add).then_inc(result_done[u], 1)

        @block.tensor
        def _(pe):
            pe.wait_ge(w_mod_in, 16)
            pe.wait_ge(c_rows_done, 1)
            for i in range(2):
                for m in range(KC):
                    for k in range(KC):
                        last = pe.matmul(a_bank[0][:, (i * KC + m) * B:(i * KC + m + 1) * B],
                                         w_mod[:, k, i * D + m * P:i * D + (m + 1) * P], c_silu[:, k, :],
                                         start=(k == 0), stop=(k == KC - 1))
            last.then_inc(mod_cols_ready, 1)
            for b in range(B):
                for i in range(2):
                    for k in range(KC):
                        last = pe.matmul(score_bank[2 * b + i][:, :, :].rearrange("p a t -> p (a t)"), c_rows[:, k, b, :],
                                         w_mod[:, k, 2 * D + i * 512:2 * D + (i + 1) * 512], start=(k == 0), stop=(k == KC - 1))
                last.then_inc(mod_rows_ready[b], 1)
            pe.wait_ge(consts_in, 16 * 8)
            pe.wait_ge(w_in_in, 16 * 6)
            pe.wait_ge(mod_cols_done, 2)

            EW = HG * HD

            def scores(b, r):
                for g in range(HG):
                    q0 = PAD * g
                    last = pe.matmul(score_bank[g][:, r, :], kT[b][q0:q0 + HD, r, :], qT[b][q0:q0 + HD, r, :],
                                     start=True, stop=True)
                if r == NR - 1:
                    last.then_inc(scores_ready[b], 1)

            def attend(b, r):
                for g in range(HG):
                    pe.matmul(o_bank[b][PAD * g:PAD * g + HD, r, :], state[b][:, r, g * HD:(g + 1) * HD], qdT[b][:, r, :],
                              start=True, stop=False)
                for g in range(HG):
                    h = r * HG + g
                    last = pe.matmul(o_bank[b][PAD * g:PAD * g + HD, r, :], v[b][:, h * HD:(h + 1) * HD], probs[b][:, g, r, :],
                                     start=False, stop=True)
                if r == NR - 1:
                    last.then_inc(o_ready[b], 1)

            def output_rows(b, n):
                pe.wait_ge(o_copied[b], n)
                for r in range(NR):
                    last = pe.transpose(o_rows_bank[b][:, r, :], oP[b][:, r, :], ident[:, :])
                last.then_inc(o_rows_ready[b], 1)

            def gate_state(b, n):
                pe.wait_ge(k_dec_done[b], n)
                at_least(pe, state_new_done[1 - b], n - (1 - b))
                if b == 0:
                    at_least(pe, x2_done[1], n - 1)
                pe.matmul(g_bank[:, 0:D], g1T[b][:, :], w_g2[:, :], start=True, stop=True)
                for r in range(NR):
                    last = pe.matmul(g_bank[:, D + r * EW:D + (r + 1) * EW], k_dec[b][:, HG * r:HG * (r + 1), :].rearrange("p h d -> p (h d)"),
                                     v[b][:, r * EW:(r + 1) * EW], start=True, stop=True)
                last.then_inc(gate_state_ready[b], 1)

            def transpose_x(b, n):
                pe.wait_ge(xn_done[b], n + 1)
                at_least(pe, qkT_done[b], n)
                for k in range(KC):
                    last = pe.transpose(a_bank[b][:, k * P:(k + 1) * P], xn[b][:, k * P:(k + 1) * P], ident[:, :])
                last.then_inc(xT_ready[b], 1)

            def project_qk(b, k):
                last = pe.matmul(a_bank[b][:, :], hT[b][:, k, :], w_in[:, k, 0:2 * D], start=(k == 0), stop=(k == KC - 1))
                if k == KC - 1:
                    last.then_inc(qk_ready[b], 1)

            def project_v(b):
                for k in range(KC):
                    pe.matmul(v_bank[:, 0:D], hT[b][:, k, :], w_in[:, k, 2 * D:3 * D], start=(k == 0), stop=(k == KC - 1))

            def project_g1(b):
                for k in range(KC):
                    last = pe.matmul(v_bank[0:HD, D:D + P], w_in[:, k, 3 * D:3 * D + HD], hT[b][:, k, :],
                                     start=(k == 0), stop=(k == KC - 1))
                last.then_inc(vg_ready[b], 1)

            def transpose_q(b):
                for r in range(NR):
                    pe.transpose(a_bank[b][:, r * P:(r + 1) * P], rot[b][:, 0, HG * r:HG * (r + 1), :].rearrange("p h d -> p (h d)"), ident[:, :])

            def transpose_k(b):
                for r in range(NR):
                    last = pe.transpose(kT_bank[b][:, r * P:(r + 1) * P], rot[b][:, 1, HG * r:HG * (r + 1), :].rearrange("p h d -> p (h d)"), ident[:, :])
                last.then_inc(qkT_ready[b], 1)

            def transpose_o(b, n):
                pe.wait_ge(o_n_done[b], n)
                for k in range(KC):
                    last = pe.transpose(oT_bank[b][:, k * P:(k + 1) * P],
                                        o_n[b][:, :, :].rearrange("p h d -> p (h d)")[:, k * P:(k + 1) * P], ident[:, :])
                last.then_inc(oT_ready[b], 1)

            def project_y(b, n):
                pe.wait_ge(oT_done[b], n)
                for k in range(KC):
                    last = pe.matmul(y_bank[b], oT[b][:, k, :], w_og[b][:, k, :], start=(k == 0), stop=(k == KC - 1))
                last.then_inc(y_ready[b], 1)

            def step(n, parts):
                if "a" in parts:
                    transpose_x(0, n)
                if "b" in parts:
                    if "c" not in parts:
                        pe.wait_ge(mod_rows_done, 2)
                    pe.wait_ge(qkT_done[0], n)
                    at_least(pe, o_g_done[1], n - 1)
                    at_least(pe, x2_done[0], n - 1)
                    scores(0, 0)
                if "c" in parts:
                    pe.wait_ge(state_new_done[1], n - 1)
                    transpose_o(1, n - 1)
                if "a" in parts:
                    transpose_x(1, n)
                if "b" in parts:
                    scores(0, 1)
                if "a" in parts:
                    pe.wait_ge(hT_done[0], n + 1)
                    project_qk(0, 0)
                if "b" in parts:
                    scores(0, 2)
                if "c" in parts:
                    project_y(1, n - 1)
                if "b" in parts:
                    scores(0, 3)
                if "a" in parts:
                    project_qk(0, 1)
                if "b" in parts:
                    gate_state(0, n)
                if "a" in parts:
                    pe.wait_ge(hT_done[1], n + 1)
                    project_qk(1, 0)
                if "b" in parts:
                    pe.wait_ge(qkT_done[1], n)
                    pe.wait_ge(qd_done[0], n)
                    pe.wait_ge(state_done[0], n)
                    pe.wait_ge(probs_done[0], n)
                    scores(1, 0)
                    attend(0, 0)
                    scores(1, 1)
                    attend(0, 1)
                    scores(1, 2)
                    attend(0, 2)
                if "a" in parts:
                    project_qk(1, 1)
                if "b" in parts:
                    scores(1, 3)
                    attend(0, 3)
                    gate_state(1, n)
                if "a" in parts:
                    at_least(pe, o_copied[0], n)
                    project_v(0)
                    project_g1(0)
                if "b" in parts:
                    pe.wait_ge(probs_done[1], n)
                    output_rows(0, n)
                if "c" in parts:
                    for b in range(B):
                        pe.wait_ge(h2_done[b], n - 1)
                        for k in range(KC):
                            last = pe.transpose(h2T_bank[:, b * D + k * P:b * D + (k + 1) * P], h2[b][:, k * P:(k + 1) * P], ident[:, :])
                    last.then_inc(h2T_ready, 1)
                if "b" in parts:
                    pe.wait_ge(state_done[1], n)
                    pe.wait_ge(qd_done[1], n)
                    for r in range(NR):
                        attend(1, r)
                if "a" in parts:
                    pe.wait_ge(vg_done[0], n + 1)
                    project_v(1)
                    project_g1(1)
                if "b" in parts:
                    output_rows(1, n)
                if "a" in parts:
                    pe.wait_ge(rot_done[0], n + 1)
                    transpose_q(0)
                    at_least(pe, o_g_done[0], n)
                    transpose_k(0)
                if "b" in parts:
                    transpose_o(0, n)
                if "a" in parts:
                    pe.wait_ge(rot_done[1], n + 1)
                    transpose_q(1)
                if "b" in parts:
                    project_y(0, n)
                if "a" in parts:
                    pe.wait_ge(vg_done[1], n + 1)
                    transpose_k(1)
                if "c" in parts:
                    for b in range(B):
                        pe.wait_ge(h2T_done[b], n - 1)

            run_steps(pe, step)

            for b in range(B):
                pe.wait_ge(h2T_done[b], NCH)
            pe.wait_ge(w_r_in, 16)
            for t in range(NT):
                for k in range(KC):
                    last = pe.matmul(ROUTE_BANK[:, t * 2 * E:t * 2 * E + E + 1], h2T[:, k, t * P:(t + 1) * P], w_r[:, k, :],
                                     start=(k == 0), stop=(k == KC - 1))
            last.then_inc(logits_ready, 1)

            pe.wait_ge(masks_done, 1)
            pe.matmul(COUNT_BANK[:, 0:NT * E], before[:, :], mask[:, :, :].rearrange("p t e -> p (t e)"), start=True, stop=False)
            for d in range(1, NT):
                pe.matmul(COUNT_BANK[:, d * E:NT * E], ones[:, :], mask[:, 0:NT - d, :].rearrange("p t e -> p (t e)"),
                          start=False, stop=(d == NT - 1))
            pe.matmul(COUNT_BANK[:, NT * E:NT * E + E], ones[:, :], mask_sum[:, :], start=True, stop=True).then_inc(counts_ready, 1)

            pe.matmul(ROUTE_BANK[:, 0:NJ], zero_r[:, :], zero_r[:, 0:NJ], start=True, stop=False)
            with pe.Fori(0, NT // 2) as i:
                for u in range(2):
                    pe.wait_ge(hot_done[u], i + 1)
                    for k in range(TOPK):
                        last = pe.matmul(ROUTE_BANK[:, 0:NJ], row_hot[:, u, k, :], blk_hot[:, u, k, :], start=False, stop=False)
                    last.then_inc(hot_used[u], 1)
            pe.matmul(ROUTE_BANK[:, 0:NJ], zero_r[:, :], zero_r[:, 0:NJ], start=False, stop=True).then_inc(tokens_ready, 1)
            pe.wait_ge(ws_in, 16 * 4)
            pe.wait_ge(iota_done, 2)

            def shared(first):
                with pe.Fori(first, first + SHARED_STEPS // 2) as q:
                    for m in range(SM):
                        if m >= 2:
                            pe.wait_ge(s_hid_done, q * SM + (m - 1))
                        for g in range(2):
                            for k in range(KC):
                                last = pe.matmul(bank[2 * (m % 2) + g][:, :], ws_gu[:, k, g, m * P:(m + 1) * P],
                                                 h2T[:, k, bass.ds(q * 512, 512)], start=(k == 0), stop=(k == KC - 1))
                        last.then_inc(s_gu_ready, 1)
                    pe.wait_ge(s_hid_done, q * SM + SM)
                    for t in range(SHARED_T):
                        pe.wait_ge(s_y_done, q * SHARED_T + max(t - 1, 0))
                        for m in range(SM):
                            last = pe.matmul(bank[6 + t % 2][:, 0:D], s_hid[:, m, t * P:(t + 1) * P], ws_d[:, m, :],
                                             start=(m == 0), stop=(m == SM - 1))
                        last.then_inc(s_y_ready, 1)

            def expert_of(job):
                return pe.value_load(job_expert[0:1, bass.ds(job, 1)], min_val=0, max_val=E - 1)

            def job_step(i, u, parts):
                s = i * 4 + u
                if "x" in parts:
                    pe.wait_ge(gathered[u], i * 16 + 16)
                    at_least(pe, xeT_done, s - 1)
                    for k in range(KC):
                        last = pe.transpose(bank[u % 2][:, k * P:(k + 1) * P], xg[u][:, k * P:(k + 1) * P], ident[:, :])
                    last.then_inc(xeT_ready, 1)
                if "g" in parts:
                    e = expert_of(s - 1)
                    pe.wait_ge(xeT_done, s)
                    at_least(pe, hid_done, s - 2)
                    for k in range(KC):
                        last = pe.matmul(bank[2 + (u + 1) % 2][:, 0:2 * I_E], xeT[(u + 1) % 2][:, k, :],
                                         w_gu_flat[:, bass.ds(e * (KC * 2 * I_E) + k * 2 * I_E, 2 * I_E)], start=(k == 0), stop=(k == KC - 1))
                    last.then_inc(gu_ready, 1)
                if "h" in parts:
                    pe.wait_ge(hid_done, s - 1)
                    at_least(pe, hidT_done, s - 3)
                    for h in range(2):
                        last = pe.transpose(bank[4 + u % 2][0:HC, h * P:(h + 1) * P], hid[u % 2][:, h * HC:(h + 1) * HC], ident[:, :])
                    last.then_inc(hidT_ready, 1)
                if "y" in parts:
                    e = expert_of(s - 3)
                    pe.wait_ge(hidT_done, s - 2)
                    at_least(pe, ye_done, s - 4)
                    for h in range(2):
                        last = pe.matmul(bank[6 + (u + 1) % 2][:, 0:D], hidT[(u + 1) % 2][:, h, :],
                                         w_d_flat[:, bass.ds(e * (2 * D) + h * D, D)], start=(h == 0), stop=(h == 1))
                    last.then_inc(ye_ready, 1)

            shared(0)
            pe.wait_ge(s_y_done, NT // 2)
            pe.wait_ge(w_e_in, 32)
            run_jobs(pe, job_step)
            for done in (xeT_done, hid_done, ye_done):
                pe.wait_ge(done, NJ)
            shared(SHARED_STEPS // 2)


def constants():
    f = np.float32
    slope = (2.0 ** (-8.0 * (np.arange(H, dtype=f) + 1.0) / H)).astype(f)
    log_lam = -slope
    theta = (f(10000.0) ** (-2.0 * np.arange(HD // 2, dtype=f) / HD)).astype(f)
    ang = np.arange(N, dtype=f)[:, None] * theta[None, :]
    cos, sin = np.cos(ang).astype(f), np.sin(ang).astype(f)
    rope = np.stack([np.concatenate([cos, cos], 1), np.concatenate([-sin, sin], 1)], 1)
    i = np.arange(P, dtype=f)
    diff = i[None, :] - i[:, None]
    dec = np.where(diff[:, None, :] >= 0, np.exp(log_lam[None, :, None] * np.maximum(diff, 0)[:, None, :]), 0).astype(f)
    decay = dec.reshape(P, NR, HG, P).transpose(0, 2, 1, 3)
    dq = np.exp(log_lam[:, None] * (i[None, :] + 1)).astype(f)
    dqT = np.repeat(dq.reshape(NR, HG, P).transpose(1, 0, 2), PAD, axis=0)
    dk = np.exp(log_lam[None] * (P - 1 - i[:, None])).astype(f)
    mask = np.zeros((P, NR, HG, HD), f)
    for g in range(HG):
        mask[PAD * g:PAD * g + HD, :, g, :] = 1
    lam_c = np.exp(log_lam * P).astype(f).reshape(1, NR, HG, 1)
    return {
        "rope": rope.astype(f), "decay": np.ascontiguousarray(decay), "decay_q": dqT, "decay_k": dk,
        "decay_s": (mask * lam_c).reshape(P, NR, HG * HD), "state_mask": mask.reshape(P, NR, HG * HD), "ident": np.eye(P, dtype=f),
    }


def kernel(**inputs):
    import concourse.bacc as bacc
    from concourse.bass_utils import run_bass_kernel_spmd

    a = {k: np.asarray(v) for k, v in inputs.items()}
    shared_gu = a["L0_ffn_shared_gate_up"].reshape(2, SI, D).transpose(2, 0, 1)
    arrays = {
        "x": a["L0_attn_x"].reshape(B * N, D),
        "Wq": a["L0_attn_Wq"], "Wk": a["L0_attn_Wk"], "Wv": a["L0_attn_Wv"], "Wo": a["L0_attn_Wo"],
        "Wg1": a["L0_attn_Wg1"], "Wg2": a["L0_attn_Wg2"],
        "norm_w": a["L0_attn_norm_weight"].reshape(KC, P).T,
        "c": a["L0_c"].reshape(B, KC, P).transpose(2, 1, 0),
        "wmod": a["L0_wmod"],
        "router_w": np.concatenate([a["L0_ffn_gate_w"], a["L0_ffn_shared_gate_vec"]], 0).T,
        "expert_gu": a["L0_ffn_expert_gate_up"].transpose(0, 2, 1),
        "expert_d": a["L0_ffn_expert_down"].transpose(0, 2, 1),
        "shared_gu": shared_gu,
        "shared_d": a["L0_ffn_shared_down"].T,
    }
    arrays.update(constants())
    arrays = {f"in_{k}": np.ascontiguousarray(v) for k, v in arrays.items()}
    nc = bacc.Bacc("TRN2", target_bir_lowering=False, num_devices=1)
    args = [nc.dram_tensor(k, v.shape, mybir.dt.from_np(v.dtype), kind="ExternalInput").ap() for k, v in arrays.items()]
    out = nc.dram_tensor("out_rows", [B * N, D], F32, kind="ExternalOutput").ap()
    build(nc, *args, out)
    r = run_bass_kernel_spmd(nc, [arrays], core_ids=[0])
    return r.results[0]["out_rows"].reshape(B, N, D)
```

```python
from contextlib import ExitStack

import numpy as np

import concourse.bass as bass
from concourse import mybir

F32 = mybir.dt.float32
I32 = mybir.dt.int32
U32 = mybir.dt.uint32
BF16 = mybir.dt.bfloat16
F32R = mybir.dt.float32r
ALU = mybir.AluOpType
ACT = mybir.ActivationFunctionType
AX = mybir.AxisListType

P = 128
B, N, D = 2, 1024, 256
H, HD = 16, 16
KC = D // P
NCH = N // P
NT = B * NCH
HG = 4
NR = H // HG
PAD = P // HG
LN_EPS = 1e-5
RMS_EPS = 1e-6
GATE_MIN = 0.25
E, TOPK = 16, 4
I_E = 176
HC = I_E // 2
SI = 704
SM = -(-SI // P)
NQ = NT * TOPK
NJ = NT * TOPK + E - 1
SHARED_T = 4
SHARED_STEPS = NT // SHARED_T
EARLY = SHARED_STEPS // 2
RW = 32
VB = 6
HOT = 4


def at_least(eng, semaphore, value):
    if not (isinstance(value, int) and value <= 0):
        eng.wait_ge(semaphore, value)


def build(nc, x, Wq, Wk, Wv, Wo, Wg1, Wg2, norm_w, c, wmod, router_w, expert_gu, expert_d, shared_gu, shared_d,
          rope, decay, decay_q, decay_k, decay_s, state_mask, ident_in, out):
    h2_rows = nc.dram_tensor("h2_rows", [NT * P, D], F32, kind="Internal").ap()
    y_rows = nc.dram_tensor("y_rows", [(NQ + NJ) * P, D], F32, kind="Internal").ap()
    with ExitStack() as ctx, ExitStack() as attention, ExitStack() as routing:
        def sb(name, shape, dt=F32):
            return ctx.enter_context(nc.sbuf_tensor(name, shape, dt))

        def sem(name):
            return ctx.enter_context(nc.semaphore(name))

        def sem2(name):
            return [sem(f"{name}{b}") for b in range(B)]

        def sb2(name, shape, dt=F32):
            return [sb(f"{name}{b}", shape, dt) for b in range(B)]

        ident = sb("ident", [P, P])
        settle_from, settle_to = sb("settle_from", [1, 1]), sb("settle_to", [1, 32])
        x_all = sb("x_all", [P, NT, D])
        mod_rows = sb2("mod_rows", [P, 4, D])
        w_gu = sb("w_gu", [P, E, KC, 2 * I_E])
        w_r = sb("w_r", [P, KC, RW])
        h2T = sb("h2T", [P, KC, NT * P])

        def at(name, shape, dt=F32):
            return attention.enter_context(nc.sbuf_tensor(name, shape, dt))

        def at2(name, shape, dt=F32):
            return [at(f"{name}{b}", shape, dt) for b in range(B)]

        score_bank = [ctx.enter_context(nc.psum_tensor(f"score_bank{g}", [P, HG, P], F32)) for g in range(HG)]
        a_bank = [ctx.enter_context(nc.psum_tensor(f"a_bank{b}", [P, 512], F32)) for b in range(B)]
        v_bank = ctx.enter_context(nc.psum_tensor("v_bank", [P, 512], F32))
        g_bank = ctx.enter_context(nc.psum_tensor("g_bank", [P, 512], F32))

        qk = at2("qk", [P, 2 * H, HD])
        rope_a = at2("rope_a", [P, 2 * H, HD])
        rope_b = at2("rope_b", [P, 2 * H, HD])
        rot = at2("rot", [P, 2, H, PAD])

        w_in = at("w_in", [P, KC, 3 * D + HD])
        w_g2 = at("w_g2", [HD, D])
        w_o = at("w_o", [P, KC, D])
        w_og = at2("w_og", [P, KC, D])
        norm_half = at("norm_half", [P, KC])
        norm_col = at("norm_col", [P, KC])
        c_raw = at("c_raw", [P, KC, B])
        c_silu = at("c_silu", [P, KC, B])
        c_rows = at("c_rows", [P, KC, B, P])
        mod_cols = at("mod_cols", [P, 2, KC, B])
        gate_abs = at2("gate_abs", [P, D])
        gate_sgn = at2("gate_sgn", [P, D])
        gate_max = at2("gate_max", [P, D])
        rope_t = at("rope_t", [P, NCH, 2, HD])
        decay_t = at("decay_t", [P, HG, NR, P])
        decay_q_t = at("decay_q_t", [P, NR, P])
        decay_k_t = at("decay_k_t", [P, H])
        decay_s_t = at("decay_s_t", [P, NR, HG * HD])
        state_mask_t = at("state_mask_t", [P, NR, HG * HD])
        half_neg = at("half_neg", [P, H])
        bn = at("bn", [P, NT, 6])
        mean_var = at("mean_var", [P, NT, 2])
        rstd1 = at("rstd1", [P, NT])

        xn = at2("xn", [P, D])
        hT = at2("hT", [P, KC, P])
        v = at2("v", [P, D])
        g1T = at2("g1T", [HD, P])
        k_dec = at2("k_dec", [P, H, PAD])
        qT = at2("qT", [P, NR, P])
        kT = at2("kT", [P, NR, P])
        probs_all = at("probs_all", [P, B, HG, NR, P])
        probs = [probs_all[:, b] for b in range(B)]
        w_mod = probs_all[:, :, :, :, :].rearrange("p b g r t -> p (b g r t)")[:, 0:KC * 6 * D].rearrange("p (k n) -> p k n", k=KC)
        state = at2("state", [P, NR, HG * HD])
        state_old = at2("state_old", [P, NR, HG * HD])
        state_new = at2("state_new", [P, NR, HG * HD])
        th = at2("th", [P, D])
        qdT = at2("qdT", [P, NR, P])
        oP = at2("oP", [P, NR, P])
        o_g = at2("o_g", [P, H, HD])
        o_sq = at2("o_sq", [P, H, HD])
        ss = at2("ss", [P, H])
        ss_eps = at2("ss_eps", [P, H])
        rms = at2("rms", [P, H])
        o_n = at2("o_n", [P, H, HD])
        oT = at2("oT", [P, KC, P])

        bn2 = at2("bn2", [P, 6])
        mv2 = at2("mv2", [P, 2])
        var2 = at2("var2", [P, 1])
        rstd2 = at2("rstd2", [P, 1])
        xn2 = at2("xn2", [P, D])
        h2_scaled = at2("h2_scaled", [P, D])
        h2 = at2("h2", [P, D])

        attention.close()
        ws_gu = sb("ws_gu", [P, KC, 2, SM * P])
        ws_d = sb("ws_d", [P, SM, D])
        w_d = sb("w_d", [HC, E, 2, D])
        weight = sb("weight", [P, NT, TOPK])
        shared_gate = sb("shared_gate", [P, NT])
        iota_f = sb("iota_f", [P, P])
        token_id = sb("token_id", [P, NT])
        slot = sb("slot", [P, NQ], I32)
        job_expert = sb("job_expert", [1, NJ], I32)
        token_of = sb("token_of", [P, NJ], I32)
        choice_of = sb("choice_of", [P, NJ], I32)
        s_silu = [sb(f"s_silu{i}", [P, 512]) for i in range(2)]
        s_up = [sb(f"s_up{i}", [P, 512]) for i in range(2)]
        s_hid = sb("s_hid", [P, SM, 512])
        acc = sb("acc", [P, EARLY * SHARED_T, D])
        def rt(name, shape, dt=F32):
            return routing.enter_context(nc.sbuf_tensor(name, shape, dt))

        logits = rt("logits", [P, NT, E + 1])
        top8 = rt("top8", [P, NT, 8])
        top8_i = rt("top8_i", [P, NT, 8], U32)
        choice = rt("choice", [P, NQ])
        gap = rt("gap", [P, NT, TOPK])
        weight_e = rt("weight_e", [P, NT, TOPK])
        weight_sum = rt("weight_sum", [P, NT])
        weight_rec = rt("weight_rec", [P, NT])
        shared_th = rt("shared_th", [P, NT])
        before = rt("before", [P, P], BF16)
        ones = rt("ones", [P, P], BF16)
        onehot = rt("onehot", [P, NQ, E])
        mask = rt("mask", [P, NT, E], BF16)
        mask_sum = rt("mask_sum", [P, E], BF16)
        count_i = rt("count_i", [P, E], I32)
        blocks_i = rt("blocks_i", [P, E], I32)
        blocks = rt("blocks", [P, E])
        one_row = rt("one_row", [P, E])
        block_end = rt("block_end", [P, E])
        block_start = rt("block_start", [P, E])
        place = rt("place", [P, NT, E])
        placed = rt("placed", [P, NQ, E])
        slot_f = rt("slot_f", [P, NQ])
        slot_blk_i = rt("slot_blk_i", [P, NQ], I32)
        slot_row_i = rt("slot_row_i", [P, NQ], I32)
        slot_blk = rt("slot_blk", [P, NQ])
        slot_row = rt("slot_row", [P, NQ])
        job_ge = rt("job_ge", [1, NJ, E])
        job_sum = rt("job_sum", [1, NJ])
        logitsT = rt("logitsT", [P, NT // HG, P])
        number_i = rt("number_i", [P, NQ], I32)
        number_hi_i = rt("number_hi_i", [P, NQ], I32)
        number_lo_i = rt("number_lo_i", [P, NQ], I32)
        number = rt("number", [P, NQ, 2])
        row_hot = rt("row_hot", [P, HOT, TOPK, P], BF16)
        blk_hot = rt("blk_hot", [P, HOT, TOPK, 2, NJ], BF16)
        zero_b = rt("zero_b", [P, 2 * NJ], BF16)
        empty_row = rt("empty_row", [P, NJ])
        slot_high = rt("slot_high", [P, NJ])
        slot_num = rt("slot_num", [P, NJ])
        slot_empty = rt("slot_empty", [P, NJ])
        slot_tok = rt("slot_tok", [P, NJ])
        slot_tok_i = rt("slot_tok_i", [P, NJ], I32)
        slot_dst = rt("slot_dst", [P, NJ])
        routing.close()
        idx = [sb(f"idx{i}", [P, 1], I32) for i in range(4)]
        xg = [sb(f"xg{i}", [P, D]) for i in range(4)]
        xeT = [sb(f"xeT{i}", [P, KC, P]) for i in range(2)]
        sg = [sb(f"sg{i}", [P, I_E]) for i in range(2)]
        hid = [sb(f"hid{i}", [P, I_E]) for i in range(2)]
        hidT = [sb(f"hidT{i}", [HC, 2, P]) for i in range(2)]
        ys = [sb(f"ys{i}", [P, D]) for i in range(4)]
        sidx = [sb(f"sidx{i}", [P, 1], I32) for i in range(4)]
        y4 = [sb(f"y4_{i}", [P, TOPK, D]) for i in range(4)]
        pre = [sb(f"pre{i}", [P, D]) for i in range(SHARED_T)]
        total = sb("total", [P, D])
        total_g = sb("total_g", [P, D])
        result = [sb(f"result{i}", [P, D]) for i in range(2)]

        x_in = [sem(f"x_in{i}") for i in range(3)]
        consts_in, decay_in, w_mod_in, c_in, w_qk_in, w_in_in = sem("consts_in"), sem("decay_in"), sem("w_mod_in"), sem("c_in"), sem("w_qk_in"), sem("w_in_in")
        c_silu_done, c_rows_done = sem("c_silu_done"), sem("c_rows_done")
        mod_cols_ready, mod_cols_done = sem("mod_cols_ready"), sem("mod_cols_done")
        mod_rows_ready, mod_rows_done = sem2("mod_rows_ready"), sem("mod_rows_done")
        gate_steps, mod_copied = sem("gate_steps"), sem("mod_copied")
        gb_steps = sem("gb_steps")
        consts_set = sem("consts_set")
        ln1_steps, rstd1_done = sem("ln1_steps"), sem("rstd1_done")

        xn_done, xT_ready, hT_done = sem2("xn_done"), sem2("xT_ready"), sem2("hT_done")
        qk_ready, vg_ready, qk_done, vg_done = sem2("qk_ready"), sem2("vg_ready"), sem2("qk_done"), sem2("vg_done")
        rope_a_done, rope_b_done, rot_done = sem2("rope_a_done"), sem2("rope_b_done"), sem2("rot_done")
        k_dec_done, qkT_ready, qkT_done = sem2("k_dec_done"), sem2("qkT_ready"), sem2("qkT_done")
        scores_ready, probs_done = sem2("scores_ready"), sem2("probs_done")
        gate_state_ready, th_done = sem2("gate_state_ready"), sem2("th_done")
        state_old_done, state_new_done, state_done = sem2("state_old_done"), sem2("state_new_done"), sem2("state_done")
        o_ready, o_copied, o_rows_ready, o_g_done = sem2("o_ready"), sem2("o_copied"), sem2("o_rows_ready"), sem2("o_g_done")
        qd_done = sem2("qd_done")
        o_sq_done, ss_done, ss_eps_done, rms_done, o_n_done = (sem2("o_sq_done"), sem2("ss_done"), sem2("ss_eps_done"),
                                                               sem2("rms_done"), sem2("o_n_done"))
        oT_ready, oT_done, y_ready, x2_done = sem2("oT_ready"), sem2("oT_done"), sem2("y_ready"), sem2("x2_done")
        ln2_steps, var2_done, rstd2_done, xn2_done = sem2("ln2_steps"), sem2("var2_done"), sem2("rstd2_done"), sem2("xn2_done")
        h2_scaled_done, h2_done, h2_stored = sem2("h2_scaled_done"), sem2("h2_done"), sem2("h2_stored")
        h2T_ready, h2T_done = sem("h2T_ready"), sem2("h2T_done")
        w_e_in, ws_in, w_r_in = sem("w_e_in"), sem("ws_in"), sem("w_r_in")
        logits_ready, gap_done, exp_done = sem("logits_ready"), sem("gap_done"), sem("exp_done")
        iota_done, route, counts_ready, masks_done = sem("iota_done"), sem("route"), sem("counts_ready"), sem("masks_done")
        hot_done, hot_used, tokens_ready, tokens_done = sem("hot_done"), sem("hot_used"), sem("tokens_ready"), sem("tokens_done")
        logitsT_ready, logitsT_done, gates_done = sem("logitsT_ready"), sem("logitsT_done"), sem("gates_done")
        s_gu_ready, s_silu_done, s_hid_done, s_y_ready, s_y_done = (sem("s_gu_ready"), sem("s_silu_done"), sem("s_hid_done"),
                                                                    sem("s_y_ready"), sem("s_y_done"))
        idx_done = sem("idx_done")
        gathered = [sem(f"gathered{i}") for i in range(4)]
        xeT_ready, xeT_done = sem("xeT_ready"), sem("xeT_done")
        gu_ready, sg_done, hid_done = sem("gu_ready"), sem("sg_done"), sem("hid_done")
        hidT_ready, hidT_done, ye_ready, ye_done = sem("hidT_ready"), sem("hidT_done"), sem("ye_ready"), sem("ye_done")
        y_stored = [sem(f"y_stored{i}") for i in range(4)]
        sidx_done = sem("sidx_done")
        y_back = [sem(f"y_back{i}") for i in range(4)]
        sums, result_done = sem("sums"), sem("result_done")
        stored = [sem(f"stored{i}") for i in range(2)]

        def heads(ap):
            return ap.rearrange("p (h d) -> p h d", d=HD)

        def flat(t):
            return t[:, :, :].rearrange("p a t -> p (a t)")

        o_bank = [v_bank[:, :].rearrange("p (r t) -> p r t", t=P), score_bank[0]]
        o_rows_bank = [a_bank[0][:, :].rearrange("p (r t) -> p r t", t=P), score_bank[0]]
        kT_bank = [flat(score_bank[1]), v_bank[:, :]]
        oT_bank = [flat(score_bank[2])[:, 0:D], g_bank[:, D:2 * D]]
        y_bank = [flat(score_bank[2])[:, D:2 * D], g_bank[:, 0:D]]
        h2T_bank = flat(score_bank[3])

        def run_steps(eng, step):
            step(0, "a")
            step(1, "ab")
            with eng.Fori(2, NCH) as n:
                step(n, "abc")
            step(NCH, "bc")
            step(NCH + 1, "c")

        bank = [t[:, :, :].rearrange("p a t -> p (a t)") for t in score_bank] + [a_bank[0][:, :], v_bank[:, :], a_bank[1][:, :], g_bank[:, :]]
        w_gu_flat = w_gu[:, :, :, :].rearrange("p e k n -> p (e k n)")
        w_d_flat = w_d[:, :, :, :].rearrange("p e c n -> p (e c n)")
        ROUTE_BANK, COUNT_BANK, LOGITS_BANK = bank[4], bank[5], bank[5]

        def down_bank(q, t):
            return bank[6 + t % 2 if q < EARLY or t < 2 else 4 + t % 2][:, 0:D]

        def settle_pool(i):
            nc.gpsimd.tensor_tensor(settle_to[0:1, i:i + 1], settle_from[0:1, 0:1], settle_from[0:1, 0:1], ALU.add)

        def settle_dve(i):
            nc.vector.memset(settle_to[0:1, i:i + 1], 0.0)

        x_parts = (0, 1, NCH // 2, NCH)

        late = range(EARLY, SHARED_STEPS)
        combined = [t for q in late for m in range(SHARED_T) for t in (q * SHARED_T + m, (q - EARLY) * SHARED_T + m)]
        loads = {(EARLY, 1): (0, 1), (EARLY, 3): (2,), (EARLY, 4): (3,), (EARLY, 5): (4, 5), (EARLY + 1, 1): (6,), (EARLY + 1, 2): (7,)}
        order = {q: "e" * SHARED_T + "o" * SHARED_T for q in late}

        def finished_count(q, kind, i):
            return (q - EARLY) * 2 * SHARED_T + [j for j, k in enumerate(order[q]) if k == kind][i] + 1

        finished = [(q - EARLY if k == "e" else q) * SHARED_T + order[q][:j].count(k) for q in late for j, k in enumerate(order[q])]

        def gate(eng, b, row, i, steps):
            g, n = mod_rows[b][:, row, :], 5 * b
            eng.tensor_scalar(gate_sgn[i][:, :], g, 0.0, 2.0, ALU.is_ge, ALU.mult).then_inc(steps, 1)
            eng.wait_ge(steps, n + 1)
            eng.tensor_scalar(gate_sgn[i][:, :], gate_sgn[i][:, :], 1.0, None, ALU.subtract).then_inc(steps, 1)
            eng.wait_ge(steps, n + 2)
            eng.tensor_tensor(gate_abs[i][:, :], gate_sgn[i][:, :], g, ALU.mult).then_inc(steps, 1)
            eng.wait_ge(steps, n + 3)
            eng.tensor_scalar(gate_max[i][:, :], gate_abs[i][:, :], GATE_MIN, None, ALU.max).then_inc(steps, 1)
            eng.wait_ge(steps, n + 4)
            eng.tensor_tensor(g, gate_sgn[i][:, :], gate_max[i][:, :], ALU.mult).then_inc(steps, 1)
            eng.wait_ge(steps, n + 5)

        def run_jobs(eng, step):
            for s in range(4):
                step(0, s, "xghy"[0:s + 1])
            for u in range(4):
                step(1, u, "xghy")
            with eng.Fori(2, NJ // 4) as i:
                for u in range(4):
                    step(i, u, "xghy")
            for s in range(NJ // 4 * 4, NJ + 3):
                step(s // 4, s % 4, "xghy"[max(0, s - NJ + 1):])

        block = ctx.enter_context(nc.Block())

        @block.sync
        def _(sp):
            sp.dma_start(c_raw[:, :, :], c).then_inc(c_in, 16)
            x_rows = x.rearrange("(b j p) d -> p b j d", b=B, p=P)
            for i in range(3):
                for b in range(B):
                    sp.dma_start(x_all[:, b * NCH + x_parts[i]:b * NCH + x_parts[i + 1], :],
                                 x_rows[:, b, x_parts[i]:x_parts[i + 1], :]).then_inc(x_in[i], 16)
                if i == 0:
                    sp.dma_start(ident[:, :], ident_in).then_inc(x_in[0], 16)
            sp.dma_start(rope_t[:, :, :, :], rope.rearrange("(j p) s d -> p j s d", p=P)).then_inc(consts_in, 16)
            sp.dma_start(decay_q_t[:, :, :], decay_q).then_inc(consts_in, 16)
            sp.dma_start(decay_k_t[:, :], decay_k).then_inc(consts_in, 16)
            sp.dma_start(decay_s_t[:, :, :], decay_s).then_inc(consts_in, 16)
            sp.dma_start(state_mask_t[:, :, :], state_mask).then_inc(consts_in, 16)
            sp.dma_start(norm_col[:, :], norm_w).then_inc(consts_in, 16)
            sp.dma_start(decay_t[:, :, :, :], decay).then_inc(decay_in, 16)

            sp.dma_start(w_gu[:, :, :, :], expert_gu.rearrange("e (k p) n -> p e k n", p=P)).then_inc(w_e_in, 16)
            sp.dma_start(w_r[:, :, :], router_w.rearrange("(k p) e -> p k e", p=P)).then_inc(w_r_in, 16)

            def store_h2(n):
                for b in range(B):
                    sp.wait_ge(h2_done[b], n)
                    sp.dma_start(h2_rows[bass.ds((n + (b * NCH - 1)) * P, P), :], h2[b][:, :]).then_inc(h2_stored[b], 16)

            with sp.Fori(1, NCH - 1) as n:
                store_h2(n)
            for b in range(B):
                sp.wait_ge(qkT_ready[b], NCH)
                sp.wait_ge(k_dec_done[b], NCH)
            sp.dma_start(ws_gu[:, :, :, :], shared_gu.rearrange("(k p) s n -> p k s n", p=P)).then_inc(ws_in, 16)
            sp.dma_start(ws_d[:, :, :], shared_d.rearrange("(m p) n -> p m n", p=P)).then_inc(ws_in, 16)
            store_h2(NCH - 1)
            store_h2(NCH)
            for b in range(B):
                sp.wait_ge(h2_stored[b], 16 * NCH)
                sp.wait_ge(h2T_done[b], NCH)
            sp.dma_start(w_d[:, :, :, :], expert_d.rearrange("e (c p) n -> p e c n", p=HC)).then_inc(w_e_in, 16)
            for i, t in enumerate(finished):
                sp.wait_ge(result_done, i + 1)
                sp.dma_start(out[t * P:(t + 1) * P, :], result[i % 2][:, :]).then_inc(stored[i % 2], 16)
            for u in range(2):
                sp.wait_ge(stored[u], 16 * (NT // 2))

        @block.scalar
        def _(act):
            act.dma_start(w_mod, wmod.rearrange("(k p) n -> p k n", p=P)).then_inc(w_mod_in, 16)
            for w, off in ((Wq, 0), (Wk, D), (Wv, 2 * D), (Wg1, 3 * D)):
                act.dma_start(w_in[:, :, off:off + w.shape[1]], w.rearrange("(k p) n -> p k n", p=P)).then_inc(w_qk_in if off < 2 * D else w_in_in, 16)
            act.dma_start(w_g2[:, :], Wg2).then_inc(w_in_in, 16)
            act.dma_start(w_o[:, :, :], Wo.rearrange("(k p) n -> p k n", p=P)).then_inc(w_in_in, 16)
            act.wait_ge(c_in, 16)
            act.activation(c_silu[:, :, :], c_raw[:, :, :], ACT.Silu).then_inc(c_silu_done, 1)

            def copy_mod(b):
                act.wait_ge(mod_rows_ready[b], 1)
                for i in range(2):
                    last = act.copy(mod_rows[b][:, 2 * i:2 * i + 2, :], score_bank[2 * b + i][:, :, :].rearrange("p a t -> p (a t)").rearrange("p (i d) -> p i d", d=D))
                last.then_inc(mod_copied, 1)

            def modulate(b, n, parts):
                act.wait_ge(xT_ready[b], n + 1)
                if "b" not in parts:
                    act.wait_ge(mod_cols_done, 2)
                for k in range(KC):
                    last = act.activation(hT[b][:, k, :], a_bank[b][:, k * P:(k + 1) * P], ACT.Identity,
                                          bias=mod_cols[:, 0, k, b:b + 1], scale=mod_cols[:, 1, k, b:b + 1])
                last.then_inc(hT_done[b], 1)

            def silu_qk(b, n):
                act.wait_ge(qk_ready[b], n + 1)
                act.activation(qk[b][:, :, :], heads(a_bank[b][:, :]), ACT.Silu).then_inc(qk_done[b], 1)

            def copy_vg(b, n):
                act.wait_ge(vg_ready[b], n + 1)
                act.copy(v[b][:, :], v_bank[:, 0:D])
                act.copy(g1T[b][:, :], v_bank[0:HD, D:D + P]).then_inc(vg_done[b], 1)

            def copy_qT(b, n):
                act.wait_ge(qkT_ready[b], n + 1)
                act.copy(qT[b][:, :, :], a_bank[b][:, :].rearrange("p (r t) -> p r t", t=P))

            def copy_kT(b, n):
                act.copy(kT[b][:, :, :], kT_bank[b].rearrange("p (r t) -> p r t", t=P)).then_inc(qkT_done[b], 1)

            def gate_tanh(b, n):
                act.wait_ge(gate_state_ready[b], n)
                act.activation(th[b][:, :], g_bank[:, 0:D], ACT.Tanh, scale=0.5).then_inc(th_done[b], 1)

            def copy_o(b, n):
                act.wait_ge(o_ready[b], n)
                act.copy(oP[b][:, :, :], o_bank[b][:, :, :]).then_inc(o_copied[b], 1)

            def square(b, n):
                act.wait_ge(o_g_done[b], n)
                act.activation(o_sq[b][:, :, :], o_g[b][:, :, :], ACT.Square).then_inc(o_sq_done[b], 1)

            def copy_oT(b, n):
                act.wait_ge(oT_ready[b], n)
                if isinstance(n, int) and n == 1:
                    act.wait_ge(mod_cols_done, 3)
                for k in range(KC):
                    last = act.activation(oT[b][:, k, :], oT_bank[b][:, k * P:(k + 1) * P], ACT.Copy, scale=norm_half[:, k:k + 1])
                last.then_inc(oT_done[b], 1)

            def step(n, parts):
                if "a" in parts:
                    modulate(0, n, parts)
                if "c" in parts:
                    copy_oT(1, n - 1)
                if "a" in parts:
                    modulate(1, n, parts)
                if "a" in parts:
                    silu_qk(0, n)
                if "b" in parts:
                    gate_tanh(0, n)
                if "a" in parts:
                    silu_qk(1, n)
                if "b" in parts:
                    copy_o(0, n)
                    gate_tanh(1, n)
                    square(0, n)
                if "a" in parts:
                    copy_vg(0, n)
                if "c" in parts:
                    act.wait_ge(h2T_ready, n - 1)
                    for b in range(B):
                        act.copy(h2T[:, :, bass.ds((n + (b * NCH - 2)) * P, P)],
                                 h2T_bank[:, b * D:(b + 1) * D].rearrange("p (k t) -> p k t", k=KC)).then_inc(h2T_done[b], 1)
                if "b" in parts:
                    copy_o(1, n)
                    copy_oT(0, n)
                    square(1, n)
                if "a" in parts:
                    copy_vg(1, n)
                if parts == "a":
                    for b in range(B):
                        copy_mod(b)
                if "a" in parts:
                    copy_qT(0, n)
                    copy_kT(0, n)
                    copy_qT(1, n)
                    copy_kT(1, n)

            run_steps(act, step)
            for b in range(B):
                act.wait_ge(h2_stored[b], 16 * NCH)
            act.wait_ge(logitsT_ready, 1)
            act.copy(logitsT[:, :, :], LOGITS_BANK.rearrange("p (q t) -> p q t", t=P)).then_inc(logitsT_done, 1)

            def shared_silu(q, m):
                i = q * SM + m
                act.wait_ge(s_gu_ready, i + 1)
                at_least(act, s_hid_done, i - 1)
                act.activation(s_silu[m % 2][:, :], bank[2 * (m % 2)], ACT.Silu)
                act.copy(s_up[m % 2][:, :], bank[2 * (m % 2) + 1]).then_inc(s_silu_done, 1)

            def job_step(i, u, parts):
                s = i * 4 + u
                if "x" in parts:
                    act.wait_ge(xeT_ready, s + 1)
                    at_least(act, gu_ready, s - 1)
                    act.copy(xeT[u % 2][:, :, :], bank[u % 2][:, 0:D].rearrange("p (k t) -> p k t", k=KC)).then_inc(xeT_done, 1)
                if "g" in parts:
                    act.wait_ge(gu_ready, s)
                    at_least(act, hid_done, s - 2)
                    act.activation(sg[(u + 1) % 2][:, :], bank[2 + (u + 1) % 2][:, 0:I_E], ACT.Silu).then_inc(sg_done, 1)
                if "y" in parts:
                    act.wait_ge(ye_ready, s - 2)
                    at_least(act, y_stored[(u + 1) % 4], (i + (u - 3) // 4) * 16)
                    act.copy(ys[(u + 1) % 4][:, :], bank[6 + (u + 1) % 2][:, 0:D]).then_inc(ye_done, 1)

            for q in range(EARLY):
                for m in range(SM):
                    shared_silu(q, m)
                    if (q, m) == (0, 1):
                        act.wait_ge(gap_done, 1)
                        act.activation(weight_e[:, :, :], gap[:, :, :], ACT.Exp)
                        act.activation(shared_th[:, :], logits[:, :, E], ACT.Tanh, scale=0.5).then_inc(exp_done, 1)
                if q == 0:
                    act.wait_ge(gates_done, 1)
                for t in range(SHARED_T):
                    n = q * SHARED_T + t
                    act.wait_ge(s_y_ready, n + 1)
                    act.activation(acc[:, n, :], bank[6 + t % 2][:, 0:D], ACT.Copy, scale=shared_gate[:, n:n + 1]).then_inc(s_y_done, 1)
            run_jobs(act, job_step)
            for q in late:
                for m in range(SM):
                    shared_silu(q, m)

        @block.gpsimd
        def _(pool):
            pool.memset(half_neg[:, :], -0.5).then_inc(consts_set, 1)
            pool.memset(settle_from[:, :], 0.0).then_inc(consts_set, 1)
            for b in range(B):
                pool.memset(state[b][:, :, :], 0.0).then_inc(state_done[b], 1)
                pool.memset(rot[b][:, :, :, :], 0.0).then_inc(consts_set, 1)
                pool.memset(k_dec[b][:, :, :], 0.0).then_inc(consts_set, 1)
            pool.wait_ge(consts_set, 6)
            rstd_view = rstd1[:, :].rearrange("p (b j) -> p b j", b=B)

            def rstd(i):
                pool.wait_ge(ln1_steps, B * x_parts[i + 1] * 2 + i + 1)
                cols = slice(x_parts[i], x_parts[i + 1])
                pool.tensor_tensor(rstd_view[:, :, cols], rstd_view[:, :, cols],
                                   half_neg[:, 0:B * (x_parts[i + 1] - x_parts[i])].rearrange("p (b j) -> p b j", b=B), ALU.pow).then_inc(rstd1_done, 1)

            rstd(0)
            pool.wait_ge(consts_in, 16 * 6)

            def rope_sin(b, n):
                half = HD // 2
                pool.wait_ge(qk_done[b], n + 1)
                settle_pool(4 + b)
                sin = rope_t[:, bass.ds(n, 1), 1, :]
                pool.tensor_tensor(rope_b[b][:, :, 0:half], qk[b][:, :, half:HD],
                                   sin[:, :, 0:half].to_broadcast([P, 2 * H, half]), ALU.mult)
                pool.tensor_tensor(rope_b[b][:, :, half:HD], qk[b][:, :, 0:half],
                                   sin[:, :, half:HD].to_broadcast([P, 2 * H, half]), ALU.mult).then_inc(rope_b_done[b], 1)

            def decay_keys(b, n):
                pool.wait_ge(rot_done[b], n + 1)
                at_least(pool, gate_state_ready[b], n)
                pool.tensor_tensor(k_dec[b][:, :, 0:HD], rot[b][:, 1, :, 0:HD],
                                   decay_k_t[:, :].unsqueeze(2).to_broadcast([P, H, HD]), ALU.mult).then_inc(k_dec_done[b], 1)

            def rms_norm(b, n):
                pool.wait_ge(ss_eps_done[b], n)
                pool.tensor_tensor(rms[b][:, :], ss_eps[b][:, :], half_neg[:, :], ALU.pow).then_inc(rms_done[b], 1)

            def second_norm(b, n):
                pool.wait_ge(var2_done[b], n)
                pool.tensor_tensor(rstd2[b][:, :], var2[b][:, :], half_neg[:, 0:1], ALU.pow).then_inc(rstd2_done[b], 1)
                pool.wait_ge(xn2_done[b], n)
                pool.tensor_tensor(h2_scaled[b][:, :], xn2[b][:, :], mod_rows[b][:, 2, :], ALU.mult).then_inc(h2_scaled_done[b], 1)
                pool.wait_ge(h2_scaled_done[b], n)
                pool.tensor_tensor(h2[b][:, :], h2_scaled[b][:, :], mod_rows[b][:, 1, :], ALU.add).then_inc(h2_done[b], 1)

            def step(n, parts):
                if "b" in parts:
                    for b in range(B):
                        pool.wait_ge(state_done[b], n)
                        pool.tensor_tensor(state_old[b][:, :, :], state[b][:, :, :], decay_s_t[:, :, :],
                                           ALU.mult).then_inc(state_old_done[b], 1)
                if "a" in parts:
                    rope_sin(0, n)
                if parts == "a":
                    rstd(1)
                if parts == "ab":
                    pool.wait_ge(mod_rows_done, B)
                if parts == "bc":
                    for b in range(B):
                        gate(pool, b, 3, 1, gb_steps)
                if "c" in parts:
                    second_norm(1, n - 1)
                if "a" in parts:
                    decay_keys(0, n)
                    rope_sin(1, n)
                if "b" in parts:
                    rms_norm(0, n)
                if "a" in parts:
                    decay_keys(1, n)
                if parts == "a":
                    rstd(2)
                if "b" in parts:
                    rms_norm(1, n)
                if "c" in parts:
                    for b in range(B):
                        pool.wait_ge(h2_stored[b], (n - 1) * 16)
                    pool.wait_ge(h2T_ready, n - 1)
                if "b" in parts:
                    second_norm(0, n)

            run_steps(pool, step)

            for b in range(B):
                pool.wait_ge(h2_stored[b], 16 * NCH)
                pool.wait_ge(h2T_done[b], NCH)
            pool.iota(iota_f[:, :], [[1, P]], base=0, channel_multiplier=0, allow_small_or_imprecise_dtypes=True).then_inc(iota_done, 1)
            pool.iota(token_id[:, :], [[P, NT]], base=0, channel_multiplier=1, allow_small_or_imprecise_dtypes=True).then_inc(iota_done, 1)
            pool.iota(number_i[:, :], [[P * TOPK, NT], [1, TOPK]], base=1, channel_multiplier=TOPK).then_inc(iota_done, 1)
            pool.iota(empty_row[:, :], [[P, NJ]], base=NQ * P + 1, channel_multiplier=1, allow_small_or_imprecise_dtypes=True).then_inc(iota_done, 1)
            pool.memset(ones[:, :], 1.0).then_inc(iota_done, 1)
            pool.memset(one_row[:, :], 1.0).then_inc(iota_done, 1)
            pool.memset(zero_b[:, :], 0.0).then_inc(iota_done, 1)

            def shared_mult(q, m):
                if m == 0:
                    at_least(pool, s_y_ready, q * SHARED_T)
                pool.wait_ge(s_silu_done, q * SM + m + 1)
                pool.tensor_tensor(s_hid[:, m, :], s_silu[m % 2][:, :], s_up[m % 2][:, :], ALU.mult).then_inc(s_hid_done, 1)

            for q in range(EARLY):
                for m in range(SM):
                    shared_mult(q, m)

            def gather_job(s, u):
                pool.tensor_copy(idx[u][:, :], token_of[:, bass.ds(s, 1)]).then_inc(idx_done, 1)
                pool.wait_ge(idx_done, s + 1)
                settle_pool(6 + u)
                pool.indirect_dma_start(xg[u][:, :], None, h2_rows, bass.IndirectOffsetOnAxis(ap=idx[u][:, 0:1], axis=0)).then_inc(gathered[u], 16)

            def scatter_job(s, u):
                pool.wait_ge(ye_done, s + 1)
                pool.tensor_copy(sidx[u][:, :], choice_of[:, bass.ds(s, 1)]).then_inc(sidx_done, 1)
                pool.wait_ge(sidx_done, s + 1)
                settle_pool(10 + u)
                pool.indirect_dma_start(y_rows, bass.IndirectOffsetOnAxis(ap=sidx[u][:, 0:1], axis=0), ys[u][:, :], None).then_inc(y_stored[u], 16)

            def job_step(i, u):
                s = i * 4 + u
                pool.wait_ge(gathered[u], i * 16)
                pool.wait_ge(xeT_ready, s - 3)
                gather_job(s, u)
                if not isinstance(s, int) or s >= 7:
                    scatter_job(s - 7, (u + 1) % 4)

            pool.wait_ge(tokens_done, 2)
            for u in range(4):
                gather_job(u, u)
            for u in range(4):
                job_step(1, u)
            with pool.Fori(2, NJ // 4) as i:
                for u in range(4):
                    job_step(i, u)
            for u in range(NJ % 4):
                job_step(NJ // 4, u)
            for s in range(NJ - 7, NJ):
                scatter_job(s, s % 4)
            for q in late:
                for m in range(SM):
                    shared_mult(q, m)
                    for pair in loads.get((q, m), ()):
                        if pair == 0:
                            for u in range(4):
                                pool.wait_ge(y_stored[u], 16 * len(range(u, NJ, 4)))
                        if pair >= 2:
                            pool.wait_ge(result_done, finished_count(EARLY + (pair - 2) // SHARED_T, "e", (pair - 2) % SHARED_T))
                        for i in (2 * pair, 2 * pair + 1):
                            t = combined[i]
                            pool.dma_start(y4[i % 4][:, :, :], y_rows[t * P * TOPK:(t + 1) * P * TOPK, :].rearrange("(p k) d -> p k d", k=TOPK)).then_inc(y_back[i % 4], 16)

        @block.vector
        def _(dve):
            dve.wait_ge(c_silu_done, 1)
            dve.tensor_copy(c_rows[:, :, :, :], c_silu[:, :, :].unsqueeze(3).to_broadcast([P, KC, B, P])).then_inc(c_rows_done, 1)

            def statistics(i):
                tiles = [b * NCH + j for b in range(B) for j in range(x_parts[i], x_parts[i + 1])]
                before = B * x_parts[i] * 2 + i
                dve.wait_ge(x_in[i], 16 * (B + 1 if i == 0 else B))
                for t in tiles:
                    dve.bn_stats(bn[:, t, :], x_all[:, t, :]).then_inc(ln1_steps, 1)
                dve.wait_ge(ln1_steps, before + len(tiles))
                for t in tiles:
                    dve.bn_aggr(mean_var[:, t, :], bn[:, t, :]).then_inc(ln1_steps, 1)
                dve.wait_ge(ln1_steps, before + 2 * len(tiles))
                cols = slice(x_parts[i], x_parts[i + 1])
                dve.tensor_scalar(rstd1[:, :].rearrange("p (b j) -> p b j", b=B)[:, :, cols],
                                  mean_var[:, :, 1].rearrange("p (b j) -> p b j", b=B)[:, :, cols], LN_EPS, None, ALU.add).then_inc(ln1_steps, 1)

            statistics(0)
            dve.wait_ge(mod_cols_ready, 1)
            dve.tensor_copy(mod_cols[:, 0, :, :], a_bank[0][:, 0:KC * B].rearrange("p (k b) -> p k b", b=B)).then_inc(mod_cols_done, 1)
            dve.tensor_scalar(mod_cols[:, 1, :, :], a_bank[0][:, KC * B:2 * KC * B].rearrange("p (k b) -> p k b", b=B),
                              1.0, None, ALU.add).then_inc(mod_cols_done, 1)

            def scale_wo():
                dve.tensor_scalar(norm_half[:, :], norm_col[:, :], 0.5, None, ALU.mult).then_inc(mod_cols_done, 1)
                dve.wait_ge(w_in_in, 16 * 4)
                for b in range(B):
                    dve.wait_ge(mod_copied, b + 1)
                    gate(dve, b, 0, 0, gate_steps)
                    dve.tensor_scalar(mod_rows[b][:, 2, :], mod_rows[b][:, 2, :], 1.0, None, ALU.add)
                    dve.tensor_tensor(w_og[b][:, :, :], w_o[:, :, :], mod_rows[b][:, 0, :].unsqueeze(1).to_broadcast([P, KC, D]),
                                      ALU.mult).then_inc(mod_rows_done, 1)

            def tile(b, n):
                return bass.ds(n + (b * NCH - 1), 1)

            def first_norm(n):
                for b in range(B):
                    at_least(dve, xT_ready[b], n)
                    t = bass.ds(n % NCH + b * NCH, 1)
                    dve.tensor_scalar(xn[b][:, :], x_all[:, t, :], mean_var[:, t, 0], rstd1[:, t],
                                      ALU.subtract, ALU.mult).then_inc(xn_done[b], 1)

            def rotate_cos(b, n):
                dve.wait_ge(qk_done[b], n + 1)
                dve.tensor_tensor(rope_a[b][:, :, :], qk[b][:, :, :],
                                  rope_t[:, bass.ds(n, 1), 0, :].to_broadcast([P, 2 * H, HD]), ALU.mult).then_inc(rope_a_done[b], 1)

            def rotate_sum(b, n):
                dve.wait_ge(rope_a_done[b], n + 1)
                dve.wait_ge(rope_b_done[b], n + 1)
                at_least(dve, k_dec_done[b], n)
                dve.tensor_tensor(rot[b][:, :, :, 0:HD], rope_a[b][:, :, :].rearrange("p (s h) d -> p s h d", s=2),
                                  rope_b[b][:, :, :].rearrange("p (s h) d -> p s h d", s=2), ALU.add).then_inc(rot_done[b], 1)

            def mask_scores(b, n):
                dve.wait_ge(scores_ready[b], n)
                for g in range(HG):
                    last = dve.tensor_tensor(probs[b][:, g], score_bank[g][:, :, :], decay_t[:, g, :, :], ALU.mult)
                last.then_inc(probs_done[b], 1)

            def mask_state(b, n):
                dve.wait_ge(th_done[b], n)
                dve.tensor_tensor(state_new[b][:, :, :], g_bank[:, D:2 * D].rearrange("p (r e) -> p r e", r=NR),
                                  state_mask_t[:, :, :], ALU.mult).then_inc(state_new_done[b], 1)

            def decay_queries(b, n):
                dve.wait_ge(qkT_done[b], n)
                dve.tensor_tensor(qdT[b][:, :, :], qT[b][:, :, :], decay_q_t[:, :, :], ALU.mult).then_inc(qd_done[b], 1)

            def update_state(b, n):
                dve.wait_ge(o_ready[b], n)
                dve.wait_ge(state_new_done[b], n)
                dve.wait_ge(state_old_done[b], n)
                dve.tensor_tensor(state[b][:, :, :], state_old[b][:, :, :], state_new[b][:, :, :], ALU.add).then_inc(state_done[b], 1)

            def gate_output(b, n):
                dve.wait_ge(o_rows_ready[b], n)
                dve.wait_ge(th_done[b], n)
                dve.scalar_tensor_tensor(o_g[b][:, :, :], heads(th[b][:, :]), 1.0,
                                         o_rows_bank[b][:, :, :].rearrange("p r (g d) -> p (r g) d", g=HG)[:, :, 0:HD],
                                         ALU.add, ALU.mult).then_inc(o_g_done[b], 1)

            def mean_square(b, n):
                dve.wait_ge(o_sq_done[b], n)
                dve.tensor_reduce(ss[b][:, :], o_sq[b][:, :, :], AX.X, ALU.add).then_inc(ss_done[b], 1)
                dve.wait_ge(ss_done[b], n)
                dve.tensor_scalar(ss_eps[b][:, :], ss[b][:, :], 1.0 / (4 * HD), RMS_EPS, ALU.mult, ALU.add).then_inc(ss_eps_done[b], 1)

            def normalize_output(b, n):
                dve.wait_ge(rms_done[b], n)
                dve.tensor_tensor(o_n[b][:, :, :], o_g[b][:, :, :], rms[b][:, :].unsqueeze(2).to_broadcast([P, H, HD]),
                                  ALU.mult).then_inc(o_n_done[b], 1)

            def add_residual(b, n):
                dve.wait_ge(y_ready[b], n)
                dve.tensor_tensor(x_all[:, tile(b, n), :], y_bank[b].unsqueeze(1), x_all[:, tile(b, n), :], ALU.add).then_inc(x2_done[b], 1)

            def statistics2(b, n):
                dve.wait_ge(x2_done[b], n)
                settle_dve(b)
                dve.bn_stats(bn2[b][:, :], x_all[:, tile(b, n), :]).then_inc(ln2_steps[b], 1)
                dve.wait_ge(ln2_steps[b], n * 2 - 1)
                settle_dve(2 + b)
                dve.bn_aggr(mv2[b][:, :], bn2[b][:, :]).then_inc(ln2_steps[b], 1)
                dve.wait_ge(ln2_steps[b], n * 2)
                dve.tensor_scalar(var2[b][:, :], mv2[b][:, 1:2], LN_EPS, None, ALU.add).then_inc(var2_done[b], 1)

            def normalize_x2(b, n):
                dve.wait_ge(rstd2_done[b], n)
                dve.tensor_scalar(xn2[b][:, :], x_all[:, tile(b, n), :], mv2[b][:, 0:1], rstd2[b][:, 0:1],
                                  ALU.subtract, ALU.mult).then_inc(xn2_done[b], 1)

            def step(n, parts):
                if parts == "ab":
                    dve.wait_ge(decay_in, 16)
                if "b" in parts:
                    decay_queries(0, n)
                if "c" in parts:
                    add_residual(1, n - 1)
                if "b" in parts:
                    mask_scores(0, n)
                if "c" in parts:
                    statistics2(1, n - 1)
                if parts == "a":
                    statistics(1)
                    dve.wait_ge(consts_in, 16 * 6)
                if "a" in parts:
                    rotate_cos(0, n)
                if "b" in parts:
                    mask_state(0, n)
                if "a" in parts:
                    rotate_sum(0, n)
                if "b" in parts:
                    decay_queries(1, n)
                if "c" in parts:
                    normalize_x2(1, n - 1)
                if "b" in parts:
                    mask_scores(1, n)
                    gate_output(0, n)
                if "a" in parts:
                    rotate_cos(1, n)
                if "b" in parts:
                    mean_square(0, n)
                if "a" in parts:
                    rotate_sum(1, n)
                    if parts != "abc":
                        dve.wait_ge(rstd1_done, n + 2)
                    first_norm(n + 1)
                if parts == "a":
                    statistics(2)
                    scale_wo()
                if "b" in parts:
                    update_state(0, n)
                    mask_state(1, n)
                    update_state(1, n)
                    normalize_output(0, n)
                    gate_output(1, n)
                    mean_square(1, n)
                    add_residual(0, n)
                    statistics2(0, n)
                    normalize_output(1, n)
                    normalize_x2(0, n)

            dve.wait_ge(rstd1_done, 1)
            first_norm(0)
            run_steps(dve, step)

            for b in range(B):
                dve.wait_ge(h2_stored[b], 16 * NCH)
            links = 0

            def link(instruction):
                nonlocal links
                links += 1
                instruction.then_inc(route, 1)
                dve.wait_ge(route, links)

            def per_choice(ap):
                return ap.unsqueeze(2).to_broadcast([P, NT, TOPK, E])

            dve.wait_ge(logits_ready, 1)
            link(dve.tensor_copy(logits[:, :, :], ROUTE_BANK.rearrange("p (t e) -> p t e", t=NT)[:, :, 0:E + 1]))
            for t in range(NT):
                last = dve.max(top8[:, t, :], logits[:, t, 0:E])
            link(last)
            dve.tensor_tensor(gap[:, :, :], top8[:, :, 0:TOPK], top8[:, :, 0:1].to_broadcast([P, NT, TOPK]), ALU.subtract).then_inc(gap_done, 1)
            for t in range(NT):
                last = dve.max_index(top8_i[:, t, :], top8[:, t, :], logits[:, t, 0:E])
            link(last)
            link(dve.tensor_copy(choice[:, :].rearrange("p (t k) -> p t k", k=TOPK), top8_i[:, :, 0:TOPK]))
            dve.wait_ge(iota_done, 7)
            dve.tensor_scalar(before[:, :], iota_f[:, :], token_id[:, 0:1], None, ALU.is_gt)
            link(dve.tensor_tensor(onehot[:, :, :], iota_f[:, 0:E].unsqueeze(1).to_broadcast([P, NQ, E]),
                                   choice[:, :].unsqueeze(2).to_broadcast([P, NQ, E]), ALU.is_equal))
            with nc.allow_low_precision(reason="counts up to 16 are exact in bfloat16"):
                link(dve.tensor_reduce(mask[:, :, :], onehot[:, :, :].rearrange("p (t k) e -> p t e k", k=TOPK), AX.X, ALU.add))
                dve.tensor_reduce(mask_sum[:, :], mask[:, :, :].rearrange("p t e -> p e t"), AX.X, ALU.add).then_inc(masks_done, 1)
            dve.wait_ge(counts_ready, 1)
            link(dve.tensor_scalar(count_i[:, :], COUNT_BANK[:, NT * E:NT * E + E], float(P - 1), None, ALU.add))
            link(dve.tensor_scalar(blocks_i[:, :], count_i[:, :], 7, None, ALU.logical_shift_right))
            link(dve.tensor_copy(blocks[:, :], blocks_i[:, :]))
            link(dve.tensor_tensor_scan(block_end[:, :], one_row[:, :], blocks[:, :], 0.0, ALU.mult, ALU.add))
            link(dve.tensor_tensor(block_start[:, :], block_end[:, :], blocks[:, :], ALU.subtract))
            link(dve.scalar_tensor_tensor(place[:, :, :], block_start[:, :].unsqueeze(1).to_broadcast([P, NT, E]), float(P),
                                          COUNT_BANK[:, 0:NT * E].rearrange("p (t e) -> p t e", e=E), ALU.mult, ALU.add))
            link(dve.tensor_tensor(placed[:, :, :].rearrange("p (t k) e -> p t k e", k=TOPK),
                                   onehot[:, :, :].rearrange("p (t k) e -> p t k e", k=TOPK), per_choice(place[:, :, :]), ALU.mult))
            link(dve.tensor_reduce(slot_f[:, :], placed[:, :, :], AX.X, ALU.add))
            link(dve.tensor_copy(slot[:, :], slot_f[:, :]))
            link(dve.tensor_scalar(slot_blk_i[:, :], slot[:, :], 7, None, ALU.logical_shift_right))
            link(dve.tensor_scalar(slot_row_i[:, :], slot[:, :], P - 1, None, ALU.bitwise_and))
            dve.tensor_copy(slot_blk[:, :], slot_blk_i[:, :])
            link(dve.tensor_copy(slot_row[:, :], slot_row_i[:, :]))
            dve.wait_ge(exp_done, 1)
            link(dve.tensor_reduce(weight_sum[:, :], weight_e[:, :, :], AX.X, ALU.add))
            link(dve.reciprocal(weight_rec[:, :], weight_sum[:, :]))
            dve.tensor_scalar(shared_gate[:, :], shared_th[:, :], 0.5, 0.5, ALU.mult, ALU.add).then_inc(gates_done, 1)
            link(dve.tensor_tensor(weight[:, :, :], weight_e[:, :, :], weight_rec[:, :].unsqueeze(2).to_broadcast([P, NT, TOPK]), ALU.mult))
            link(dve.tensor_tensor(job_ge[:, :, :], block_end[0:1, :].unsqueeze(1).to_broadcast([1, NJ, E]),
                                   iota_f[0:1, 0:NJ].unsqueeze(2).to_broadcast([1, NJ, E]), ALU.is_le))
            link(dve.tensor_reduce(job_sum[:, :], job_ge[:, :, :], AX.X, ALU.add))
            link(dve.tensor_scalar(job_expert[:, :], job_sum[:, :], float(E - 1), None, ALU.min))
            dve.tensor_scalar(number_hi_i[:, :], number_i[:, :], VB, None, ALU.logical_shift_right)
            link(dve.tensor_scalar(number_lo_i[:, :], number_i[:, :], (1 << VB) - 1, None, ALU.bitwise_and))
            dve.tensor_copy(number[:, :, 0], number_hi_i[:, :])
            link(dve.tensor_copy(number[:, :, 1], number_lo_i[:, :]))

            def hot_rows(i, u):
                for k in range(TOPK):
                    q = i * (HOT * TOPK) + (u * TOPK + k)
                    dve.tensor_scalar(row_hot[:, u, k, :], iota_f[:, :], slot_row[:, bass.ds(q, 1)], None, ALU.is_equal)
                    last = dve.scalar_tensor_tensor(blk_hot[:, u, k, :, :], iota_f[:, 0:NJ].unsqueeze(1).to_broadcast([P, 2, NJ]),
                                                    slot_blk[:, bass.ds(q, 1)],
                                                    number[:, bass.ds(q, 1), :].rearrange("p q s -> p (q s)").unsqueeze(2).to_broadcast([P, 2, NJ]),
                                                    ALU.is_equal, ALU.mult)
                last.then_inc(hot_done, 1)

            for u in range(HOT):
                hot_rows(0, u)
            with dve.Fori(1, NT // HOT) as i:
                for u in range(HOT):
                    dve.wait_ge(hot_used, i * HOT + (u - (HOT - 1)))
                    hot_rows(i, u)
            dve.wait_ge(tokens_ready, 1)
            link(dve.tensor_scalar(slot_high[:, :], ROUTE_BANK[:, 0:NJ], float(1 << VB), None, ALU.mult))
            link(dve.tensor_tensor(slot_num[:, :], slot_high[:, :], ROUTE_BANK[:, NJ:2 * NJ], ALU.add))
            dve.tensor_scalar(slot_tok[:, :], slot_num[:, :], 1.0, 0.0, ALU.subtract, ALU.max)
            link(dve.scalar_tensor_tensor(slot_empty[:, :], slot_num[:, :], 0.0, empty_row[:, :], ALU.is_equal, ALU.mult))
            dve.scalar_tensor_tensor(slot_dst[:, :], slot_num[:, :], 1.0, slot_empty[:, :], ALU.subtract, ALU.add)
            link(dve.tensor_copy(slot_tok_i[:, :], slot_tok[:, :]))
            dve.tensor_scalar(token_of[:, :], slot_tok_i[:, :], TOPK.bit_length() - 1, None, ALU.logical_shift_right).then_inc(tokens_done, 1)
            dve.tensor_copy(choice_of[:, :], slot_dst[:, :]).then_inc(tokens_done, 1)

            def job_step(i, u, parts):
                s = i * 4 + u
                if "g" in parts:
                    dve.wait_ge(sg_done, s)
                    at_least(dve, hidT_ready, s - 2)
                    dve.tensor_tensor(hid[(u + 1) % 2][:, :], sg[(u + 1) % 2][:, :], bank[2 + (u + 1) % 2][:, I_E:2 * I_E],
                                      ALU.mult).then_inc(hid_done, 1)
                if "h" in parts:
                    dve.wait_ge(hidT_ready, s - 1)
                    at_least(dve, ye_ready, s - 3)
                    dve.tensor_copy(hidT[u % 2][:, :, :], bank[4 + u % 2][0:HC, 0:2 * P].rearrange("p (c t) -> p c t", c=2)).then_inc(hidT_done, 1)

            run_jobs(dve, job_step)
            dve.wait_ge(gb_steps, 5 * B)

            adds, pairs, done = 0, 0, 0

            def add(instruction, behind=0):
                nonlocal adds
                adds += 1
                instruction.then_inc(sums, 1)
                dve.wait_ge(sums, adds - behind)

            def add_rows(own, early):
                nonlocal pairs
                y = [y4[(2 * pairs + i) % 4] for i in range(2)]
                for i in range(2):
                    dve.wait_ge(y_back[(2 * pairs + i) % 4], 16 * (pairs // 2 + 1))
                target = pre[own % SHARED_T][:, :]
                for k in range(TOPK):
                    if k == 0:
                        add(dve.tensor_scalar(target, y[0][:, 0, :], weight[:, own, 0:1], None, ALU.mult), 1)
                    else:
                        add(dve.scalar_tensor_tensor(target, y[0][:, k, :], weight[:, own, k:k + 1], target, ALU.mult, ALU.add), 1)
                    add(dve.scalar_tensor_tensor(total[:, :], y[1][:, k, :], weight[:, early, k:k + 1], total[:, :] if k else acc[:, early, :],
                                                 ALU.mult, ALU.add), k < TOPK - 1)
                pairs += 1

            def finish(t):
                nonlocal done
                add(dve.tensor_tensor(total_g[:, :], total[:, :], mod_rows[t // NCH][:, 3, :], ALU.mult))
                at_least(dve, stored[done % 2], 16 * (done // 2))
                dve.tensor_tensor(result[done % 2][:, :], total_g[:, :], x_all[:, t, :], ALU.add).then_inc(result_done, 1)
                done += 1

            for q in late:
                for j, kind in enumerate(order[q]):
                    m = order[q][:j].count(kind)
                    if kind == "e":
                        add_rows(q * SHARED_T + m, (q - EARLY) * SHARED_T + m)
                        finish((q - EARLY) * SHARED_T + m)
                    else:
                        t = q * SHARED_T + m
                        dve.wait_ge(s_y_ready, t + 1)
                        add(dve.scalar_tensor_tensor(total[:, :], down_bank(q, m), shared_gate[:, t:t + 1], pre[m][:, :],
                                                     ALU.mult, ALU.add))
                        finish(t)

        @block.tensor
        def _(pe):
            pe.wait_ge(w_mod_in, 16)
            pe.wait_ge(c_silu_done, 1)
            for i in range(2):
                for m in range(KC):
                    for k in range(KC):
                        last = pe.matmul(a_bank[0][:, (i * KC + m) * B:(i * KC + m + 1) * B],
                                         w_mod[:, k, i * D + m * P:i * D + (m + 1) * P], c_silu[:, k, :],
                                         start=(k == 0), stop=(k == KC - 1))
            last.then_inc(mod_cols_ready, 1)

            def shared_hidden(q, m, halves=(0, 1)):
                i = q * SM + m
                if i >= 2:
                    pe.wait_ge(s_silu_done, i - 1)
                for g in halves:
                    for k in range(KC):
                        last = pe.matmul(bank[2 * (m % 2) + g], ws_gu[:, k, g, m * P:(m + 1) * P], h2T[:, k, q * 512:(q + 1) * 512],
                                         start=(k == 0), stop=(k == KC - 1))
                if halves[-1] == 1:
                    last.then_inc(s_gu_ready, 1)

            def modulate_rows(b):
                for i in range(2):
                    for k in range(KC):
                        last = pe.matmul(score_bank[2 * b + i][:, :, :].rearrange("p a t -> p (a t)"), c_rows[:, k, b, :],
                                         w_mod[:, k, 2 * D + i * 512:2 * D + (i + 1) * 512], start=(k == 0), stop=(k == KC - 1))
                last.then_inc(mod_rows_ready[b], 1)

            pe.wait_ge(mod_cols_done, 2)

            EW = HG * HD

            def scores(b, r):
                for g in range(HG):
                    q0 = PAD * g
                    last = pe.matmul(score_bank[g][:, r, :], kT[b][q0:q0 + HD, r, :], qT[b][q0:q0 + HD, r, :],
                                     start=True, stop=True)
                if r == NR - 1:
                    last.then_inc(scores_ready[b], 1)

            def attend(b, r):
                for g in range(HG):
                    pe.matmul(o_bank[b][PAD * g:PAD * g + HD, r, :], state[b][:, r, g * HD:(g + 1) * HD], qdT[b][:, r, :],
                              start=True, stop=False)
                for g in range(HG):
                    h = r * HG + g
                    last = pe.matmul(o_bank[b][PAD * g:PAD * g + HD, r, :], v[b][:, h * HD:(h + 1) * HD], probs[b][:, g, r, :],
                                     start=False, stop=True)
                if r == NR - 1:
                    last.then_inc(o_ready[b], 1)

            def output_rows(b, n):
                pe.wait_ge(o_copied[b], n)
                for r in range(NR):
                    last = pe.transpose(o_rows_bank[b][:, r, :], oP[b][:, r, :], ident[:, :])
                last.then_inc(o_rows_ready[b], 1)

            def gate_state(b, n):
                pe.wait_ge(k_dec_done[b], n)
                at_least(pe, state_new_done[1 - b], n - (1 - b))
                if b == 0:
                    at_least(pe, x2_done[1], n - 1)
                pe.matmul(g_bank[:, 0:D], g1T[b][:, :], w_g2[:, :], start=True, stop=True)
                for r in range(NR):
                    last = pe.matmul(g_bank[:, D + r * EW:D + (r + 1) * EW], k_dec[b][:, HG * r:HG * (r + 1), :].rearrange("p h d -> p (h d)"),
                                     v[b][:, r * EW:(r + 1) * EW], start=True, stop=True)
                last.then_inc(gate_state_ready[b], 1)

            def transpose_x(b, n):
                pe.wait_ge(xn_done[b], n + 1)
                at_least(pe, qkT_done[b], n)
                for k in range(KC):
                    last = pe.transpose(a_bank[b][:, k * P:(k + 1) * P], xn[b][:, k * P:(k + 1) * P], ident[:, :])
                last.then_inc(xT_ready[b], 1)

            def project_qk(b, k):
                last = pe.matmul(a_bank[b][:, :], hT[b][:, k, :], w_in[:, k, 0:2 * D], start=(k == 0), stop=(k == KC - 1))
                if k == KC - 1:
                    last.then_inc(qk_ready[b], 1)

            def project_v(b):
                for k in range(KC):
                    pe.matmul(v_bank[:, 0:D], hT[b][:, k, :], w_in[:, k, 2 * D:3 * D], start=(k == 0), stop=(k == KC - 1))

            def project_g1(b):
                for k in range(KC):
                    last = pe.matmul(v_bank[0:HD, D:D + P], w_in[:, k, 3 * D:3 * D + HD], hT[b][:, k, :],
                                     start=(k == 0), stop=(k == KC - 1))
                last.then_inc(vg_ready[b], 1)

            def transpose_q(b):
                for r in range(NR):
                    pe.transpose(a_bank[b][:, r * P:(r + 1) * P], rot[b][:, 0, HG * r:HG * (r + 1), :].rearrange("p h d -> p (h d)"), ident[:, :])

            def transpose_k(b):
                for r in range(NR):
                    last = pe.transpose(kT_bank[b][:, r * P:(r + 1) * P], rot[b][:, 1, HG * r:HG * (r + 1), :].rearrange("p h d -> p (h d)"), ident[:, :])
                last.then_inc(qkT_ready[b], 1)

            def transpose_o(b, n):
                pe.wait_ge(o_n_done[b], n)
                for k in range(KC):
                    last = pe.transpose(oT_bank[b][:, k * P:(k + 1) * P],
                                        o_n[b][:, :, :].rearrange("p h d -> p (h d)")[:, k * P:(k + 1) * P], ident[:, :])
                last.then_inc(oT_ready[b], 1)

            def project_y(b, n):
                pe.wait_ge(oT_done[b], n)
                if isinstance(n, int) and n == 1 and b == 0:
                    pe.wait_ge(mod_rows_done, B)
                for k in range(KC):
                    last = pe.matmul(y_bank[b], oT[b][:, k, :], w_og[b][:, k, :], start=(k == 0), stop=(k == KC - 1))
                last.then_inc(y_ready[b], 1)

            def router_logits(tiles):
                for t in tiles:
                    q0 = RW * (t % HG)
                    for k in range(KC):
                        last = pe.matmul(LOGITS_BANK[q0:q0 + RW, t // HG * P:(t // HG + 1) * P], w_r[:, k, :], h2T[:, k, t * P:(t + 1) * P],
                                         start=(k == 0), stop=(k == KC - 1))
                return last

            def step(n, parts):
                if "a" in parts:
                    transpose_x(0, n)
                if "b" in parts:
                    pe.wait_ge(qkT_done[0], n)
                    at_least(pe, o_g_done[1], n - 1)
                    at_least(pe, x2_done[0], n - 1)
                    scores(0, 0)
                if "a" in parts:
                    transpose_x(1, n)
                if "b" in parts:
                    scores(0, 1)
                if parts == "a":
                    pe.wait_ge(w_qk_in, 16 * 2)
                if "a" in parts:
                    pe.wait_ge(hT_done[0], n + 1)
                    project_qk(0, 0)
                if parts == "c":
                    pe.wait_ge(o_g_done[1], n - 1)
                    pe.wait_ge(ws_in, 16 * 2)
                    shared_hidden(0, 0)
                if "b" in parts:
                    scores(0, 2)
                if "c" in parts:
                    pe.wait_ge(state_new_done[1], n - 1)
                    transpose_o(1, n - 1)
                if "a" in parts:
                    project_qk(0, 1)
                if "c" in parts:
                    project_y(1, n - 1)
                if parts == "c":
                    pe.wait_ge(x2_done[0], n - 1)
                    shared_hidden(0, 1, [0])
                    pe.wait_ge(w_r_in, 16)
                    router_logits([t for t in range(NT) if t % NCH < NCH - 1])
                if "b" in parts:
                    scores(0, 3)
                if "a" in parts:
                    pe.wait_ge(hT_done[1], n + 1)
                    project_qk(1, 0)
                if "b" in parts:
                    gate_state(0, n)
                if "a" in parts:
                    project_qk(1, 1)
                if "b" in parts:
                    pe.wait_ge(qkT_done[1], n)
                    pe.wait_ge(qd_done[0], n)
                    pe.wait_ge(state_done[0], n)
                    pe.wait_ge(probs_done[0], n)
                    scores(1, 0)
                    attend(0, 0)
                    scores(1, 1)
                    attend(0, 1)
                    scores(1, 2)
                    attend(0, 2)
                    scores(1, 3)
                    attend(0, 3)
                    gate_state(1, n)
                if "a" in parts and "b" in parts:
                    pe.wait_ge(qk_done[0], n + 1)
                if "b" in parts:
                    output_rows(0, n)
                if parts == "a":
                    pe.wait_ge(w_in_in, 16 * 4)
                if "a" in parts:
                    project_v(0)
                    project_g1(0)
                if "b" in parts:
                    pe.wait_ge(probs_done[1], n)
                if "c" in parts:
                    for b in range(B):
                        pe.wait_ge(h2_done[b], n - 1)
                        for k in range(KC):
                            last = pe.transpose(h2T_bank[:, b * D + k * P:b * D + (k + 1) * P], h2[b][:, k * P:(k + 1) * P], ident[:, :])
                    last.then_inc(h2T_ready, 1)
                if "b" in parts:
                    pe.wait_ge(state_done[1], n)
                    pe.wait_ge(qd_done[1], n)
                    for r in range(NR):
                        attend(1, r)
                if "a" in parts:
                    pe.wait_ge(vg_done[0], n + 1)
                    project_v(1)
                    project_g1(1)
                if parts == "a":
                    for b in range(B):
                        modulate_rows(b)
                if "b" in parts:
                    output_rows(1, n)
                    transpose_o(0, n)
                if "a" in parts:
                    pe.wait_ge(rot_done[0], n + 1)
                    at_least(pe, o_g_done[0], n)
                    transpose_q(0)
                    if parts == "a":
                        pe.wait_ge(mod_copied, B)
                    transpose_k(0)
                if "a" in parts:
                    pe.wait_ge(rot_done[1], n + 1)
                    transpose_q(1)
                if "b" in parts:
                    project_y(0, n)
                if "a" in parts:
                    pe.wait_ge(vg_done[1], n + 1)
                    transpose_k(1)
                if "c" in parts:
                    for b in range(B):
                        pe.wait_ge(h2T_done[b], n - 1)

            run_steps(pe, step)

            for b in range(B):
                pe.wait_ge(h2T_done[b], NCH)
            router_logits([b * NCH + NCH - 1 for b in range(B)]).then_inc(logitsT_ready, 1)
            pe.wait_ge(logitsT_done, 1)
            for i in range(NT // HG):
                last = pe.transpose(ROUTE_BANK[:, i * P:(i + 1) * P], logitsT[:, i, :], ident[:, :])
            last.then_inc(logits_ready, 1)

            def count_tokens():
                pe.wait_ge(masks_done, 1)
                pe.matmul(COUNT_BANK[:, 0:NT * E], before[:, :], mask[:, :, :].rearrange("p t e -> p (t e)"), start=True, stop=False)
                for d in range(1, NT):
                    pe.matmul(COUNT_BANK[:, d * E:NT * E], ones[:, :], mask[:, 0:NT - d, :].rearrange("p t e -> p (t e)"),
                              start=False, stop=(d == NT - 1))
                pe.matmul(COUNT_BANK[:, NT * E:NT * E + E], ones[:, :], mask_sum[:, :], start=True, stop=True).then_inc(counts_ready, 1)
                pe.matmul(ROUTE_BANK[:, 0:2 * NJ], zero_b[:, 0:P], zero_b[:, :], start=True, stop=False)

            def place_tokens(t):
                pe.wait_ge(hot_done, t + 1)
                for k in range(TOPK):
                    last = pe.matmul(ROUTE_BANK[:, 0:2 * NJ], row_hot[:, t % HOT, k, :], blk_hot[:, t % HOT, k, :, :].rearrange("p s j -> p (s j)"),
                                     start=False, stop=False)
                last.then_inc(hot_used, 1)

            def shared_down(q, t, parts):
                for m in parts:
                    last = pe.matmul(down_bank(q, t), s_hid[:, m, t * P:(t + 1) * P], ws_d[:, m, :],
                                     start=(m == 0), stop=(m == SM - 1))
                if parts[-1] == SM - 1:
                    last.then_inc(s_y_ready, 1)

            def shared_out(q):
                if q >= EARLY:
                    pe.wait_ge(ye_done, NJ)
                pe.wait_ge(s_hid_done, (q + 1) * SM - 1)
                for t in range(2):
                    y_bank_free(q, t)
                    shared_down(q, t, range(SM - 1))
                pe.wait_ge(s_hid_done, (q + 1) * SM)
                for t in range(2):
                    shared_down(q, t, [SM - 1])
                for t in range(2, SHARED_T):
                    if q == 0:
                        for i in range((t - 2) * 2, (t - 1) * 2):
                            place_tokens(i)
                    y_bank_free(q, t)
                    shared_down(q, t, range(SM))

            def y_bank_free(q, t):
                if q < EARLY:
                    at_least(pe, s_y_done, q * SHARED_T + t - 1)
                elif q > EARLY:
                    pe.wait_ge(result_done, finished_count(q - 1, "o", t))

            def expert_of(job):
                return pe.value_load(job_expert[0:1, bass.ds(job, 1)], min_val=0, max_val=E - 1)

            def job_step(i, u, parts):
                s = i * 4 + u
                if parts == "hy":
                    pe.wait_ge(xeT_done, NJ)
                    shared_hidden(EARLY, 0)
                if "x" in parts:
                    pe.wait_ge(gathered[u], i * 16 + 16)
                    at_least(pe, xeT_done, s - 1)
                    for k in range(KC):
                        last = pe.transpose(bank[u % 2][:, k * P:(k + 1) * P], xg[u][:, k * P:(k + 1) * P], ident[:, :])
                    last.then_inc(xeT_ready, 1)
                if "g" in parts:
                    e = expert_of(s - 1)
                    pe.wait_ge(xeT_done, s)
                    at_least(pe, hid_done, s - 2)
                    for k in range(KC):
                        last = pe.matmul(bank[2 + (u + 1) % 2][:, 0:2 * I_E], xeT[(u + 1) % 2][:, k, :],
                                         w_gu_flat[:, bass.ds(e * (KC * 2 * I_E) + k * 2 * I_E, 2 * I_E)], start=(k == 0), stop=(k == KC - 1))
                    last.then_inc(gu_ready, 1)
                if "h" in parts:
                    pe.wait_ge(hid_done, s - 1)
                    at_least(pe, hidT_done, s - 3)
                    for h in range(2):
                        last = pe.transpose(bank[4 + u % 2][0:HC, h * P:(h + 1) * P], hid[u % 2][:, h * HC:(h + 1) * HC], ident[:, :])
                    last.then_inc(hidT_ready, 1)
                if "y" in parts:
                    e = expert_of(s - 3)
                    if isinstance(s, int) and s == 3:
                        pe.wait_ge(s_y_done, EARLY * SHARED_T)
                    pe.wait_ge(hidT_done, s - 2)
                    at_least(pe, ye_done, s - 4)
                    for h in range(2):
                        last = pe.matmul(bank[6 + (u + 1) % 2][:, 0:D], hidT[(u + 1) % 2][:, h, :],
                                         w_d_flat[:, bass.ds(e * (2 * D) + h * D, D)], start=(h == 0), stop=(h == 1))
                    last.then_inc(ye_ready, 1)

            for q in range(EARLY):
                for m in range(SM):
                    if m > 0:
                        shared_hidden(q, m, (1,) if (q, m) == (0, 1) else (0, 1))
                    if q == 0 and m == SM // 2:
                        count_tokens()
                    if q == EARLY - 1:
                        for t in range(SHARED_T + m * (NT - SHARED_T) // SM, SHARED_T + (m + 1) * (NT - SHARED_T) // SM):
                            place_tokens(t)
                if q + 1 < EARLY:
                    shared_hidden(q + 1, 0)
                else:
                    pe.matmul(ROUTE_BANK[:, 0:2 * NJ], zero_b[:, 0:P], zero_b[:, :], start=False, stop=True).then_inc(tokens_ready, 1)
                shared_out(q)
            pe.wait_ge(tokens_done, 2)
            pe.wait_ge(w_e_in, 32)
            run_jobs(pe, job_step)
            for q in late:
                for m in range(1, SM):
                    shared_hidden(q, m)
                if q + 1 < SHARED_STEPS:
                    shared_hidden(q + 1, 0)
                shared_out(q)


def constants():
    f = np.float32
    slope = (2.0 ** (-8.0 * (np.arange(H, dtype=f) + 1.0) / H)).astype(f)
    log_lam = -slope
    theta = (f(10000.0) ** (-2.0 * np.arange(HD // 2, dtype=f) / HD)).astype(f)
    ang = np.arange(N, dtype=f)[:, None] * theta[None, :]
    cos, sin = np.cos(ang).astype(f), np.sin(ang).astype(f)
    rope = np.stack([np.concatenate([cos, cos], 1), np.concatenate([-sin, sin], 1)], 1)
    i = np.arange(P, dtype=f)
    diff = i[None, :] - i[:, None]
    dec = np.where(diff[:, None, :] >= 0, np.exp(log_lam[None, :, None] * np.maximum(diff, 0)[:, None, :]), 0).astype(f)
    decay = dec.reshape(P, NR, HG, P).transpose(0, 2, 1, 3)
    dq = np.exp(log_lam[:, None] * (i[None, :] + 1)).astype(f)
    dqT = np.repeat(dq.reshape(NR, HG, P).transpose(1, 0, 2), PAD, axis=0)
    dk = np.exp(log_lam[None] * (P - 1 - i[:, None])).astype(f)
    mask = np.zeros((P, NR, HG, HD), f)
    for g in range(HG):
        mask[PAD * g:PAD * g + HD, :, g, :] = 1
    lam_c = np.exp(log_lam * P).astype(f).reshape(1, NR, HG, 1)
    return {
        "rope": rope.astype(f), "decay": np.ascontiguousarray(decay), "decay_q": dqT, "decay_k": dk,
        "decay_s": (mask * lam_c).reshape(P, NR, HG * HD), "state_mask": mask.reshape(P, NR, HG * HD), "ident": np.eye(P, dtype=f),
    }


def kernel(**inputs):
    import concourse.bacc as bacc
    from concourse.bass_utils import run_bass_kernel_spmd

    a = {k: np.asarray(v) for k, v in inputs.items()}
    pad = SM * P - SI
    shared_gu = np.pad(a["L0_ffn_shared_gate_up"].reshape(2, SI, D).transpose(2, 0, 1), ((0, 0), (0, 0), (0, pad)))
    router = np.concatenate([a["L0_ffn_gate_w"], a["L0_ffn_shared_gate_vec"]], 0).T
    arrays = {
        "x": a["L0_attn_x"].reshape(B * N, D),
        "Wq": a["L0_attn_Wq"], "Wk": a["L0_attn_Wk"], "Wv": a["L0_attn_Wv"], "Wo": a["L0_attn_Wo"],
        "Wg1": a["L0_attn_Wg1"], "Wg2": a["L0_attn_Wg2"],
        "norm_w": a["L0_attn_norm_weight"].reshape(KC, P).T,
        "c": a["L0_c"].reshape(B, KC, P).transpose(2, 1, 0),
        "wmod": a["L0_wmod"],
        "router_w": np.pad(router, ((0, 0), (0, RW - E - 1))),
        "expert_gu": a["L0_ffn_expert_gate_up"].transpose(0, 2, 1),
        "expert_d": a["L0_ffn_expert_down"].transpose(0, 2, 1),
        "shared_gu": shared_gu,
        "shared_d": np.pad(a["L0_ffn_shared_down"].T, ((0, pad), (0, 0))),
    }
    arrays.update(constants())
    arrays = {f"in_{k}": np.ascontiguousarray(v) for k, v in arrays.items()}
    nc = bacc.Bacc("TRN2", target_bir_lowering=False, num_devices=1)
    args = [nc.dram_tensor(k, v.shape, mybir.dt.from_np(v.dtype), kind="ExternalInput").ap() for k, v in arrays.items()]
    out = nc.dram_tensor("out_rows", [B * N, D], F32, kind="ExternalOutput").ap()
    build(nc, *args, out)
    r = run_bass_kernel_spmd(nc, [arrays], core_ids=[0])
    return r.results[0]["out_rows"].reshape(B, N, D)
```
